# Optimizing a Trainium2 kernel written in Bass

```python
import numpy as np
import jax
import jax.numpy as jnp

def _softmax(x, axis=-1):
    return jax.nn.softmax(x, axis=axis)

def _gelu(x):
    return jax.nn.gelu(x, approximate=True)

def _silu(x):
    return jax.nn.silu(x)

def _sigmoid(x):
    return jax.nn.sigmoid(x)

def _layernorm(x, axis=-1, eps=1e-05):
    m = jnp.mean(x, axis=axis, keepdims=True)
    v = jnp.var(x, axis=axis, keepdims=True)
    return (x - m) / jnp.sqrt(v + eps)

def _scatter_add(tgt, idx, src, axis=0):
    return tgt.at[idx].add(src)

def _segment_sum(src, seg, n):
    return jax.ops.segment_sum(src, seg, n)
kernel_name = 'mk_decoder_preln_d2_seqx_r8_2c9508'

def setup_inputs(seed: int=0):
    np.random.seed(seed)
    _w = jnp.asarray

    def _rec_inputs():
        import jax
        import jax.numpy as jnp
        _rk = jax.random.key(seed)
        x = 7.22e-05 + 1 * jax.random.normal(jax.random.fold_in(_rk, 1), (32, 128, 128), jnp.float32)
        _lenS = 128 - jax.random.randint(jax.random.fold_in(_rk, 7), (32,), 0, max(1, 128 // 4) + 1, jnp.int32)
        _lenS2 = 128 - jax.random.randint(jax.random.fold_in(_rk, 8), (32,), 0, max(1, 128 // 4) + 1, jnp.int32)
        _ctx_1024P = jax.random.normal(jax.random.fold_in(_rk, 11), (32, 16, 128), jnp.float32)
        _ctx_1024c = jax.random.dirichlet(jax.random.fold_in(_rk, 511), 0.3 * jnp.ones((16,), jnp.float32), (32, 128))
        _ctx_1024t = jnp.einsum('bsk,bkd->bsd', _ctx_1024c, _ctx_1024P)
        _ctx_1024t = _ctx_1024t * jax.lax.rsqrt(jnp.mean(jnp.square(_ctx_1024t)) + 1e-12) * 0.953939
        ctx_1024 = 4.13588e-05 + 0.999923 * (_ctx_1024t + 0.3 * jax.random.normal(jax.random.fold_in(_rk, 611), (32, 128, 128), jnp.float32))
        return (x, ctx_1024)
    x, ctx_1024 = _rec_inputs()

    def _L0_attn_setup():
        import jax, jax.numpy as jnp
        import numpy as np
        D_MODEL = 128
        NHEAD = 16
        HEAD_DIM = D_MODEL // NHEAD
        SCALE = float(np.sqrt(HEAD_DIM))
        key = jax.random.key(seed)
        ks = jax.random.split(key, 6)
        B, T = (2, 256)
        x = jax.random.normal(ks[0], (B, T, D_MODEL), dtype=jnp.float32)
        s = 1.0 / np.sqrt(D_MODEL)
        qkv_w = jax.random.uniform(ks[1], (3 * D_MODEL, D_MODEL), jnp.float32, -s, s)
        qkv_b = jax.random.uniform(ks[2], (3 * D_MODEL,), jnp.float32, -s, s)
        out_w = jax.random.uniform(ks[3], (D_MODEL, D_MODEL), jnp.float32, -s, s)
        out_b = jax.random.uniform(ks[4], (D_MODEL,), jnp.float32, -s, s)
        decay_alpha = jnp.full((NHEAD,), 0.1, dtype=jnp.float32)
        return {'x': x, 'qkv_w': qkv_w, 'qkv_b': qkv_b, 'out_w': out_w, 'out_b': out_b, 'decay_alpha': decay_alpha}
    _L0_attn_all = _L0_attn_setup()
    _L0_attn_in = {k: v for k, v in _L0_attn_all.items() if k in ('qkv_w', 'qkv_b', 'out_w', 'out_b', 'decay_alpha')}
    del _L0_attn_all

    def _L0_xattn_setup():
        import jax, jax.numpy as jnp
        import numpy as np
        B, SD, SE, D, H = (4, 256, 256, 128, 16)
        HD = D // H

        def _mha(xq, xk, xv, Wq, bq, Wk, bk, Wv, bv, Wo, bo, causal):
            q = jnp.einsum('bsd,hde->bhse', xq, Wq) + bq[None, :, None, :]
            k = jnp.einsum('bsd,hde->bhse', xk, Wk) + bk[None, :, None, :]
            v = jnp.einsum('bsd,hde->bhse', xv, Wv) + bv[None, :, None, :]
            scale = 1.0 / jnp.sqrt(jnp.asarray(HD, q.dtype))
            scores = jnp.einsum('bhqe,bhke->bhqk', q, k) * scale
            if causal:
                mask = jnp.tril(jnp.ones((q.shape[2], k.shape[2]), bool))
                scores = jnp.where(mask, scores, jnp.finfo(scores.dtype).min)
            w = jax.nn.softmax(scores, axis=-1)
            out = jnp.einsum('bhqk,bhke->bhqe', w, v)
            out = out.transpose(0, 2, 1, 3).reshape(out.shape[0], out.shape[2], D)
            return out @ Wo + bo
        key = jax.random.key(seed)
        ks = jax.random.split(key, 19)
        sd = 1.0 / np.sqrt(D)
        n = lambda k, shape, s: jax.random.normal(k, shape, jnp.float32) * s
        inp = {'x': n(ks[0], (B, SD, D), 1.0), 'encoder_k': n(ks[1], (B, SE, D), 1.0), 'encoder_v': n(ks[2], (B, SE, D), 1.0), 'Wq1': n(ks[3], (H, D, HD), sd), 'bq1': jnp.zeros((H, HD), jnp.float32), 'Wk1': n(ks[4], (H, D, HD), sd), 'bk1': jnp.zeros((H, HD), jnp.float32), 'Wv1': n(ks[5], (H, D, HD), sd), 'bv1': jnp.zeros((H, HD), jnp.float32), 'Wo1': n(ks[6], (D, D), sd), 'bo1': jnp.zeros((D,), jnp.float32), 'Wq2': n(ks[7], (H, D, HD), sd), 'bq2': jnp.zeros((H, HD), jnp.float32), 'Wk2': n(ks[8], (H, D, HD), sd), 'bk2': jnp.zeros((H, HD), jnp.float32), 'Wv2': n(ks[9], (H, D, HD), sd), 'bv2': jnp.zeros((H, HD), jnp.float32), 'Wo2': n(ks[10], (D, D), sd), 'bo2': jnp.zeros((D,), jnp.float32)}
        return inp
    _L0_xattn_all = _L0_xattn_setup()
    _L0_xattn_in = {k: v for k, v in _L0_xattn_all.items() if k in ('Wq1', 'bq1', 'Wk1', 'bk1', 'Wv1', 'bv1', 'Wo1', 'bo1', 'Wq2', 'bq2', 'Wk2', 'bk2', 'Wv2', 'bv2', 'Wo2', 'bo2')}
    del _L0_xattn_all

    def _L0_ffn_setup():
        import math
        import jax, jax.numpy as jnp
        import numpy as np
        B, L, D, F_FF, E = (4, 256, 128, 512, 8)
        TOP_K = 1
        CAPACITY_FACTOR = 1.25
        key = jax.random.key(seed)
        ks = jax.random.split(key, 4)
        h = jax.random.normal(ks[0], (B, L, D), dtype=jnp.float32)
        gate_w = jax.random.normal(ks[1], (E, D), dtype=jnp.float32) * 0.02
        gate_b = jnp.zeros((E,), dtype=jnp.float32)
        w1 = jax.random.normal(ks[2], (E, D, F_FF), dtype=jnp.float32) * 0.02
        b1 = jnp.zeros((E, F_FF), dtype=jnp.float32)
        w2 = jax.random.normal(ks[3], (E, F_FF, D), dtype=jnp.float32) * 0.02
        b2 = jnp.zeros((E, D), dtype=jnp.float32)
        return {'h': h, 'gate_w': gate_w, 'gate_b': gate_b, 'w1': w1, 'b1': b1, 'w2': w2, 'b2': b2}
    _L0_ffn_all = _L0_ffn_setup()
    _L0_ffn_in = {k: v for k, v in _L0_ffn_all.items() if k in ('gate_w', 'gate_b', 'w1', 'b1', 'w2', 'b2')}
    del _L0_ffn_all

    def _L1_attn_setup():
        import jax, jax.numpy as jnp
        import numpy as np
        import math
        B, S, E, H = (2, 256, 128, 16)
        D = E // H
        key = jax.random.key(seed)
        ks = jax.random.split(key, 5)
        scale_p = 1.0 / math.sqrt(D)
        return {'x': jax.random.normal(ks[0], (B, S, E), dtype=jnp.float32), 'Wq': jax.random.normal(ks[1], (D, D), dtype=jnp.float32) * scale_p, 'Wk': jax.random.normal(ks[2], (D, D), dtype=jnp.float32) * scale_p, 'Wv': jax.random.normal(ks[3], (D, D), dtype=jnp.float32) * scale_p, 'W_out': jax.random.normal(ks[4], (E, E), dtype=jnp.float32) * (1.0 / math.sqrt(E)), 'b_out': jnp.zeros((E,), dtype=jnp.float32)}
    _L1_attn_all = _L1_attn_setup()
    _L1_attn_in = {k: v for k, v in _L1_attn_all.items() if k in ('Wq', 'Wk', 'Wv', 'W_out', 'b_out')}
    del _L1_attn_all

    def _L1_xattn_setup():
        import jax, jax.numpy as jnp
        import numpy as np
        DECAY = 0.9
        key = jax.random.key(seed)
        k1, k2, k3 = jax.random.split(key, 3)
        B, S, D = (8, 512, 128)
        q = jax.random.normal(k1, (B, S, D), dtype=jnp.float32)
        k = jax.random.normal(k2, (B, S, D), dtype=jnp.float32)
        v = jax.random.normal(k3, (B, S, D), dtype=jnp.float32)
        return {'q': q, 'k': k, 'v': v}
    _L1_xattn_all = _L1_xattn_setup()
    _L1_xattn_in = {k: v for k, v in _L1_xattn_all.items() if k in ()}
    del _L1_xattn_all

    def _L1_ffn_setup():
        import jax, jax.numpy as jnp
        import numpy as np
        B, M, D, E, K = (512, 4, 128, 8, 2)
        H = 4 * D
        key = jax.random.key(seed)
        k0, k1, k2, k3 = jax.random.split(key, 4)
        x = jax.random.normal(k0, (B, M, D), jnp.float32)
        Wg = jax.random.normal(k1, (D, E), jnp.float32) * D ** (-0.5)
        bg = jnp.zeros((E,), jnp.float32)
        W1 = jax.random.normal(k2, (E, D, H), jnp.float32) * D ** (-0.5)
        b1 = jnp.zeros((E, H), jnp.float32)
        W2 = jax.random.normal(k3, (E, H, D), jnp.float32) * H ** (-0.5)
        b2 = jnp.zeros((E, D), jnp.float32)
        return {'x': x, 'Wg': Wg, 'bg': bg, 'W1': W1, 'b1': b1, 'W2': W2, 'b2': b2}
    _L1_ffn_all = _L1_ffn_setup()
    _L1_ffn_in = {k: v for k, v in _L1_ffn_all.items() if k in ('Wg', 'bg', 'W1', 'b1', 'W2', 'b2')}
    del _L1_ffn_all
    return {'x': x, 'ctx_1024': ctx_1024, 'L0_attn_qkv_w': _L0_attn_in['qkv_w'], 'L0_attn_qkv_b': _L0_attn_in['qkv_b'], 'L0_attn_out_w': _L0_attn_in['out_w'], 'L0_attn_out_b': _L0_attn_in['out_b'], 'L0_attn_decay_alpha': _L0_attn_in['decay_alpha'], 'L0_xattn_Wq1': _L0_xattn_in['Wq1'], 'L0_xattn_bq1': _L0_xattn_in['bq1'], 'L0_xattn_Wk1': _L0_xattn_in['Wk1'], 'L0_xattn_bk1': _L0_xattn_in['bk1'], 'L0_xattn_Wv1': _L0_xattn_in['Wv1'], 'L0_xattn_bv1': _L0_xattn_in['bv1'], 'L0_xattn_Wo1': _L0_xattn_in['Wo1'], 'L0_xattn_bo1': _L0_xattn_in['bo1'], 'L0_xattn_Wq2': _L0_xattn_in['Wq2'], 'L0_xattn_bq2': _L0_xattn_in['bq2'], 'L0_xattn_Wk2': _L0_xattn_in['Wk2'], 'L0_xattn_bk2': _L0_xattn_in['bk2'], 'L0_xattn_Wv2': _L0_xattn_in['Wv2'], 'L0_xattn_bv2': _L0_xattn_in['bv2'], 'L0_xattn_Wo2': _L0_xattn_in['Wo2'], 'L0_xattn_bo2': _L0_xattn_in['bo2'], 'L0_ffn_gate_w': _L0_ffn_in['gate_w'], 'L0_ffn_gate_b': _L0_ffn_in['gate_b'], 'L0_ffn_w1': _L0_ffn_in['w1'], 'L0_ffn_b1': _L0_ffn_in['b1'], 'L0_ffn_w2': _L0_ffn_in['w2'], 'L0_ffn_b2': _L0_ffn_in['b2'], 'L1_attn_Wq': _L1_attn_in['Wq'], 'L1_attn_Wk': _L1_attn_in['Wk'], 'L1_attn_Wv': _L1_attn_in['Wv'], 'L1_attn_W_out': _L1_attn_in['W_out'], 'L1_attn_b_out': _L1_attn_in['b_out'], 'L1_ffn_Wg': _L1_ffn_in['Wg'], 'L1_ffn_bg': _L1_ffn_in['bg'], 'L1_ffn_W1': _L1_ffn_in['W1'], 'L1_ffn_b1': _L1_ffn_in['b1'], 'L1_ffn_W2': _L1_ffn_in['W2'], 'L1_ffn_b2': _L1_ffn_in['b2']}

def reference(x, ctx_1024, L0_attn_qkv_w, L0_attn_qkv_b, L0_attn_out_w, L0_attn_out_b, L0_attn_decay_alpha, L0_xattn_Wq1, L0_xattn_bq1, L0_xattn_Wk1, L0_xattn_bk1, L0_xattn_Wv1, L0_xattn_bv1, L0_xattn_Wo1, L0_xattn_bo1, L0_xattn_Wq2, L0_xattn_bq2, L0_xattn_Wk2, L0_xattn_bk2, L0_xattn_Wv2, L0_xattn_bv2, L0_xattn_Wo2, L0_xattn_bo2, L0_ffn_gate_w, L0_ffn_gate_b, L0_ffn_w1, L0_ffn_b1, L0_ffn_w2, L0_ffn_b2, L1_attn_Wq, L1_attn_Wk, L1_attn_Wv, L1_attn_W_out, L1_attn_b_out, L1_ffn_Wg, L1_ffn_bg, L1_ffn_W1, L1_ffn_b1, L1_ffn_W2, L1_ffn_b2):
    import jax
    import jax.numpy as jnp

    def _L0_attn_ref(x, qkv_w, qkv_b, out_w, out_b, decay_alpha):
        import jax, jax.numpy as jnp
        import numpy as np
        D_MODEL = 128
        NHEAD = 16
        HEAD_DIM = D_MODEL // NHEAD
        SCALE = float(np.sqrt(HEAD_DIM))
        B, T, D = x.shape
        qkv = x @ qkv_w.T + qkv_b
        qkv = qkv.reshape(B, T, 3, NHEAD, HEAD_DIM).transpose(2, 0, 3, 1, 4)
        q, k, v = (qkv[0], qkv[1], qkv[2])
        logits = jnp.einsum('bhqd,bhkd->bhqk', q, k) / SCALE
        pos = jnp.arange(T, dtype=jnp.float32)
        dist = jnp.abs(pos[None, :] - pos[:, None])
        alpha = jax.nn.softplus(decay_alpha)
        logits = logits - alpha[:, None, None] * dist[None]
        attn = jax.nn.softmax(logits, axis=-1)
        out = jnp.einsum('bhqk,bhkd->bhqd', attn, v)
        out = out.transpose(0, 2, 1, 3).reshape(B, T, D)
        out = out @ out_w.T + out_b
        return out

    def _L0_xattn_ref(x, encoder_k, encoder_v, Wq1, bq1, Wk1, bk1, Wv1, bv1, Wo1, bo1, Wq2, bq2, Wk2, bk2, Wv2, bv2, Wo2, bo2):
        import jax, jax.numpy as jnp
        import numpy as np
        B, SD, SE, D, H = (4, 256, 256, 128, 16)
        HD = D // H

        def _mha(xq, xk, xv, Wq, bq, Wk, bk, Wv, bv, Wo, bo, causal):
            q = jnp.einsum('bsd,hde->bhse', xq, Wq) + bq[None, :, None, :]
            k = jnp.einsum('bsd,hde->bhse', xk, Wk) + bk[None, :, None, :]
            v = jnp.einsum('bsd,hde->bhse', xv, Wv) + bv[None, :, None, :]
            scale = 1.0 / jnp.sqrt(jnp.asarray(HD, q.dtype))
            scores = jnp.einsum('bhqe,bhke->bhqk', q, k) * scale
            if causal:
                mask = jnp.tril(jnp.ones((q.shape[2], k.shape[2]), bool))
                scores = jnp.where(mask, scores, jnp.finfo(scores.dtype).min)
            w = jax.nn.softmax(scores, axis=-1)
            out = jnp.einsum('bhqk,bhke->bhqe', w, v)
            out = out.transpose(0, 2, 1, 3).reshape(out.shape[0], out.shape[2], D)
            return out @ Wo + bo
        h = _mha(x, x, x, Wq1, bq1, Wk1, bk1, Wv1, bv1, Wo1, bo1, causal=True)
        out = _mha(h, encoder_k, encoder_v, Wq2, bq2, Wk2, bk2, Wv2, bv2, Wo2, bo2, causal=False)
        return out

    def _L0_ffn_ref(h, gate_w, gate_b, w1, b1, w2, b2):
        import math
        import jax, jax.numpy as jnp
        import numpy as np
        B, L, D, F_FF, E = (4, 256, 128, 512, 8)
        TOP_K = 1
        CAPACITY_FACTOR = 1.25
        Bh, Lh, Dh = h.shape
        T = Bh * Lh
        capacity = max(1, math.ceil(CAPACITY_FACTOR * (T * TOP_K / E)))
        x = h.reshape(T, Dh)
        logits = x @ gate_w.T + gate_b
        probs = jax.nn.softmax(logits, axis=-1)
        idx = jnp.argmax(probs, axis=-1)
        top_prob = jnp.max(probs, axis=-1)
        one_hot = jax.nn.one_hot(idx, E, dtype=jnp.int32)
        pos = jnp.take_along_axis(jnp.cumsum(one_hot, axis=0), idx[:, None], axis=1)[:, 0] - 1
        keep = pos < capacity
        safe_pos = jnp.where(keep, pos, 0)
        buf = jnp.zeros((E, capacity, Dh), dtype=x.dtype)
        buf = buf.at[idx, safe_pos].add(x * keep[:, None].astype(x.dtype))
        hdn = jax.nn.relu(jnp.einsum('ecd,edf->ecf', buf, w1) + b1[:, None, :])
        eout = jnp.einsum('ecf,efd->ecd', hdn, w2) + b2[:, None, :]
        gathered = eout[idx, safe_pos]
        out = gathered * (top_prob * keep.astype(x.dtype))[:, None]
        return out.reshape(Bh, Lh, Dh)

    def _L1_attn_ref(x, Wq, Wk, Wv, W_out, b_out):
        import jax, jax.numpy as jnp
        import numpy as np
        import math
        B, S, E, H = (2, 256, 128, 16)
        D = E // H
        b, s, e = x.shape
        xh = x.reshape(b, s, H, D)
        q = jnp.einsum('bshd,ed->bshe', xh, Wq)
        k = jnp.einsum('bshd,ed->bshe', xh, Wk)
        v = jnp.einsum('bshd,ed->bshe', xh, Wv)
        energy = jnp.einsum('bqhd,bkhd->bhqk', q, k) / jnp.sqrt(jnp.float32(e))
        attn = jax.nn.softmax(energy, axis=-1)
        out = jnp.einsum('bhqk,bkhd->bqhd', attn, v).reshape(b, s, e)
        return out @ W_out.T + b_out

    def _L1_xattn_ref(q, k, v):
        import jax, jax.numpy as jnp
        import numpy as np
        DECAY = 0.9
        kv = jnp.swapaxes(k * v, 0, 1)

        def step(r, kv_t):
            r = DECAY * r + kv_t
            return (r, r)
        r0 = jnp.zeros(q.shape[:1] + q.shape[2:], dtype=q.dtype)
        _, rs = jax.lax.scan(step, r0, kv)
        return q * jnp.swapaxes(rs, 0, 1)

    def _L1_ffn_ref(x, Wg, bg, W1, b1, W2, b2):
        import jax, jax.numpy as jnp
        import numpy as np
        B, M, D, E, K = (512, 4, 128, 8, 2)
        H = 4 * D
        Bn, Mn, Dn = x.shape
        xf = x.reshape(-1, Dn)
        logits = xf @ Wg + bg
        topv, topi = jax.lax.top_k(logits, K)
        topw = jax.nn.softmax(topv, axis=-1)
        gates = jnp.sum(jax.nn.one_hot(topi, E, dtype=xf.dtype) * topw[..., None], axis=1)

        def body(acc, p):
            W1e, b1e, W2e, b2e, ge = p
            y = jax.nn.gelu(xf @ W1e + b1e, approximate=False) @ W2e + b2e
            return (acc + ge[:, None] * y, None)
        out, _ = jax.lax.scan(body, jnp.zeros_like(xf), (W1, b1, W2, b2, gates.T))
        return out.reshape(Bn, Mn, Dn)
    x = x + _L0_attn_ref(_layernorm(x, axis=-1), L0_attn_qkv_w, L0_attn_qkv_b, L0_attn_out_w, L0_attn_out_b, L0_attn_decay_alpha)
    x = x + _L0_xattn_ref(_layernorm(x, axis=-1), ctx_1024, ctx_1024, L0_xattn_Wq1, L0_xattn_bq1, L0_xattn_Wk1, L0_xattn_bk1, L0_xattn_Wv1, L0_xattn_bv1, L0_xattn_Wo1, L0_xattn_bo1, L0_xattn_Wq2, L0_xattn_bq2, L0_xattn_Wk2, L0_xattn_bk2, L0_xattn_Wv2, L0_xattn_bv2, L0_xattn_Wo2, L0_xattn_bo2)
    x = x + _L0_ffn_ref(_layernorm(x, axis=-1), L0_ffn_gate_w, L0_ffn_gate_b, L0_ffn_w1, L0_ffn_b1, L0_ffn_w2, L0_ffn_b2)
    x = x + _L1_attn_ref(_layernorm(x, axis=-1), L1_attn_Wq, L1_attn_Wk, L1_attn_Wv, L1_attn_W_out, L1_attn_b_out)
    x = x + _L1_xattn_ref(_layernorm(x, axis=-1), ctx_1024, ctx_1024)
    x = x + _L1_ffn_ref(_layernorm(x, axis=-1), L1_ffn_Wg, L1_ffn_bg, L1_ffn_W1, L1_ffn_b1, L1_ffn_W2, L1_ffn_b2)
    return x

_drawn_inputs = setup_inputs


def setup_inputs(seed=0):
    import zlib

    import numpy as np

    out = dict(_drawn_inputs(seed))
    spreads = {'L0_attn_decay_alpha': (0.10000000149011612, 0.6),
     'L0_xattn_bq1': (0.0, 0.8),
     'L0_xattn_bk1': (0.0, 0.8),
     'L0_xattn_bv1': (0.0, 0.427),
     'L0_xattn_bo1': (0.0, 0.365),
     'L0_xattn_bq2': (0.0, 0.347),
     'L0_xattn_bk2': (0.0, 0.8),
     'L0_xattn_bv2': (0.0, 0.1),
     'L0_xattn_bo2': (0.0, 0.1),
     'L0_ffn_gate_b': (0.0, 0.554),
     'L0_ffn_b1': (0.0, 0.8),
     'L0_ffn_b2': (0.0, 0.56),
     'L1_attn_b_out': (0.0, 0.1),
     'L1_ffn_bg': (0.0, 0.726),
     'L1_ffn_b1': (0.0, 0.8),
     'L1_ffn_b2': (0.0, 0.8)}
    factors = {'L0_ffn_gate_w': 3.578, 'L0_ffn_w1': 6.779, 'L0_ffn_w2': 5.32}
    for name, (base, spread) in spreads.items():
        noise = np.random.default_rng([zlib.crc32(name.encode()), seed]).standard_normal(out[name].shape)
        drawn = base * np.exp(spread * noise) if base else spread * noise
        out[name] = jnp.asarray(drawn.astype(out[name].dtype))
    for name, factor in factors.items():
        out[name] = (out[name] * factor).astype(out[name].dtype)
    return out
```

```python
from contextlib import ExitStack, contextmanager

import numpy as np
import concourse.bass as bass
from concourse import mybir

ALU = mybir.AluOpType
ACT = mybir.ActivationFunctionType
AX = mybir.AxisListType
F32 = mybir.dt.float32
BF16 = mybir.dt.bfloat16
U32 = mybir.dt.uint32

P = 128
NSEQ = 32
H = 16
HD = 8
GS = 2
NG = NSEQ // GS
GT = GS * P
RING = 4
HB = 4
NB = H // HB
EPS = 1e-5
DECAY = 0.9
NE = 8
FF = 512
FC = FF // P
CAP = 640
TB = 8
BT = NSEQ * P // TB

Q_PART = (0, 0, 0, 1, 1, 2)
K_PART = (0, 1, 2, 0, 1, 0)
PAIRS = len(Q_PART)
ROWS_QK = PAIRS * HD
ROWS_ALL = ROWS_QK + 2


def wait(eng, sem, count, most=None, unit=1):
    if isinstance(count, int):
        if most is not None:
            count = min(count, most)
        if count <= 0:
            return
    eng.wait_ge(sem, count * unit)


def settle(eng, passed):
    eng.sem_inc(passed, 1)


@contextmanager
def semaphores(nc):
    taken = []

    def take(name):
        taken.append(nc.alloc_semaphore(name))
        return taken[-1]

    yield take
    nc.clear_and_free_semaphores(taken)
    nc.all_engine_barrier()


def attention_stage(nc, name, X, w, scale, extra, q_from_h, kv_dram, h_out, hT, const, x_dram=None):
    with semaphores(nc) as take, ExitStack() as ctx:
        def sb(n, shape, dt=F32):
            return ctx.enter_context(nc.sbuf_tensor(f"{name}_{n}", shape, dt))

        def psum(n, shape):
            return ctx.enter_context(nc.psum_tensor(f"{name}_{n}", shape, F32))

        def sem(n):
            return take(f"{name}_{n}")

        own_kv = kv_dram is None
        ps_s = psum("ps_s", [P, 2, 512])
        ps_t = psum("ps_t", [P, 2, 512])
        ps_o = psum("ps_o", [P, NB, P])
        ps_x = psum("ps_x", [P, 512])
        ps_q = psum("ps_q", [P, 512])
        ps_e = psum("ps_e", [P, 512])

        wq, wk, wv, wo = (sb(k, [P, P]) for k in ("wq", "wk", "wv", "wo"))
        bq, bk = sb("bq", [P, 1]), sb("bk", [P, 1])
        bqs = sb("bqs", [P, 1])
        bv, bo = sb("bv", [P, P]), sb("bo", [P, P])
        bo_col = sb("bo_col", [P, 1])
        xn = sb("xn", [P, 2, GS, P])
        stat6 = sb("stat6", [P, GS, 6])
        stat = sb("stat", [P, GS, 2])
        vareps = sb("vareps", [P, GS])
        rstd = sb("rstd", [P, GS])
        xnT = sb("xnT", [P, GT])
        qf, kf = sb("qf", [P, GT]), sb("kf", [P, GT])
        rest = sb("rest", [P, GT])
        qp, kp = sb("qp", [P, 3, GT], BF16), sb("kp", [P, 3, GT], BF16)
        qst = sb("qst", [ROWS_ALL, RING, H, GT], BF16)
        kst = sb("kst", [ROWS_ALL, RING, H, GT], BF16)
        v1 = sb("v1", [P, RING, GS, H, 32])
        mx = sb("mx", [P, 2, H])
        mp = sb("mp", [H, 2, 2, P], BF16)
        pt = sb("pt", [P, NB, HB * P])
        osb = sb("osb", [P, GS, NB * P])
        rden = sb("rden", [P, H])
        on = sb("on", [P, GS, P])
        oT = sb("oT", [P, GT])

        passed_pool, passed_dve, passed_sync = sem("passed_pool"), sem("passed_dve"), sem("passed_sync")
        w_in = sem("w_in")
        bias_ready = sem("bias_ready")
        set_up = sem("set_up")
        in_dma = [sem(f"in_dma{k}") for k in range(6 if x_dram is not None else 2)]
        stats_a, stats_ready, var_ready, rstd_ready = sem("stats_a"), sem("stats_ready"), sem("var_ready"), sem("rstd_ready")
        xn_ready, xtr_done, xT_ready = sem("xn_ready"), sem("xtr_done"), sem("xT_ready")
        q_done, k_done, v_done = sem("q_done"), sem("k_done"), sem("v_done")
        qf_ready, kf_ready, v_ready = sem("qf_ready"), sem("kf_ready"), sem("v_ready")
        part, q_split, k_split = sem("part"), sem("q_split"), sem("k_split")
        stack_dma = [sem(f"stack_dma{k}") for k in range(RING)]
        s_ready, s_max = sem("s_ready"), sem("s_max")
        mtr_done, m_hi, m_split = sem("mtr_done"), sem("m_hi"), sem("m_split")
        m_dma = [sem(f"m_dma{k}") for k in range(2)]
        t_ready, p_ready, pv_done = sem("t_ready"), sem("p_ready"), sem("pv_done")
        o_copied, otr_done, den_ready, o_normed = sem("o_copied"), sem("otr_done"), sem("den_ready"), sem("o_normed")
        ontr_done, oT_ready, oproj_done, biased, x_done = sem("ontr_done"), sem("oT_ready"), sem("oproj_done"), sem("biased"), sem("x_done")

        N_W = 4 + (2 if w["bq"] is not None else 0) + (1 if w["bv"] is not None else 0) + 1

        def schedule(eng, body, engines_loop):
            for i in range(-4, 1):
                body(eng, i, i % RING, i // RING)
            with engines_loop(0, 3) as lap:
                for t in range(1, 1 + RING):
                    body(eng, lap * RING + t, t % RING, lap + t // RING)
            for i in range(1 + 3 * RING, NG + 1):
                body(eng, i, i % RING, i // RING)

        def wrap(g):
            return g if isinstance(g, int) else g % NG

        def seq_on(n):
            return not isinstance(n, int) or 0 <= n < NSEQ

        def group_on(g):
            return not isinstance(g, int) or 0 <= g < NG

        block = ctx.enter_context(nc.Block())

        @block.sync
        def _(sync):
            for tile, key in ((wq, "wq"), (wk, "wk"), (wv, "wv"), (wo, "wo")):
                sync.dma_start(tile[:, :], w[key]).then_inc(w_in, 16)
            if w["bq"] is not None:
                sync.dma_start(bq[:, :], w["bq"]).then_inc(w_in, 16)
                sync.dma_start(bk[:, :], w["bk"]).then_inc(w_in, 16)
            if w["bv"] is not None:
                sync.dma_start(bv[:, :], w["bv"].partition_broadcast(P)).then_inc(w_in, 16)
            if h_out:
                sync.dma_start(bo_col[:, :], w["bo"].rearrange("(a b) -> a b", b=1)).then_inc(w_in, 16)
            else:
                sync.dma_start(bo[:, :], w["bo"].partition_broadcast(P)).then_inc(w_in, 16)
            if x_dram is not None:
                for g in range(NG):
                    sync.dma_start(X[:, GS * g:GS * (g + 1), :],
                                   x_dram[GS * g:GS * (g + 1)].rearrange("s t d -> t s d")).then_inc(in_dma[min(g, 5)], 16)
            sync.wait_ge(set_up, 2)

            def body(sync, i, r, lap):
                p1, p2 = i + 4, i + 3
                if not own_kv and group_on(p1):
                    wait(sync, xtr_done, p1 - 1)
                    settle(sync, passed_sync)
                    sync.dma_start(xn[:, r % 2, :, :], kv_dram[bass.ds(wrap(p1) * GS, GS)].rearrange("s t d -> t s d")).then_inc(in_dma[r % 2], 16)
                if seq_on(2 * i + 2):
                    max_rows(sync, 2 * i + 2, 0, (r + 1) % RING)
                if group_on(p2):
                    slot = (r + 3) % RING
                    wait(sync, t_ready, (p2 - RING + 1) * GS * NB)
                    settle(sync, passed_sync)
                    wait(sync, q_split, p2 + 1)
                    for k in range(PAIRS):
                        sync.dma_start(qst[HD * k:HD * (k + 1), slot, :, :], qp[:, Q_PART[k], :]).then_inc(stack_dma[slot], 16)
                if seq_on(2 * i + 3):
                    max_rows(sync, 2 * i + 3, 1, (r + 1) % RING)
                if group_on(p2):
                    wait(sync, k_split, p2 + 1)
                    for k in range(PAIRS):
                        sync.dma_start(kst[HD * k:HD * (k + 1), slot, :, :], kp[:, K_PART[k], :]).then_inc(stack_dma[slot], 16)

            def max_rows(sync, m, s, slot):
                wait(sync, m_split, m + 1)
                settle(sync, passed_sync)
                for k in range(2):
                    sync.dma_start(qst[ROWS_QK + k:ROWS_QK + k + 1, slot, :, s * P:(s + 1) * P],
                                   mp[:, s, k, :]).then_inc(m_dma[s], 16)

            schedule(sync, body, sync.Fori)

        @block.gpsimd
        def _(pool):
            nc.gpsimd.memset(v1[:, :, :, :, :], 0.0).then_inc(part, 1)
            pool.wait_ge(part, 1)
            nc.gpsimd.memset(v1[:, :, :, :, HD:HD + 1], 1.0).then_inc(set_up, 1)
            pool.wait_ge(set_up, 1)
            nc.gpsimd.memset(kst[32:ROWS_ALL, :, :, :], 1.0).then_inc(set_up, 1)

            def split(pool, src, dst, ready, done, g, n0):
                wait(pool, ready, g + 1)
                settle(pool, passed_pool)
                nc.gpsimd.tensor_copy(dst[:, 0, :], src[:, :]).then_inc(part, 1)
                wait(pool, part, n0 + 1)
                nc.gpsimd.tensor_tensor(rest[:, :], src[:, :], dst[:, 0, :], ALU.subtract).then_inc(part, 1)
                wait(pool, part, n0 + 2)
                settle(pool, passed_pool)
                nc.gpsimd.tensor_copy(dst[:, 1, :], rest[:, :]).then_inc(part, 1)
                wait(pool, part, n0 + 3)
                nc.gpsimd.tensor_tensor(dst[:, 2, :], rest[:, :], dst[:, 1, :], ALU.subtract).then_inc(done, 1)

            def body(pool, i, r, lap):
                p1, p2 = i + 4, i + 3
                if group_on(p2):
                    prev = (r + 2) % RING
                    wait(pool, stack_dma[prev], lap + (r + 2) // RING + 1, unit=16 * 2 * PAIRS)
                    wait(pool, k_split, p2)
                    split(pool, qf, qp, qf_ready, q_split, p2, 1 + 6 * p2)
                    wait(pool, q_split, p2 + 1)
                    split(pool, kf, kp, kf_ready, k_split, p2, 1 + 6 * p2 + 3)
                if own_kv and group_on(p1):
                    wait(pool, stats_ready, p1 + 1)
                    settle(pool, passed_pool)
                    nc.gpsimd.tensor_scalar(vareps[:, :], stat[:, :, 1], EPS, None, ALU.add).then_inc(var_ready, 1)
                    wait(pool, var_ready, p1 + 1)
                    nc.gpsimd.tensor_tensor(rstd[:, :], vareps[:, :], const["minus_half"][:, 0:GS], ALU.pow).then_inc(rstd_ready, 1)

            schedule(pool, body, pool.Fori)

        @block.vector
        def _(dve):
            dve.wait_ge(w_in, 16 * N_W)
            if w["bq"] is not None:
                dve.tensor_scalar(bqs[:, :], bq[:, :], scale, None, ALU.mult).then_inc(bias_ready, 1)
            dve.wait_ge(set_up, 2)

            def smax(dve, m, s, c):
                wait(dve, s_ready, m * NB + c + 1)
                if c == 0:
                    wait(dve, mtr_done, m - 1)
                dve.tensor_reduce(mx[:, s, HB * c:HB * (c + 1)], ps_s[:, c % 2, :].rearrange("q (h k) -> q h k", h=HB),
                                  AX.X, ALU.max).then_inc(s_max, 1)

            def msplit(dve, m, s, uses):
                wait(dve, mtr_done, m + 1)
                wait(dve, m_dma[s], uses, unit=32)
                dve.tensor_scalar(mp[:, s, 0, :], ps_q[0:H, 0:P], -1.0, None, ALU.mult).then_inc(m_hi, 1)
                wait(dve, m_hi, m + 1)
                dve.scalar_tensor_tensor(out=mp[:, s, 1, :], in0=ps_q[0:H, 0:P], scalar=-1.0, in1=mp[:, s, 0, :],
                                         op0=ALU.mult, op1=ALU.subtract).then_inc(m_split, 1)

            def normalise(dve, n, s):
                wait(dve, otr_done, n + 1)
                heads = ps_e[:, :].rearrange("q (h e) -> q h e", e=32)
                dve.reciprocal(rden[:, :], heads[:, :, HD:HD + 1].rearrange("q h e -> q (h e)")).then_inc(den_ready, 1)
                wait(dve, den_ready, n + 1)
                dve.tensor_tensor(on[:, s, :].rearrange("q (h e) -> q h e", e=HD), heads[:, :, 0:HD],
                                  rden[:, :].unsqueeze(2).to_broadcast([P, H, HD]), ALU.mult).then_inc(o_normed, 1)

            def body(dve, i, r, lap):
                p1, p2 = i + 4, i + 3
                for s in range(GS):
                    m = 2 * i + 3 + s
                    for c in range(NB):
                        if seq_on(m):
                            smax(dve, m, (1 + s) % 2, c)
                        at = (s, c)
                        if at == (0, 0) and seq_on(2 * i - 2):
                            normalise(dve, 2 * i - 2, 0)
                        if at == (0, 1) and seq_on(2 * i + 2):
                            msplit(dve, 2 * i + 2, 0, i + 1)
                        if at == (0, 2) and own_kv and group_on(p1):
                            if x_dram is not None:
                                if isinstance(p1, int) and p1 < 5:
                                    dve.wait_ge(in_dma[p1], 16)
                                if isinstance(p1, int) and p1 == 4:
                                    dve.wait_ge(in_dma[5], 16 * (NG - 5))
                            wait(dve, xn_ready, GS * p1)
                            for j in range(GS):
                                dve.bn_stats(stat6[:, j, :], X[:, bass.ds(wrap(p1) * GS + j, 1), :].rearrange("t s d -> t (s d)")).then_inc(stats_a, 1)
                            for j in range(GS):
                                wait(dve, stats_a, GS * p1 + j + 1)
                                settle(dve, passed_dve)
                                op = dve.bn_aggr(stat[:, j, :], stat6[:, j, :])
                            op.then_inc(stats_ready, 1)
                        if at == (0, 3) and seq_on(2 * i - 1):
                            normalise(dve, 2 * i - 1, 1)
                        if at == (1, 0) and own_kv and group_on(p1):
                            wait(dve, rstd_ready, p1 + 1)
                            wait(dve, xtr_done, p1 - 1)
                            for j in range(GS):
                                dve.tensor_scalar(xn[:, r % 2, j, :], X[:, bass.ds(wrap(p1) * GS + j, 1), :].rearrange("t s d -> t (s d)"),
                                                  stat[:, j, 0:1], rstd[:, j:j + 1], ALU.subtract, ALU.mult).then_inc(xn_ready, 1)
                        if at == (1, 1) and seq_on(2 * i + 3):
                            msplit(dve, 2 * i + 3, 1, i + 1)
                        if at == (1, 1) and group_on(p2):
                            wait(dve, v_done, p2 + 1)
                            wait(dve, pv_done, (p2 - RING + 1) * GS * NB)
                            out = v1[:, (r + 3) % RING, :, :, 0:HD]
                            vals = ps_x[:, 0:GT].rearrange("t (s h e) -> t s h e", s=GS, e=HD)
                            if w["bv"] is not None:
                                for j in range(GS):
                                    op = dve.tensor_tensor(out[:, j], vals[:, j], bv[:, :].rearrange("t (h e) -> t h e", e=HD), ALU.add)
                            else:
                                op = dve.tensor_copy(out, vals)
                            op.then_inc(v_ready, 1)
                        if at == (1, 2) and group_on(i - 1) and not h_out:
                            g = i - 1
                            wait(dve, oproj_done, g + 1)
                            res = ps_e[:, 0:GT].rearrange("t (s d) -> t s d", s=GS)
                            dve.tensor_tensor(res, res, bo[:, :].unsqueeze(1).to_broadcast([P, GS, P]), ALU.add).then_inc(biased, 1)
                            wait(dve, biased, g + 1)
                            xg = X[:, bass.ds(g * GS, GS), :]
                            dve.tensor_tensor(xg, xg, res, ALU.add).then_inc(x_done, 1)

            schedule(dve, body, dve.Fori)

        @block.scalar
        def _(act):
            act.wait_ge(w_in, 16 * N_W)
            if w["bq"] is not None:
                act.wait_ge(bias_ready, 1)

            def exp_bank(act, n, c):
                wait(act, t_ready, n * NB + c + 1)
                wait(act, pv_done, (n - 1) * NB + c + 1)
                nc.scalar.activation(pt[:, c, :], ps_t[:, c % 2, :], ACT.Exp).then_inc(p_ready, 1)

            def copy_o(act, n, s):
                wait(act, pv_done, (n + 1) * NB)
                wait(act, otr_done, n - 1)
                nc.scalar.activation(osb[:, s, :], ps_o[:, :, :].rearrange("p b q -> p (b q)"), ACT.Identity).then_inc(o_copied, 1)

            def body(act, i, r, lap):
                p1, p2 = i + 4, i + 3
                for s in range(GS):
                    n = 2 * i + s
                    for c in range(NB):
                        if seq_on(n):
                            exp_bank(act, n, c)
                        at = (s, c)
                        if at == (0, 0) and seq_on(2 * i - 1):
                            copy_o(act, 2 * i - 1, 1)
                        if at == (0, 1) and group_on(p2):
                            wait(act, q_done, p2 + 1)
                            wait(act, q_split, p2)
                            nc.scalar.activation(qf[:, :], ps_q[:, 0:GT], ACT.Identity, scale=scale,
                                                 **({"bias": bqs[:, :]} if w["bq"] is not None else {})).then_inc(qf_ready, 1)
                        if at == (0, 3) and group_on(p2):
                            wait(act, k_done, p2 + 1)
                            wait(act, k_split, p2)
                            nc.scalar.activation(kf[:, :], ps_q[:, 0:GT], ACT.Identity,
                                                 **({"bias": bk[:, :]} if w["bq"] is not None else {})).then_inc(kf_ready, 1)
                        if at == (1, 0) and seq_on(2 * i):
                            copy_o(act, 2 * i, 0)
                        if at == (1, 1) and group_on(i - 1):
                            wait(act, ontr_done, i)
                            wait(act, oproj_done, i - 1)
                            nc.scalar.activation(oT[:, :], ps_e[:, 0:GT], ACT.Identity).then_inc(oT_ready, 1)
                        if at == (1, 2) and group_on(i - 1) and h_out:
                            wait(act, oproj_done, i)
                            nc.scalar.activation(hT[:, bass.ds((i - 1) * GT, GT)], ps_e[:, 0:GT], ACT.Identity,
                                                 bias=bo_col[:, :]).then_inc(x_done, 1)
                        if at == (1, 3) and group_on(p1):
                            wait(act, xtr_done, p1 + 1)
                            wait(act, v_done, p1)
                            nc.scalar.activation(xnT[:, :], ps_x[:, 0:GT], ACT.Identity).then_inc(xT_ready, 1)

            schedule(act, body, act.Fori)

        @block.tensor
        def _(pe):
            pe.wait_ge(w_in, 16 * N_W)

            def scores(pe, m, s, c, slot, uses):
                wait(pe, s_max, m * NB + c - 1)
                if c == 0:
                    wait(pe, stack_dma[slot], uses, unit=16 * 2 * PAIRS)
                if extra == "alibi":
                    pe.matmul(ps_s[:, c % 2, :], const["dist"][:, :], const["slope"][:, 0, HB * c:HB * (c + 1), :],
                              start=True, stop=False, skip_group_check=True)
                if extra == "causal":
                    pe.matmul(ps_s[:, c % 2, :], const["ident16"][:, :], const["mask_qk"][:, :, :],
                              start=True, stop=False, skip_group_check=True)
                for j in range(HB):
                    h = HB * c + j
                    op = pe.matmul(ps_s[:, c % 2, j * P:(j + 1) * P], qst[0:ROWS_QK, slot, h, s * P:(s + 1) * P],
                                   kst[0:ROWS_QK, slot, h, s * P:(s + 1) * P], start=extra is None, stop=True, skip_group_check=extra is not None)
                op.then_inc(s_ready, 1)

            def scores_t(pe, n, s, c, slot, i):
                wait(pe, p_ready, n * NB + c - 1)
                if c == 0:
                    wait(pe, m_dma[s], i + 1, unit=32)
                if extra == "alibi":
                    for k in range(3):
                        pe.matmul(ps_t[:, c % 2, :], const["dist"][:, :], const["slope"][:, k, HB * c:HB * (c + 1), :],
                                  start=k == 0, stop=False, skip_group_check=True)
                if extra == "causal":
                    pe.matmul(ps_t[:, c % 2, :], const["ident16"][:, :], const["mask_kq"][:, :, :],
                              start=True, stop=False, skip_group_check=True)
                for j in range(HB):
                    h = HB * c + j
                    op = pe.matmul(ps_t[:, c % 2, j * P:(j + 1) * P], kst[0:ROWS_ALL, slot, h, s * P:(s + 1) * P],
                                   qst[0:ROWS_ALL, slot, h, s * P:(s + 1) * P], start=extra is None, stop=True, skip_group_check=extra is not None)
                op.then_inc(t_ready, 1)

            def weigh(pe, n, s, c, slot, g):
                wait(pe, p_ready, n * NB + c + 1)
                if c == 0:
                    wait(pe, o_copied, n)
                    wait(pe, v_ready, g + 1)
                for j in range(HB):
                    op = pe.matmul(ps_o[32 * j:32 * (j + 1), c, :], v1[:, slot, s, HB * c + j, :],
                                   pt[:, c, j * P:(j + 1) * P], start=True, stop=True, tile_position=(0, 32 * j))
                op.then_inc(pv_done, 1)

            def body(pe, i, r, lap):
                p1, p2 = i + 4, i + 3
                for s in range(GS):
                    m, n = 2 * i + 3 + s, 2 * i + s
                    m_slot = (r + 1 + s) % RING
                    for c in range(NB):
                        at = (s, c)
                        if seq_on(m):
                            scores(pe, m, (1 + s) % 2, c, m_slot, lap + (r + 1 + s) // RING + 1)
                        if seq_on(n):
                            scores_t(pe, n, s, c, r, i)
                        if c > 0 and seq_on(n):
                            weigh(pe, n, s, c - 1, r, i)
                        if c == 0 and seq_on(n - 1):
                            weigh(pe, n - 1, 1 - s, NB - 1, (r - 1 + s) % RING, i - 1 + s)
                        if at == (0, 0) and group_on(p2):
                            wait(pe, xT_ready, p2 + 1)
                            wait(pe, m_split, 2 * i + 2, NSEQ)
                            wait(pe, kf_ready, p2)
                            src = hT[:, bass.ds(p2 * GT, GT)] if q_from_h else xnT[:, :]
                            pe.matmul(ps_q[:, 0:GT], wq[:, :], src, start=True, stop=True).then_inc(q_done, 1)
                        if at == (0, 1) and seq_on(2 * i + 2):
                            transpose_max(pe, 2 * i + 2, 0, i)
                        if at == (0, 2) and group_on(p2):
                            wait(pe, m_split, 2 * i + 3, NSEQ)
                            wait(pe, qf_ready, p2 + 1)
                            pe.matmul(ps_q[:, 0:GT], wk[:, :], xnT[:, :], start=True, stop=True).then_inc(k_done, 1)
                        if at == (0, 2) and seq_on(2 * i - 1):
                            transpose_out(pe, 2 * i - 1, 1)
                        if at == (0, 3) and group_on(p2):
                            wait(pe, xT_ready, p2 + 1)
                            for j in range(GS):
                                op = pe.matmul(ps_x[:, j * P:(j + 1) * P], xnT[:, j * P:(j + 1) * P], wv[:, :], start=True, stop=True)
                            op.then_inc(v_done, 1)
                        if at == (1, 0) and group_on(i - 1):
                            wait(pe, o_normed, 2 * i)
                            for j in range(GS):
                                op = pe.transpose(ps_e[:, j * P:(j + 1) * P], on[:, j, :], const["ident"][:, :])
                            op.then_inc(ontr_done, 1)
                        if at == (1, 1) and seq_on(2 * i + 3):
                            transpose_max(pe, 2 * i + 3, 1, i)
                        if at == (1, 2) and group_on(i - 1):
                            wait(pe, oT_ready, i)
                            if h_out:
                                op = pe.matmul(ps_e[:, 0:GT], wo[:, :], oT[:, :], start=True, stop=True)
                            else:
                                for j in range(GS):
                                    op = pe.matmul(ps_e[:, j * P:(j + 1) * P], oT[:, j * P:(j + 1) * P], wo[:, :], start=True, stop=True)
                            op.then_inc(oproj_done, 1)
                        if at == (1, 2) and group_on(p1):
                            if own_kv:
                                wait(pe, xn_ready, GS * (p1 + 1))
                            else:
                                wait(pe, in_dma[r % 2], 2 * lap + r // 2 + 3, unit=16)
                            wait(pe, v_ready, p1)
                            for j in range(GS):
                                op = pe.transpose(ps_x[:, j * P:(j + 1) * P], xn[:, r % 2, j, :], const["ident"][:, :])
                            op.then_inc(xtr_done, 1)
                        if at == (1, 3) and seq_on(2 * i):
                            wait(pe, x_done, i)
                            transpose_out(pe, 2 * i, 0)

            def transpose_max(pe, m, s, i):
                wait(pe, s_max, (m + 1) * NB)
                wait(pe, m_split, m)
                wait(pe, qf_ready if s == 0 else kf_ready, i + 4, NG)
                pe.transpose(ps_q[0:H, 0:P], mx[:, s, :], const["ident"][:, :]).then_inc(mtr_done, 1)

            def transpose_out(pe, n, s):
                wait(pe, o_copied, n + 1)
                wait(pe, o_normed, n)
                for b in range(NB):
                    op = pe.transpose(ps_e[:, b * P:(b + 1) * P], osb[:, s, b * P:(b + 1) * P], const["ident"][:, :])
                op.then_inc(otr_done, 1)

            schedule(pe, body, pe.Fori)


def setup_stage(nc, const, c, alpha):
    with semaphores(nc) as take, ExitStack() as ctx:
        def sb(n, shape, dt=F32):
            return ctx.enter_context(nc.sbuf_tensor(f"set_{n}", shape, dt))

        def sem(n):
            return take(f"set_{n}")

        dist, mask_qk, mask_kq = sb("dist", [P, P]), sb("mqk", [P, P]), sb("mkq", [P, P])
        a = sb("a", [P, H])
        pos, neg, low = sb("pos", [P, H]), sb("neg", [P, H]), sb("low", [P, H])
        slope = sb("slope", [P, H])
        part, rest = sb("part", [P, 3, H], BF16), sb("rest", [P, 2, H])
        landed, step, act_step = sem("landed"), sem("step"), sem("act_step")
        block = ctx.enter_context(nc.Block())

        @block.sync
        def _(sync):
            sync.dma_start(const["ident"][:, :], c["ident"]).then_inc(landed, 16)
            sync.dma_start(dist[:, :], c["dist"]).then_inc(landed, 16)
            sync.dma_start(mask_qk[:, :], c["mask"]).then_inc(landed, 16)
            sync.dma_start(mask_kq[:, :], c["mask_t"]).then_inc(landed, 16)
            sync.dma_start(a[:, :], alpha.partition_broadcast(P)).then_inc(landed, 16)
            sync.wait_ge(landed, 80)

        @block.scalar
        def _(act):
            act.wait_ge(step, 1)
            nc.scalar.activation(low[:, :], neg[:, :], ACT.Exp).then_inc(act_step, 1)
            act.wait_ge(act_step, 1)
            nc.scalar.activation(neg[:, :], low[:, :], ACT.Ln, bias=1.0).then_inc(act_step, 1)

        @block.vector
        def _(dve):
            dve.memset(const["minus_half"][:, :], -0.5)
            dve.wait_ge(landed, 80)
            n = 0

            def then(op):
                nonlocal n
                n += 1
                op.then_inc(step, 1)
                dve.wait_ge(step, n)

            then(dve.scalar_tensor_tensor(out=neg[:, :], in0=a[:, :], scalar=-1.0, in1=a[:, :], op0=ALU.mult, op1=ALU.min))
            then(dve.tensor_scalar(pos[:, :], a[:, :], 0.0, None, ALU.max))
            dve.wait_ge(act_step, 2)
            then(dve.scalar_tensor_tensor(out=slope[:, :], in0=pos[:, :], scalar=-1.0, in1=neg[:, :], op0=ALU.mult, op1=ALU.subtract))
            then(dve.tensor_copy(part[:, 0, :], slope[:, :]))
            then(dve.tensor_tensor(rest[:, 0, :], slope[:, :], part[:, 0, :], ALU.subtract))
            then(dve.tensor_copy(part[:, 1, :], rest[:, 0, :]))
            then(dve.tensor_tensor(part[:, 2, :], rest[:, 0, :], part[:, 1, :], ALU.subtract))
            then(dve.tensor_copy(const["ident16"][:, :], const["ident"][:, :]))
            for k in range(3):
                then(dve.tensor_tensor(const["slope"][:, k, :, :], const["ident16"][:, :].unsqueeze(1).to_broadcast([P, H, P]),
                                       part[:, k, :].unsqueeze(2).to_broadcast([P, H, P]), ALU.mult))
            then(dve.tensor_copy(const["dist"][:, :], dist[:, :]))
            then(dve.tensor_copy(const["mask_qk"][:, :, :], mask_qk[:, :].unsqueeze(1).to_broadcast([P, HB, P])))
            then(dve.tensor_copy(const["mask_kq"][:, :, :], mask_kq[:, :].unsqueeze(1).to_broadcast([P, HB, P])))


def decay_stage(nc, X, ctx_dram, const, weights_dram):
    Q = 4
    with semaphores(nc) as take, ExitStack() as ctx:
        def sb(n, shape, dt=F32):
            return ctx.enter_context(nc.sbuf_tensor(f"decay_{n}", shape, dt))

        weights = sb("weights", [P, P])
        c = sb("c", [P, 2, Q, P])
        sq = sb("sq", [P, 2, Q * P])
        stat6, stat = sb("stat6", [P, Q, 6]), sb("stat", [P, Q, 2])
        vareps, rstd = sb("vareps", [P, Q]), sb("rstd", [P, Q])
        xn = sb("xn", [P, Q, P])
        prod = sb("prod", [P, Q, P])
        ps_r = ctx.enter_context(nc.psum_tensor("decay_ps_r", [P, 2, Q * P], F32))
        w_in, c_in = take("decay_w_in"), [take("decay_c_in0"), take("decay_c_in1")]
        squared, r_ready, stats_a, stats_ready = take("decay_squared"), take("decay_r_ready"), take("decay_stats_a"), take("decay_stats_ready")
        var_ready, rstd_ready, xn_ready, multiplied, added = (take(f"decay_{k}") for k in ("var_ready", "rstd_ready", "xn_ready", "multiplied", "added"))
        block = ctx.enter_context(nc.Block())
        N = NSEQ // Q

        @block.sync
        def _(sync):
            sync.dma_start(weights[:, :], weights_dram).then_inc(w_in, 16)
            for g in range(N):
                wait(sync, squared, g - 1)
                sync.dma_start(c[:, g % 2, :, :], ctx_dram[Q * g:Q * (g + 1)].rearrange("s t d -> t s d")).then_inc(c_in[g % 2], 16)

        @block.scalar
        def _(act):
            for g in range(N):
                act.wait_ge(c_in[g % 2], 16 * (g // 2 + 1))
                wait(act, r_ready, g - 1)
                nc.scalar.activation(sq[:, g % 2, :], c[:, g % 2, :, :].rearrange("t s d -> t (s d)"), ACT.Square).then_inc(squared, 1)

        @block.tensor
        def _(pe):
            pe.wait_ge(w_in, 16)
            for g in range(N):
                wait(pe, squared, g + 1)
                wait(pe, multiplied, g - 1)
                pe.matmul(ps_r[:, g % 2, :], weights[:, :], sq[:, g % 2, :], start=True, stop=True).then_inc(r_ready, 1)

        @block.gpsimd
        def _(pool):
            for g in range(N):
                pool.wait_ge(stats_ready, g + 1)
                nc.gpsimd.tensor_scalar(vareps[:, :], stat[:, :, 1], EPS, None, ALU.add).then_inc(var_ready, 1)
                pool.wait_ge(var_ready, g + 1)
                nc.gpsimd.tensor_tensor(rstd[:, :], vareps[:, :], const["minus_half"][:, 0:Q], ALU.pow).then_inc(rstd_ready, 1)

        @block.vector
        def _(dve):
            for g in range(N):
                for j in range(Q):
                    dve.bn_stats(stat6[:, j, :], X[:, Q * g + j, :]).then_inc(stats_a, 1)
                wait(dve, xn_ready, Q * g)
                for j in range(Q):
                    dve.wait_ge(stats_a, Q * g + j + 1)
                    op = dve.bn_aggr(stat[:, j, :], stat6[:, j, :])
                op.then_inc(stats_ready, 1)
                dve.wait_ge(rstd_ready, g + 1)
                wait(dve, multiplied, g)
                for j in range(Q):
                    dve.tensor_scalar(xn[:, j, :], X[:, Q * g + j, :], stat[:, j, 0:1], rstd[:, j:j + 1],
                                      ALU.subtract, ALU.mult).then_inc(xn_ready, 1)
                dve.wait_ge(xn_ready, Q * (g + 1))
                dve.wait_ge(r_ready, g + 1)
                wait(dve, added, g)
                dve.tensor_tensor(prod[:, :, :], xn[:, :, :], ps_r[:, g % 2, :].rearrange("t (s d) -> t s d", s=Q), ALU.mult).then_inc(multiplied, 1)
                dve.wait_ge(multiplied, g + 1)
                dve.tensor_tensor(X[:, Q * g:Q * (g + 1), :], X[:, Q * g:Q * (g + 1), :], prod[:, :, :], ALU.add).then_inc(added, 1)


def ffn_stage(nc, name, X, w, const, top2):
    Q = 4
    N = NSEQ // Q
    with semaphores(nc) as take, ExitStack() as ctx:
        def sb(n, shape, dt=F32):
            return ctx.enter_context(nc.sbuf_tensor(f"{name}_{n}", shape, dt))

        def psum(n, shape):
            return ctx.enter_context(nc.psum_tensor(f"{name}_{n}", shape, F32))

        def sem(n):
            return take(f"{name}_{n}")

        w1, w2 = sb("w1", [P, NE, FF]), sb("w2", [P, NE, FC, P])
        b1, b2 = sb("b1", [P, NE, FC]), sb("b2", [NE, P])
        wg, bg = sb("wg", [P, NE]), sb("bg", [P, NE])
        tri, low = sb("tri", [P, P]), sb("low", [P, NE, NE])
        tri16, ones16 = sb("tri16", [P, P], BF16), sb("ones16", [P, P], BF16)
        xnT = sb("xnT", [P, NSEQ * P])
        xn = sb("xn", [P, Q, P])
        stat6, stat = sb("stat6", [P, Q, 6]), sb("stat", [P, Q, 2])
        vareps, rstd = sb("vareps", [P, Q]), sb("rstd", [P, Q])
        lg = sb("lg", [P, NSEQ, NE])
        hit, hit2 = sb("hit", [P, NSEQ, NE, NE]), sb("hit2", [P, NSEQ, NE, NE])
        rank = sb("rank", [P, NSEQ, NE])
        best, second = sb("best", [P, NSEQ, NE]), sb("second", [P, NSEQ, NE])
        top, nxt, ex, den = sb("top", [P, NSEQ]), sb("nxt", [P, NSEQ]), sb("ex", [P, NSEQ, NE]), sb("den", [P, NSEQ])
        best16 = sb("best16", [P, NSEQ, NE], BF16)
        tot = sb("tot", [P, 2, NSEQ, NE])
        gate = sb("gate", [P, NSEQ, NE])
        gateT = sb("gateT", [NE, NSEQ, P])
        hid = sb("hid", [P, 2, FC, BT])
        ps_x, ps_g = psum("ps_x", [P, Q * P]), psum("ps_g", [P, Q * NE])
        ps_c = psum("ps_c", [P, NSEQ * NE])
        ps_n = psum("ps_n", [P, NSEQ * NE])
        ps_h, ps_y = psum("ps_h", [P, 2, BT]), psum("ps_y", [P, 2, P * 4])

        w_in, e_in = sem("w_in"), sem("e_in")
        stats_a, stats_ready, var_ready, rstd_ready, xn_ready = (sem(k) for k in ("stats_a", "stats_ready", "var_ready", "rstd_ready", "xn_ready"))
        xtr_done, xT_ready, lg_done, lg_ready = (sem(k) for k in ("xtr_done", "xT_ready", "lg_done", "lg_ready"))
        step, ex_ready, counted, gate_ready = (sem(k) for k in ("step", "ex_ready", "counted", "gate_ready"))
        gtr_done, gT_ready, b2_done, b2_added = (sem(k) for k in ("gtr_done", "gT_ready", "b2_done", "b2_added"))
        h_done, h_ready, y_done, y_added = (sem(k) for k in ("h_done", "h_ready", "y_done", "y_added"))
        passed_dve = sem("passed_dve")
        block = ctx.enter_context(nc.Block())
        NPAIR = NE * TB

        @block.sync
        def _(sync):
            for tile, key in ((wg, "wg"), (tri, "tri"), (b1, "b1"), (b2, "b2")):
                sync.dma_start(tile[:, :] if len(tile.shape) == 2 else tile[:, :, :], w[key]).then_inc(w_in, 16)
            sync.dma_start(bg[:, :], w["bg"].partition_broadcast(P)).then_inc(w_in, 16)
            sync.dma_start(low[:, :, :].rearrange("p a b -> p (a b)"), w["low"].partition_broadcast(P)).then_inc(w_in, 16)
            sync.dma_start(w1[:, :, :], w["w1"].rearrange("e d f -> d e f")).then_inc(e_in, 16)
            for e in range(NE):
                sync.dma_start(w2[:, e, :, :], w["w2"][e].rearrange("(c f) d -> f c d", f=P)).then_inc(e_in, 16)

        @block.gpsimd
        def _(pool):
            for g in range(N):
                pool.wait_ge(stats_ready, g + 1)
                nc.gpsimd.tensor_scalar(vareps[:, :], stat[:, :, 1], EPS, None, ALU.add).then_inc(var_ready, 1)
                pool.wait_ge(var_ready, g + 1)
                nc.gpsimd.tensor_tensor(rstd[:, :], vareps[:, :], const["minus_half"][:, 0:Q], ALU.pow).then_inc(rstd_ready, 1)

        @block.tensor
        def _(pe):
            pe.wait_ge(w_in, 96)
            for g in range(N):
                pe.wait_ge(xn_ready, Q * (g + 1))
                wait(pe, xT_ready, g)
                for j in range(Q):
                    op = pe.transpose(ps_x[:, j * P:(j + 1) * P], xn[:, j, :], const["ident"][:, :])
                op.then_inc(xtr_done, 1)
                pe.wait_ge(xT_ready, g + 1)
                wait(pe, lg_ready, g)
                for j in range(Q):
                    at = (Q * g + j) * P
                    op = pe.matmul(ps_g[:, j * NE:(j + 1) * NE], xnT[:, at:at + P], wg[:, :], start=True, stop=True)
                op.then_inc(lg_done, 1)
            if not top2:
                pe.wait_ge(step, 100)
                pe.matmul(ps_c[:, :], tri16[:, :], best16[:, :, :].rearrange("t s e -> t (s e)"), start=True, stop=True)
                pe.matmul(ps_n[:, :], ones16[:, :], best16[:, :, :].rearrange("t s e -> t (s e)"), start=True, stop=True).then_inc(counted, 1)
            pe.wait_ge(gate_ready, 1)
            for g in range(N):
                wait(pe, gT_ready, g)
                for j in range(Q):
                    op = pe.transpose(ps_x[0:NE, j * P:(j + 1) * P], gate[:, Q * g + j, :], const["ident"][:, :])
                op.then_inc(gtr_done, 1)
                pe.wait_ge(gT_ready, g + 1)
                wait(pe, b2_added, g - 1)
                for j in range(Q):
                    op = pe.matmul(ps_y[:, g % 2, j * P:(j + 1) * P], gateT[:, Q * g + j, :], b2[:, :], start=True, stop=True)
                op.then_inc(b2_done, 1)
            pe.wait_ge(b2_added, N)
            pe.wait_ge(e_in, 16 * (1 + NE))

            def hidden(t, e, b):
                for c in range(FC):
                    wait(pe, h_ready, t * FC + c - 1)
                    pe.matmul(ps_h[:, c % 2, :], w1[:, e, c * P:(c + 1) * P], xnT[:, b * BT:(b + 1) * BT],
                              start=True, stop=True).then_inc(h_done, 1)

            def output(t, e):
                wait(pe, h_ready, (t + 1) * FC)
                wait(pe, y_added, (t - 1) * Q)
                for j in range(Q):
                    for c in range(FC):
                        op = pe.matmul(ps_y[:, t % 2, j * P:(j + 1) * P], hid[:, t % 2, c, j * P:(j + 1) * P], w2[:, e, c, :],
                                       start=c == 0, stop=c == FC - 1)
                op.then_inc(y_done, 1)

            for t in range(NPAIR):
                hidden(t, t // TB, t % TB)
                if t:
                    output(t - 1, (t - 1) // TB)
            output(NPAIR - 1, NE - 1)

        @block.scalar
        def _(act):
            for g in range(N):
                act.wait_ge(xtr_done, g + 1)
                nc.scalar.activation(xnT[:, g * Q * P:(g + 1) * Q * P], ps_x[:, :], ACT.Identity).then_inc(xT_ready, 1)
            act.wait_ge(step, 101)
            nc.scalar.activation(ex[:, :, :], ex[:, :, :], ACT.Exp).then_inc(ex_ready, 1)
            for g in range(N):
                act.wait_ge(gtr_done, g + 1)
                nc.scalar.activation(gateT[:, Q * g:Q * (g + 1), :].rearrange("e s t -> e (s t)"), ps_x[0:NE, :], ACT.Identity).then_inc(gT_ready, 1)
            act.wait_ge(w_in, 96)
            for t in range(NPAIR):
                for c in range(FC):
                    act.wait_ge(h_done, t * FC + c + 1)
                    wait(act, y_done, t - 1)
                    nc.scalar.activation(hid[:, t % 2, c, :], ps_h[:, c % 2, :], ACT.Gelu if top2 else ACT.Relu,
                                         bias=b1[:, t // TB, c:c + 1]).then_inc(h_ready, 1)

        @block.vector
        def _(dve):
            for g in range(N):
                for j in range(Q):
                    dve.bn_stats(stat6[:, j, :], X[:, Q * g + j, :]).then_inc(stats_a, 1)
                wait(dve, xn_ready, Q * g)
                for j in range(Q):
                    dve.wait_ge(stats_a, Q * g + j + 1)
                    op = dve.bn_aggr(stat[:, j, :], stat6[:, j, :])
                op.then_inc(stats_ready, 1)
                dve.wait_ge(rstd_ready, g + 1)
                wait(dve, xtr_done, g)
                for j in range(Q):
                    dve.tensor_scalar(xn[:, j, :], X[:, Q * g + j, :], stat[:, j, 0:1], rstd[:, j:j + 1],
                                      ALU.subtract, ALU.mult).then_inc(xn_ready, 1)
                dve.wait_ge(w_in, 96)
                dve.wait_ge(lg_done, g + 1)
                dve.tensor_tensor(lg[:, Q * g:Q * (g + 1), :], ps_g[:, :].rearrange("t (s e) -> t s e", e=NE),
                                  bg[:, :].unsqueeze(1).to_broadcast([P, Q, NE]), ALU.add).then_inc(lg_ready, 1)
            dve.wait_ge(lg_ready, N)
            n = 0

            def then(op, by=1):
                nonlocal n
                n += by
                op.then_inc(step, by)
                dve.wait_ge(step, n)

            S4 = [P, NSEQ, NE, NE]
            mine = lg[:, :, :].unsqueeze(3).to_broadcast(S4)
            other = lg[:, :, :].unsqueeze(2).to_broadcast(S4)
            then(dve.tensor_tensor(hit[:, :, :, :], other, mine, ALU.is_gt))
            then(dve.tensor_tensor(hit2[:, :, :, :], other, mine, ALU.is_equal))
            then(dve.tensor_tensor(hit2[:, :, :, :], hit2[:, :, :, :], low[:, :, :].unsqueeze(1).to_broadcast(S4), ALU.mult))
            then(dve.tensor_tensor(hit[:, :, :, :], hit[:, :, :, :], hit2[:, :, :, :], ALU.add))
            then(dve.tensor_reduce(rank[:, :, :], hit[:, :, :, :], AX.X, ALU.add))
            then(dve.tensor_scalar(best[:, :, :], rank[:, :, :], 0.0, None, ALU.is_equal))
            then(dve.tensor_reduce(top[:, :], lg[:, :, :], AX.X, ALU.max))
            S3 = [P, NSEQ, NE]
            if not top2:
                then(dve.tensor_copy(tri16[:, :], tri[:, :]))
                then(dve.memset(ones16[:, :], 1.0))
                then(dve.tensor_copy(best16[:, :, :], best[:, :, :]))
            else:
                then(dve.tensor_scalar(second[:, :, :], rank[:, :, :], 1.0, None, ALU.is_equal))
            then(dve.tensor_tensor(ex[:, :, :], lg[:, :, :], top[:, :].unsqueeze(2).to_broadcast(S3), ALU.subtract), by=101 - n)
            dve.wait_ge(ex_ready, 1)
            if not top2:
                then(dve.tensor_reduce(den[:, :], ex[:, :, :], AX.X, ALU.add))
                then(dve.reciprocal(den[:, :], den[:, :]))
                dve.wait_ge(counted, 1)
                n_seq = ps_n[:, :].rearrange("t (s e) -> t s e", e=NE)
                then(dve.tensor_copy(tot[:, 0, :, :], n_seq))
                a = 0
                for d in (1, 2, 4, 8, 16):
                    then(dve.tensor_copy(tot[:, 1 - a, 0:d, :], tot[:, a, 0:d, :]))
                    then(dve.tensor_tensor(tot[:, 1 - a, d:, :], tot[:, a, d:, :], tot[:, a, :NSEQ - d, :], ALU.add))
                    a = 1 - a
                then(dve.tensor_tensor(tot[:, a, :, :], tot[:, a, :, :], n_seq, ALU.subtract))
                then(dve.tensor_tensor(tot[:, a, :, :], tot[:, a, :, :], ps_c[:, :].rearrange("t (s e) -> t s e", e=NE), ALU.add))
                then(dve.tensor_scalar(tot[:, a, :, :], tot[:, a, :, :], float(CAP), None, ALU.is_le))
                then(dve.tensor_tensor(best[:, :, :], best[:, :, :], tot[:, a, :, :], ALU.mult))
                then(dve.tensor_tensor(gate[:, :, :], best[:, :, :], den[:, :].unsqueeze(2).to_broadcast(S3), ALU.mult))
            else:
                then(dve.tensor_tensor(best[:, :, :], best[:, :, :], second[:, :, :], ALU.add))
                then(dve.tensor_tensor(ex[:, :, :], ex[:, :, :], best[:, :, :], ALU.mult))
                then(dve.tensor_reduce(den[:, :], ex[:, :, :], AX.X, ALU.add))
                then(dve.reciprocal(den[:, :], den[:, :]))
                then(dve.tensor_tensor(gate[:, :, :], ex[:, :, :], den[:, :].unsqueeze(2).to_broadcast(S3), ALU.mult))
            dve.sem_inc(gate_ready, 1)
            for g in range(N):
                dve.wait_ge(b2_done, g + 1)
                dve.tensor_tensor(X[:, Q * g:Q * (g + 1), :], X[:, Q * g:Q * (g + 1), :],
                                  ps_y[:, g % 2, :].rearrange("t (s d) -> t s d", s=Q), ALU.add).then_inc(b2_added, 1)
            dve.wait_ge(b2_added, N)
            for t in range(NPAIR):
                e, b = t // TB, t % TB
                dve.wait_ge(y_done, t + 1)
                wait(dve, y_added, (t - TB + 1) * Q)
                for j in range(Q):
                    q = b * Q + j
                    dve.scalar_tensor_tensor(out=X[:, q, :], in0=ps_y[:, t % 2, j * P:(j + 1) * P], scalar=gate[:, q, e:e + 1],
                                             in1=X[:, q, :], op0=ALU.mult, op1=ALU.add).then_inc(y_added, 1)


def store_stage(nc, X, out):
    with semaphores(nc) as take, ExitStack() as ctx:
        stored = take("stored")
        block = ctx.enter_context(nc.Block())

        @block.sync
        def _(sync):
            sync.dma_start(out.rearrange("s t d -> t s d"), X[:, :, :]).then_inc(stored, 16)
            sync.wait_ge(stored, 16)


FFN_KEYS = ("wg", "bg", "w1", "b1", "w2", "b2")


def decoder(nc, a, out, stages=99):
    with ExitStack() as ctx:
        def sb(n, shape, dt=F32):
            return ctx.enter_context(nc.sbuf_tensor(n, shape, dt))

        X = sb("X", [P, NSEQ, P])
        const = {"ident": sb("ident", [P, P]), "ident16": sb("ident16", [P, P], BF16), "minus_half": sb("minus_half", [P, 8])}
        with ExitStack() as layer0:
            def sb0(n, shape, dt=F32):
                return layer0.enter_context(nc.sbuf_tensor(n, shape, dt))

            hT = sb0("hT", [P, NSEQ * P])
            const["dist"] = sb0("dist", [P, P], BF16)
            const["slope"] = sb0("slope", [P, 3, H, P], BF16)
            const["mask_qk"] = sb0("mask_qk", [P, HB, P], BF16)
            const["mask_kq"] = sb0("mask_kq", [P, HB, P], BF16)
            setup_stage(nc, const, {"ident": a["c_ident"], "dist": a["c_dist"], "mask": a["c_mask"], "mask_t": a["c_mask_t"]},
                        a["L0_attn_decay_alpha"])
            names = ("wq", "wk", "wv", "wo", "bq", "bk", "bv", "bo")

            def weights(stage):
                return {k: a.get(f"{stage}_{k}") for k in names}

            attention_stage(nc, "alibi", X, weights("A0"), HD ** -0.5, "alibi", False, None, False, hT, const, x_dram=a["x"])
            if stages > 1:
                attention_stage(nc, "causal", X, weights("A1"), HD ** -0.5, "causal", False, None, True, hT, const)
                attention_stage(nc, "cross", X, weights("A2"), HD ** -0.5, None, True, a["ctx"], False, hT, const)
        if stages > 2:
            ffn_stage(nc, "ffn0", X, {k: a[f"F0_{k}"] for k in FFN_KEYS} | {"tri": a["c_tri"], "low": a["c_low"]}, const, False)
        if stages > 3:
            attention_stage(nc, "block", X, weights("A3"), P ** -0.5, None, False, None, False, None, const)
        if stages > 4:
            decay_stage(nc, X, a["ctx"], const, a["c_decay"])
        if stages > 5:
            ffn_stage(nc, "ffn1", X, {k: a[f"F1_{k}"] for k in FFN_KEYS} | {"tri": a["c_tri"], "low": a["c_low"]}, const, True)
        store_stage(nc, X, out)


def lay_out(inputs):
    v = {k: np.asarray(x) for k, x in inputs.items()}
    a = {"x": v["x"], "ctx": v["ctx_1024"], "L0_attn_decay_alpha": v["L0_attn_decay_alpha"]}

    def by_dim(wt):
        return wt.reshape(-1, H, HD).swapaxes(1, 2).reshape(-1, P)

    wT = v["L0_attn_qkv_w"].T
    b = v["L0_attn_qkv_b"]
    a["A0_wq"], a["A0_wk"], a["A0_wv"] = by_dim(wT[:, 0:P]), by_dim(wT[:, P:2 * P]), wT[:, 2 * P:]
    a["A0_bq"], a["A0_bk"], a["A0_bv"] = by_dim(b[0:P]).reshape(P, 1), by_dim(b[P:2 * P]).reshape(P, 1), b[2 * P:]
    a["A0_wo"], a["A0_bo"] = v["L0_attn_out_w"].T, v["L0_attn_out_b"]
    for n in (1, 2):
        for k in "qk":
            a[f"A{n}_w{k}"] = v[f"L0_xattn_W{k}{n}"].transpose(1, 2, 0).reshape(P, P)
            a[f"A{n}_b{k}"] = v[f"L0_xattn_b{k}{n}"].T.reshape(P, 1)
        a[f"A{n}_wv"] = v[f"L0_xattn_Wv{n}"].transpose(1, 0, 2).reshape(P, P)
        a[f"A{n}_bv"] = v[f"L0_xattn_bv{n}"].reshape(P)
        a[f"A{n}_wo"], a[f"A{n}_bo"] = v[f"L0_xattn_Wo{n}"], v[f"L0_xattn_bo{n}"]
    for k in "qkv":
        w = np.zeros((H, HD, HD, H) if k != "v" else (H, HD, H, HD), np.float32)
        for h in range(H):
            if k != "v":
                w[h, :, :, h] = v[f"L1_attn_W{k}"].T
            else:
                w[h, :, h, :] = v["L1_attn_Wv"].T
        a[f"A3_w{k}"] = w.reshape(P, P)
    a["A3_wo"], a["A3_bo"] = v["L1_attn_W_out"].T, v["L1_attn_b_out"]
    for n, l, up in ((0, "L0_ffn_w1", "L0_ffn"), (1, "L1_ffn_W1", "L1_ffn")):
        a[f"F{n}_w1"], a[f"F{n}_w2"] = v[l], v[l[:-1] + "2"]
        a[f"F{n}_b1"] = v[f"{up}_b1"].reshape(NE, FC, P).transpose(2, 0, 1)
        a[f"F{n}_b2"] = v[f"{up}_b2"]
    a["F0_wg"], a["F0_bg"] = v["L0_ffn_gate_w"].T, v["L0_ffn_gate_b"]
    a["F1_wg"], a["F1_bg"] = v["L1_ffn_Wg"], v["L1_ffn_bg"]
    n = np.arange(P)
    a["c_tri"] = (n[:, None] <= n[None, :]).astype(np.float32)
    a["c_low"] = (n[None, :NE] < n[:NE, None]).astype(np.float32).reshape(NE * NE)
    ahead = n[None, :] - n[:, None]
    a["c_decay"] = np.where(ahead >= 0, DECAY ** np.maximum(ahead, 0).astype(np.float64), 0.0).astype(np.float32)
    a["c_ident"] = np.eye(P, dtype=np.float32)
    a["c_dist"] = np.abs(n[:, None] - n[None, :]).astype(np.float32)
    a["c_mask"] = np.where(n[None, :] > n[:, None], np.float32(-1e30), np.float32(0))
    a["c_mask_t"] = np.ascontiguousarray(a["c_mask"].T)
    return {k: np.ascontiguousarray(x) for k, x in a.items()}


def kernel(**inputs):
    import concourse.bacc as _bacc
    from concourse.bass_utils import run_bass_kernel_spmd as _run

    nc = _bacc.Bacc("TRN2", target_bir_lowering=False, num_devices=1)
    arrays, args = {}, {}
    for name, a in lay_out(inputs).items():
        arrays[f"in_{name}"] = a
        args[name] = nc.dram_tensor(f"in_{name}", a.shape, mybir.dt.from_np(a.dtype), kind="ExternalInput").ap()
    out = nc.dram_tensor("out", (NSEQ, P, P), F32, kind="ExternalOutput").ap()
    decoder(nc, args, out)
    r = _run(nc, [arrays], core_ids=[0])
    return r.results[0]["out"]
```

```python
from contextlib import ExitStack, contextmanager

import numpy as np
import concourse.bass as bass
from concourse import mybir

ALU = mybir.AluOpType
ACT = mybir.ActivationFunctionType
AX = mybir.AxisListType
F32 = mybir.dt.float32
BF16 = mybir.dt.bfloat16
U32 = mybir.dt.uint32
I32 = mybir.dt.int32

P = 128
NSEQ = 32
H = 16
HD = 8
GS = 2
NG = NSEQ // GS
GT = GS * P
RING = 4
HB = 4
NB = H // HB
EPS = 1e-5
DECAY = 0.9
NE = 8
FF = 512
FC = FF // P
CAP = 640
ST = 2
SLOTS = ST * P
RB = 4
ROW = P + 2
STEPS = NSEQ * P // SLOTS


def blocks_for(k):
    return -(-(k * NSEQ * P // SLOTS + NE - 1) // RB) * RB


TABLE = NE + STEPS + NE * NE + blocks_for(2) + 2

Q_PART = (0, 0, 0, 1, 1, 2)
K_PART = (0, 1, 2, 0, 1, 0)
PAIRS = len(Q_PART)
ROWS_QK = PAIRS * HD
ROWS_MAX = P - 2


def wait(eng, sem, count, most=None, unit=1):
    if isinstance(count, int):
        if most is not None:
            count = min(count, most)
        if count <= 0:
            return
    eng.wait_ge(sem, count * unit)


def settle(eng, passed):
    eng.sem_inc(passed, 1)


@contextmanager
def semaphores(nc):
    taken = []

    def take(name):
        taken.append(nc.alloc_semaphore(name))
        return taken[-1]

    yield take
    nc.clear_and_free_semaphores(taken)
    nc.all_engine_barrier()


def attention_stage(nc, name, X, w, scale, extra, q_from_h, kv_dram, h_out, hT, const, x_dram=None):
    with semaphores(nc) as take, ExitStack() as ctx:
        def sb(n, shape, dt=F32):
            return ctx.enter_context(nc.sbuf_tensor(f"{name}_{n}", shape, dt))

        def psum(n, shape):
            return ctx.enter_context(nc.psum_tensor(f"{name}_{n}", shape, F32))

        def sem(n):
            return take(f"{name}_{n}")

        own_kv = kv_dram is None
        qst, kst, v1 = const["qst"], const["kst"], const["v1"]
        ps_s = psum("ps_s", [P, 2, 512])
        ps_t = psum("ps_t", [P, 2, 512])
        ps_o = psum("ps_o", [P, NB, P])
        ps_x = psum("ps_x", [P, 512])
        ps_q = psum("ps_q", [P, 512])
        ps_e = psum("ps_e", [P, 512])

        wq, wk, wv, wo = (w[k] for k in ("wq", "wk", "wv", "wo"))
        bq, bk, bv, bo, bo_col = (w.get(k) for k in ("bq", "bk", "bv", "bo", "bo_col"))
        bqs = sb("bqs", [P, 1])
        xn = sb("xn", [P, 2, GS, P])
        stat6 = sb("stat6", [P, GS, 6])
        stat = sb("stat", [P, GS, 2])
        vareps = sb("vareps", [P, GS])
        rstd = sb("rstd", [P, GS])
        xnT = sb("xnT", [P, GT])
        qf, kf = sb("qf", [P, GT]), sb("kf", [P, GT])
        rest = sb("rest", [P, GT])
        qp, kp = sb("qp", [P, 2, 3, GT], BF16), sb("kp", [P, 2, 3, GT], BF16)
        mx = sb("mx", [P, 2, H])
        mp = sb("mp", [P, 2, 2, H], BF16)
        mpT = sb("mpT", [2 * H, 2, P], BF16)
        pt = sb("pt", [P, NB, HB * P])
        osb = sb("osb", [P, GS, NB * P])
        rden = sb("rden", [P, H])
        on = sb("on", [P, GS, P])
        oT = sb("oT", [P, GT])

        passed_pool, passed_dve, passed_sync = sem("passed_pool"), sem("passed_dve"), sem("passed_sync")
        bias_ready = sem("bias_ready")
        in_dma = [sem(f"in_dma{k}") for k in range(6 if x_dram is not None else 2)]
        stats_a, stats_ready, var_ready, rstd_ready = sem("stats_a"), sem("stats_ready"), sem("var_ready"), sem("rstd_ready")
        xn_ready, xtr_done, xT_ready = sem("xn_ready"), sem("xtr_done"), sem("xT_ready")
        q_done, k_done, v_done = sem("q_done"), sem("k_done"), sem("v_done")
        qf_ready, kf_ready, v_ready = sem("qf_ready"), sem("kf_ready"), sem("v_ready")
        part, q_split, k_split = sem("part"), sem("q_split"), sem("k_split")
        stack_dma = [sem(f"stack_dma{k}") for k in range(RING)]
        s_ready, s_max = sem("s_ready"), sem("s_max")
        mtr_done, m_hi, m_parts, m_split = sem("mtr_done"), sem("m_hi"), sem("m_parts"), sem("m_split")
        m_dma = [sem(f"m_dma{k}") for k in range(2)]
        t_ready, p_ready, pv_done = sem("t_ready"), sem("p_ready"), sem("pv_done")
        o_copied, otr_done, den_ready, o_normed = sem("o_copied"), sem("otr_done"), sem("den_ready"), sem("o_normed")
        ontr_done, oT_ready, oproj_done, biased, x_done = sem("ontr_done"), sem("oT_ready"), sem("oproj_done"), sem("biased"), sem("x_done")

        def schedule(eng, body, engines_loop):
            for i in range(-4, 1):
                body(eng, i, i % RING, i // RING)
            with engines_loop(0, 3) as lap:
                for t in range(1, 1 + RING):
                    body(eng, lap * RING + t, t % RING, lap + t // RING)
            for i in range(1 + 3 * RING, NG + 1):
                body(eng, i, i % RING, i // RING)

        def wrap(g):
            return g if isinstance(g, int) else g % NG

        def seq_on(n):
            return not isinstance(n, int) or 0 <= n < NSEQ

        def group_on(g):
            return not isinstance(g, int) or 0 <= g < NG

        block = ctx.enter_context(nc.Block())

        @block.sync
        def _(sync):
            if x_dram is not None:
                for g in range(NG):
                    sync.dma_start(X[:, GS * g:GS * (g + 1), :],
                                   x_dram[GS * g:GS * (g + 1)].rearrange("s t d -> t s d")).then_inc(in_dma[min(g, 5)], 16)

            def body(sync, i, r, lap):
                p1, p2 = i + 4, i + 3
                if not own_kv and group_on(p1):
                    wait(sync, xtr_done, p1 - 1)
                    settle(sync, passed_sync)
                    sync.dma_start(xn[:, r % 2, :, :], kv_dram[bass.ds(wrap(p1) * GS, GS)].rearrange("s t d -> t s d")).then_inc(in_dma[r % 2], 16)
                if seq_on(2 * i + 2):
                    max_rows(sync, 2 * i + 2, 0, (r + 1) % RING)
                if group_on(p2):
                    slot = (r + 3) % RING
                    wait(sync, t_ready, (p2 - RING + 1) * GS * NB)
                    settle(sync, passed_sync)
                    wait(sync, q_split, p2 + 1)
                    for k in range(PAIRS):
                        sync.dma_start(qst[HD * k:HD * (k + 1), slot, :, :], qp[:, (r + 3) % 2, Q_PART[k], :]).then_inc(stack_dma[slot], 16)
                if seq_on(2 * i + 3):
                    max_rows(sync, 2 * i + 3, 1, (r + 1) % RING)
                if group_on(p2):
                    wait(sync, k_split, p2 + 1)
                    for k in range(PAIRS):
                        sync.dma_start(kst[HD * k:HD * (k + 1), slot, :, :], kp[:, (r + 3) % 2, K_PART[k], :]).then_inc(stack_dma[slot], 16)

            def max_rows(sync, m, s, slot):
                wait(sync, m_split, m + 1)
                settle(sync, passed_sync)
                sync.dma_start(qst[ROWS_MAX:P, slot, :, s * P:(s + 1) * P], mpT[:, s, :]).then_inc(m_dma[s], 16)

            schedule(sync, body, sync.Fori)

        @block.gpsimd
        def _(pool):
            def split(pool, src, dst, ready, done, g, n0):
                wait(pool, ready, g + 1)
                nc.gpsimd.tensor_tensor(rest[:, :], src[:, :], dst[:, 0, :], ALU.subtract).then_inc(part, 1)
                nc.gpsimd.tensor_tensor(dst[:, 1, :], src[:, :], dst[:, 0, :], ALU.subtract).then_inc(part, 1)
                wait(pool, part, n0 + 2)
                nc.gpsimd.tensor_tensor(dst[:, 2, :], rest[:, :], dst[:, 1, :], ALU.subtract).then_inc(done, 1)

            def body(pool, i, r, lap):
                p1, p2 = i + 4, i + 3
                if own_kv and group_on(p1):
                    wait(pool, stats_ready, p1 + 1)
                    settle(pool, passed_pool)
                    nc.gpsimd.tensor_scalar(vareps[:, :], stat[:, :, 1], EPS, None, ALU.add).then_inc(var_ready, 1)
                    wait(pool, var_ready, p1 + 1)
                    nc.gpsimd.tensor_tensor(rstd[:, :], vareps[:, :], const["minus_half"][:, 0:GS], ALU.pow).then_inc(rstd_ready, 1)
                if group_on(p2):
                    wait(pool, k_split, p2)
                    split(pool, qf, qp[:, (r + 3) % 2], qf_ready, q_split, p2, 4 * p2)
                    wait(pool, q_split, p2 + 1)
                    split(pool, kf, kp[:, (r + 3) % 2], kf_ready, k_split, p2, 2 + 4 * p2)

            schedule(pool, body, pool.Fori)

        @block.vector
        def _(dve):
            if bq is not None:
                dve.tensor_scalar(bqs[:, :], bq[:, :], scale, None, ALU.mult).then_inc(bias_ready, 1)

            def smax(dve, m, s, c):
                wait(dve, s_ready, m * NB + c + 1)
                if c == 0:
                    wait(dve, m_parts, m - 1)
                dve.tensor_reduce(mx[:, s, HB * c:HB * (c + 1)], ps_s[:, c % 2, :].rearrange("q (h k) -> q h k", h=HB),
                                  AX.X, ALU.max).then_inc(s_max, 1)

            def msplit(dve, m, s):
                wait(dve, s_max, (m + 1) * NB)
                wait(dve, mtr_done, m - 1)
                dve.tensor_scalar(mp[:, s, 0, :], mx[:, s, :], -1.0, None, ALU.mult).then_inc(m_hi, 1)
                wait(dve, m_hi, m + 1)
                dve.scalar_tensor_tensor(out=mp[:, s, 1, :], in0=mx[:, s, :], scalar=-1.0, in1=mp[:, s, 0, :],
                                         op0=ALU.mult, op1=ALU.subtract).then_inc(m_parts, 1)

            def mcopy(dve, m, s, uses):
                wait(dve, mtr_done, m + 1)
                wait(dve, m_dma[s], uses, unit=16)
                dve.tensor_copy(mpT[:, s, :], (ps_x, ps_q)[s][0:2 * H, 0:P // 2].bitcast(BF16)).then_inc(m_split, 1)

            def normalise(dve, n, s):
                wait(dve, otr_done, n + 1)
                heads = ps_e[:, :].rearrange("q (h e) -> q h e", e=32)
                dve.reciprocal(rden[:, :], heads[:, :, HD:HD + 1].rearrange("q h e -> q (h e)")).then_inc(den_ready, 1)
                wait(dve, den_ready, n + 1)
                dve.tensor_tensor(on[:, s, :].rearrange("q (h e) -> q h e", e=HD), heads[:, :, 0:HD],
                                  rden[:, :].unsqueeze(2).to_broadcast([P, H, HD]), ALU.mult).then_inc(o_normed, 1)

            def body(dve, i, r, lap):
                p1, p2 = i + 4, i + 3
                for s in range(GS):
                    m = 2 * i + 3 + s
                    for c in range(NB):
                        if seq_on(m):
                            smax(dve, m, (1 + s) % 2, c)
                            if c == NB - 1:
                                msplit(dve, m, (1 + s) % 2)
                        at = (s, c)
                        if at == (0, 1) and seq_on(2 * i - 2):
                            normalise(dve, 2 * i - 2, 0)
                        if at == (0, 2) and seq_on(2 * i + 2):
                            mcopy(dve, 2 * i + 2, 0, i + 1)
                        if at == (0, 1) and own_kv and group_on(p1):
                            if x_dram is not None:
                                if isinstance(p1, int) and p1 < 5:
                                    dve.wait_ge(in_dma[p1], 16)
                                if isinstance(p1, int) and p1 == 4:
                                    dve.wait_ge(in_dma[5], 16 * (NG - 5))
                            wait(dve, xn_ready, GS * p1)
                            for j in range(GS):
                                dve.bn_stats(stat6[:, j, :], X[:, bass.ds(wrap(p1) * GS + j, 1), :].rearrange("t s d -> t (s d)")).then_inc(stats_a, 1)
                            for j in range(GS):
                                wait(dve, stats_a, GS * p1 + j + 1)
                                settle(dve, passed_dve)
                                op = dve.bn_aggr(stat[:, j, :], stat6[:, j, :])
                            op.then_inc(stats_ready, 1)
                        if at == (0, 3) and seq_on(2 * i - 1):
                            normalise(dve, 2 * i - 1, 1)
                        if at == (1, 0) and own_kv and group_on(p1):
                            wait(dve, rstd_ready, p1 + 1)
                            wait(dve, xtr_done, p1 - 1)
                            for j in range(GS):
                                dve.tensor_scalar(xn[:, r % 2, j, :], X[:, bass.ds(wrap(p1) * GS + j, 1), :].rearrange("t s d -> t (s d)"),
                                                  stat[:, j, 0:1], rstd[:, j:j + 1], ALU.subtract, ALU.mult).then_inc(xn_ready, 1)
                        if at == (1, 2) and seq_on(2 * i + 3):
                            mcopy(dve, 2 * i + 3, 1, i + 1)
                        if at == (1, 1) and group_on(p2):
                            wait(dve, v_done, p2 + 1)
                            wait(dve, pv_done, (p2 - RING + 1) * GS * NB)
                            out = v1[:, (r + 3) % RING, :, :, 0:HD]
                            vals = ps_x[:, 0:GT].rearrange("t (s h e) -> t s h e", s=GS, e=HD)
                            if bv is not None:
                                for j in range(GS):
                                    op = dve.tensor_tensor(out[:, j], vals[:, j], bv[:, :].rearrange("t (h e) -> t h e", e=HD), ALU.add)
                            else:
                                op = dve.tensor_copy(out, vals)
                            op.then_inc(v_ready, 1)
                        if at == (1, 2) and group_on(i - 1) and not h_out:
                            g = i - 1
                            wait(dve, oproj_done, g + 1)
                            res = ps_e[:, 0:GT].rearrange("t (s d) -> t s d", s=GS)
                            dve.tensor_tensor(res, res, bo[:, :].unsqueeze(1).to_broadcast([P, GS, P]), ALU.add).then_inc(biased, 1)
                            wait(dve, biased, g + 1)
                            xg = X[:, bass.ds(g * GS, GS), :]
                            dve.tensor_tensor(xg, xg, res, ALU.add).then_inc(x_done, 1)

            schedule(dve, body, dve.Fori)

        @block.scalar
        def _(act):
            if bq is not None:
                act.wait_ge(bias_ready, 1)

            def exp_bank(act, n, c):
                wait(act, t_ready, n * NB + c + 1)
                wait(act, pv_done, (n - 1) * NB + c + 1)
                nc.scalar.activation(pt[:, c, :], ps_t[:, c % 2, :], ACT.Exp).then_inc(p_ready, 1)

            def copy_o(act, n, s):
                wait(act, pv_done, (n + 1) * NB)
                wait(act, otr_done, n - 1)
                nc.scalar.activation(osb[:, s, :], ps_o[:, :, :].rearrange("p b q -> p (b q)"), ACT.Identity).then_inc(o_copied, 1)

            def parts_free(act, p2, r, lap):
                wait(act, stack_dma[(r + 1) % RING], lap + (r + 1) // RING + 1, unit=16 * 2 * PAIRS)

            def body(act, i, r, lap):
                p1, p2 = i + 4, i + 3
                for s in range(GS):
                    n = 2 * i + s
                    for c in range(NB):
                        if seq_on(n):
                            exp_bank(act, n, c)
                        at = (s, c)
                        if at == (0, 0) and seq_on(2 * i - 1):
                            copy_o(act, 2 * i - 1, 1)
                        if at == (0, 1) and group_on(p2):
                            wait(act, q_done, p2 + 1)
                            wait(act, q_split, p2)
                            parts_free(act, p2, r, lap)
                            for dst in (qf[:, :], qp[:, (r + 3) % 2, 0, :]):
                                op = nc.scalar.activation(dst, ps_q[:, 0:GT], ACT.Identity, scale=scale,
                                                          **({"bias": bqs[:, :]} if bq is not None else {}))
                            op.then_inc(qf_ready, 1)
                        if at == (0, 3) and group_on(p2):
                            wait(act, k_done, p2 + 1)
                            wait(act, k_split, p2)
                            for dst in (kf[:, :], kp[:, (r + 3) % 2, 0, :]):
                                op = nc.scalar.activation(dst, ps_q[:, 0:GT], ACT.Identity,
                                                          **({"bias": bk[:, :]} if bq is not None else {}))
                            op.then_inc(kf_ready, 1)
                        if at == (1, 0) and seq_on(2 * i):
                            copy_o(act, 2 * i, 0)
                        if at == (1, 1) and group_on(i - 1):
                            wait(act, ontr_done, i)
                            wait(act, oproj_done, i - 1)
                            nc.scalar.activation(oT[:, :], ps_e[:, 0:GT], ACT.Identity).then_inc(oT_ready, 1)
                        if at == (1, 2) and group_on(i - 1) and h_out:
                            wait(act, oproj_done, i)
                            nc.scalar.activation(hT[:, bass.ds((i - 1) * GT, GT)], ps_e[:, 0:GT], ACT.Identity,
                                                 bias=bo_col[:, :]).then_inc(x_done, 1)
                        if at == (1, 3) and group_on(p1):
                            wait(act, xtr_done, p1 + 1)
                            wait(act, v_done, p1)
                            nc.scalar.activation(xnT[:, :], ps_x[:, 0:GT], ACT.Identity).then_inc(xT_ready, 1)

            schedule(act, body, act.Fori)

        @block.tensor
        def _(pe):
            def scores(pe, m, s, c, slot, uses):
                wait(pe, s_max, m * NB + c - 1)
                if c == 0:
                    wait(pe, stack_dma[slot], uses, unit=16 * 2 * PAIRS)
                if extra == "alibi":
                    pe.matmul(ps_s[:, c % 2, :], const["dist"][:, :], const["slope"][:, 0, HB * c:HB * (c + 1), :],
                              start=True, stop=False, skip_group_check=True)
                if extra == "causal":
                    pe.matmul(ps_s[:, c % 2, :], const["ident16"][:, :], const["mask_qk"][:, :, :],
                              start=True, stop=False, skip_group_check=True)
                for j in range(HB):
                    h = HB * c + j
                    op = pe.matmul(ps_s[:, c % 2, j * P:(j + 1) * P], qst[0:ROWS_MAX, slot, h, s * P:(s + 1) * P],
                                   kst[0:ROWS_MAX, slot, h, s * P:(s + 1) * P], start=extra is None, stop=True, skip_group_check=extra is not None)
                op.then_inc(s_ready, 1)

            def scores_t(pe, n, s, c, slot, i):
                wait(pe, p_ready, n * NB + c - 1)
                if c == 0:
                    wait(pe, m_dma[s], i + 1, unit=16)
                if extra == "alibi":
                    for k in range(3):
                        pe.matmul(ps_t[:, c % 2, :], const["dist"][:, :], const["slope"][:, k, HB * c:HB * (c + 1), :],
                                  start=k == 0, stop=False, skip_group_check=True)
                if extra == "causal":
                    pe.matmul(ps_t[:, c % 2, :], const["ident16"][:, :], const["mask_kq"][:, :, :],
                              start=True, stop=False, skip_group_check=True)
                for j in range(HB):
                    h = HB * c + j
                    op = pe.matmul(ps_t[:, c % 2, j * P:(j + 1) * P], kst[:, slot, h, s * P:(s + 1) * P],
                                   qst[:, slot, h, s * P:(s + 1) * P], start=extra is None, stop=True, skip_group_check=extra is not None)
                op.then_inc(t_ready, 1)

            def weigh(pe, n, s, c, slot, g):
                wait(pe, p_ready, n * NB + c + 1)
                if c == 0:
                    wait(pe, o_copied, n)
                    wait(pe, v_ready, g + 1)
                for j in range(HB):
                    op = pe.matmul(ps_o[32 * j:32 * (j + 1), c, :], v1[:, slot, s, HB * c + j, :],
                                   pt[:, c, j * P:(j + 1) * P], start=True, stop=True, tile_position=(0, 32 * j))
                op.then_inc(pv_done, 1)

            def body(pe, i, r, lap):
                p1, p2 = i + 4, i + 3
                for s in range(GS):
                    m, n = 2 * i + 3 + s, 2 * i + s
                    m_slot = (r + 1 + s) % RING
                    for c in range(NB):
                        at = (s, c)
                        if seq_on(m):
                            scores(pe, m, (1 + s) % 2, c, m_slot, lap + (r + 1 + s) // RING + 1)
                        if seq_on(n):
                            scores_t(pe, n, s, c, r, i)
                        if c > 0 and seq_on(n):
                            weigh(pe, n, s, c - 1, r, i)
                        if c == 0 and seq_on(n - 1):
                            weigh(pe, n - 1, 1 - s, NB - 1, (r - 1 + s) % RING, i - 1 + s)
                        if at == (0, 0) and group_on(p2):
                            wait(pe, xT_ready, p2 + 1)
                            wait(pe, m_split, 2 * i + 2, NSEQ)
                            wait(pe, kf_ready, p2)
                            src = hT[:, bass.ds(p2 * GT, GT)] if q_from_h else xnT[:, :]
                            pe.matmul(ps_q[:, 0:GT], wq[:, :], src, start=True, stop=True).then_inc(q_done, 1)
                        if at == (0, 0) and seq_on(2 * i - 2):
                            wait(pe, x_done, i - 1)
                            transpose_out(pe, 2 * i - 2, 0)
                        if at == (0, 1) and seq_on(2 * i + 2):
                            transpose_max(pe, 2 * i + 2, 0, i)
                        if at == (0, 2) and group_on(p2):
                            wait(pe, qf_ready, p2 + 1)
                            pe.matmul(ps_q[:, 0:GT], wk[:, :], xnT[:, :], start=True, stop=True).then_inc(k_done, 1)
                        if at == (0, 2) and seq_on(2 * i - 1):
                            transpose_out(pe, 2 * i - 1, 1)
                        if at == (0, 3) and group_on(p2):
                            wait(pe, m_split, 2 * i + 3, NSEQ)
                            for j in range(GS):
                                op = pe.matmul(ps_x[:, j * P:(j + 1) * P], xnT[:, j * P:(j + 1) * P], wv[:, :], start=True, stop=True)
                            op.then_inc(v_done, 1)
                        if at == (1, 0) and group_on(i - 1):
                            wait(pe, o_normed, 2 * i)
                            for j in range(GS):
                                op = pe.transpose(ps_e[:, j * P:(j + 1) * P], on[:, j, :], const["ident"][:, :])
                            op.then_inc(ontr_done, 1)
                        if at == (1, 1) and seq_on(2 * i + 3):
                            transpose_max(pe, 2 * i + 3, 1, i)
                        if at == (1, 2) and group_on(i - 1):
                            wait(pe, oT_ready, i)
                            if h_out:
                                op = pe.matmul(ps_e[:, 0:GT], wo[:, :], oT[:, :], start=True, stop=True)
                            else:
                                for j in range(GS):
                                    op = pe.matmul(ps_e[:, j * P:(j + 1) * P], oT[:, j * P:(j + 1) * P], wo[:, :], start=True, stop=True)
                            op.then_inc(oproj_done, 1)
                        if at == (1, 2) and group_on(p1):
                            if own_kv:
                                wait(pe, xn_ready, GS * (p1 + 1))
                            else:
                                wait(pe, in_dma[r % 2], 2 * lap + r // 2 + 3, unit=16)
                            wait(pe, v_ready, p1)
                            for j in range(GS):
                                op = pe.transpose(ps_x[:, j * P:(j + 1) * P], xn[:, r % 2, j, :], const["ident"][:, :])
                            op.then_inc(xtr_done, 1)

            def transpose_max(pe, m, s, i):
                wait(pe, m_parts, m + 1)
                wait(pe, m_split, m)
                wait(pe, xT_ready if s == 0 else kf_ready, i + 4, NG)
                pe.transpose((ps_x, ps_q)[s][0:2 * H, 0:P // 2].bitcast(BF16), mp[:, s, :, :].rearrange("q k h -> q (k h)"), const["ident16"][:, :]).then_inc(mtr_done, 1)

            def transpose_out(pe, n, s):
                wait(pe, o_copied, n + 1)
                wait(pe, o_normed, n)
                for b in range(NB):
                    op = pe.transpose(ps_e[:, b * P:(b + 1) * P], osb[:, s, b * P:(b + 1) * P], const["ident"][:, :])
                op.then_inc(otr_done, 1)

            schedule(pe, body, pe.Fori)


def clear_stacks(eng, const, which, done=None):
    if which == "qst":
        eng.memset(const["qst"][:, :, :, :].bitcast(U32), 0)
    else:
        eng.memset(const["v1"][:, :, :, :, :].bitcast(U32), 0).then_inc(done, 1)
        eng.wait_ge(done, 1)
        eng.memset(const["v1"][:, :, :, :, HD:HD + 1], 1.0)
        eng.memset(const["kst"][:, :, :, :], 1.0)


def setup_stage(nc, const, c, alpha, loads):
    with semaphores(nc) as take, ExitStack() as ctx:
        def sb(n, shape, dt=F32):
            return ctx.enter_context(nc.sbuf_tensor(f"set_{n}", shape, dt))

        def sem(n):
            return take(f"set_{n}")

        dist, mask_qk, mask_kq = sb("dist", [P, P]), sb("mqk", [P, P]), sb("mkq", [P, P])
        a = sb("a", [P, H])
        pos, neg, low = sb("pos", [P, H]), sb("neg", [P, H]), sb("low", [P, H])
        slope = sb("slope", [P, H])
        part, rest = sb("part", [P, 3, H], BF16), sb("rest", [P, 2, H])
        landed, step, act_step, loaded = sem("landed"), sem("step"), sem("act_step"), sem("loaded")
        step_pool = sem("step_pool")
        block = ctx.enter_context(nc.Block())

        @block.sync
        def _(sync):
            sync.dma_start(const["ident"][:, :], c["ident"]).then_inc(landed, 16)
            sync.dma_start(dist[:, :], c["dist"]).then_inc(landed, 16)
            sync.dma_start(mask_qk[:, :], c["mask"]).then_inc(landed, 16)
            sync.dma_start(mask_kq[:, :], c["mask_t"]).then_inc(landed, 16)
            sync.dma_start(a[:, :], alpha.partition_broadcast(P)).then_inc(landed, 16)
            for tile, dram in loads:
                sync.dma_start(tile, dram).then_inc(loaded, 16)
            sync.wait_ge(landed, 80)
            sync.wait_ge(loaded, 16 * len(loads))

        @block.gpsimd
        def _(pool):
            clear_stacks(pool, const, "kst", step_pool)

        @block.scalar
        def _(act):
            act.wait_ge(step, 1)
            nc.scalar.activation(low[:, :], neg[:, :], ACT.Exp).then_inc(act_step, 1)
            act.wait_ge(act_step, 1)
            nc.scalar.activation(neg[:, :], low[:, :], ACT.Ln, bias=1.0).then_inc(act_step, 1)

        @block.vector
        def _(dve):
            dve.memset(const["minus_half"][:, :], -0.5)
            clear_stacks(dve, const, "qst")
            dve.wait_ge(landed, 80)
            n = 0

            def then(op):
                nonlocal n
                n += 1
                op.then_inc(step, 1)
                dve.wait_ge(step, n)

            then(dve.scalar_tensor_tensor(out=neg[:, :], in0=a[:, :], scalar=-1.0, in1=a[:, :], op0=ALU.mult, op1=ALU.min))
            then(dve.tensor_scalar(pos[:, :], a[:, :], 0.0, None, ALU.max))
            dve.wait_ge(act_step, 2)
            then(dve.scalar_tensor_tensor(out=slope[:, :], in0=pos[:, :], scalar=-1.0, in1=neg[:, :], op0=ALU.mult, op1=ALU.subtract))
            then(dve.tensor_copy(part[:, 0, :], slope[:, :]))
            then(dve.tensor_tensor(rest[:, 0, :], slope[:, :], part[:, 0, :], ALU.subtract))
            then(dve.tensor_copy(part[:, 1, :], rest[:, 0, :]))
            then(dve.tensor_tensor(part[:, 2, :], rest[:, 0, :], part[:, 1, :], ALU.subtract))
            then(dve.tensor_copy(const["ident16"][:, :], const["ident"][:, :]))
            for k in range(3):
                then(dve.tensor_tensor(const["slope"][:, k, :, :], const["ident16"][:, :].unsqueeze(1).to_broadcast([P, H, P]),
                                       part[:, k, :].unsqueeze(2).to_broadcast([P, H, P]), ALU.mult))
            then(dve.tensor_copy(const["dist"][:, :], dist[:, :]))
            then(dve.tensor_copy(const["mask_qk"][:, :, :], mask_qk[:, :].unsqueeze(1).to_broadcast([P, HB, P])))
            then(dve.tensor_copy(const["mask_kq"][:, :, :], mask_kq[:, :].unsqueeze(1).to_broadcast([P, HB, P])))


def decay_stage(nc, X, ctx_dram, const, weights_dram):
    Q = 4
    with semaphores(nc) as take, ExitStack() as ctx:
        def sb(n, shape, dt=F32):
            return ctx.enter_context(nc.sbuf_tensor(f"decay_{n}", shape, dt))

        weights = sb("weights", [P, P])
        c = sb("c", [P, 2, Q, P])
        sq = sb("sq", [P, 2, Q * P])
        stat6, stat = sb("stat6", [P, Q, 6]), sb("stat", [P, Q, 2])
        vareps, rstd = sb("vareps", [P, Q]), sb("rstd", [P, Q])
        xn = sb("xn", [P, Q, P])
        prod = sb("prod", [P, Q, P])
        ps_r = ctx.enter_context(nc.psum_tensor("decay_ps_r", [P, 2, Q * P], F32))
        w_in, c_in = take("decay_w_in"), [take("decay_c_in0"), take("decay_c_in1")]
        squared, r_ready, stats_a, stats_ready = take("decay_squared"), take("decay_r_ready"), take("decay_stats_a"), take("decay_stats_ready")
        var_ready, rstd_ready, xn_ready, multiplied, added = (take(f"decay_{k}") for k in ("var_ready", "rstd_ready", "xn_ready", "multiplied", "added"))
        block = ctx.enter_context(nc.Block())
        N = NSEQ // Q

        @block.sync
        def _(sync):
            sync.dma_start(weights[:, :], weights_dram).then_inc(w_in, 16)
            for g in range(N):
                wait(sync, squared, g - 1)
                sync.dma_start(c[:, g % 2, :, :], ctx_dram[Q * g:Q * (g + 1)].rearrange("s t d -> t s d")).then_inc(c_in[g % 2], 16)

        @block.scalar
        def _(act):
            for g in range(N):
                act.wait_ge(c_in[g % 2], 16 * (g // 2 + 1))
                wait(act, r_ready, g - 1)
                nc.scalar.activation(sq[:, g % 2, :], c[:, g % 2, :, :].rearrange("t s d -> t (s d)"), ACT.Square).then_inc(squared, 1)

        @block.tensor
        def _(pe):
            pe.wait_ge(w_in, 16)
            for g in range(N):
                wait(pe, squared, g + 1)
                wait(pe, multiplied, g - 1)
                pe.matmul(ps_r[:, g % 2, :], weights[:, :], sq[:, g % 2, :], start=True, stop=True).then_inc(r_ready, 1)

        @block.gpsimd
        def _(pool):
            for g in range(N):
                pool.wait_ge(stats_ready, g + 1)
                nc.gpsimd.tensor_scalar(vareps[:, :], stat[:, :, 1], EPS, None, ALU.add).then_inc(var_ready, 1)
                pool.wait_ge(var_ready, g + 1)
                nc.gpsimd.tensor_tensor(rstd[:, :], vareps[:, :], const["minus_half"][:, 0:Q], ALU.pow).then_inc(rstd_ready, 1)

        @block.vector
        def _(dve):
            for g in range(N):
                for j in range(Q):
                    dve.bn_stats(stat6[:, j, :], X[:, Q * g + j, :]).then_inc(stats_a, 1)
                wait(dve, xn_ready, Q * g)
                for j in range(Q):
                    dve.wait_ge(stats_a, Q * g + j + 1)
                    op = dve.bn_aggr(stat[:, j, :], stat6[:, j, :])
                op.then_inc(stats_ready, 1)
                dve.wait_ge(rstd_ready, g + 1)
                wait(dve, multiplied, g)
                for j in range(Q):
                    dve.tensor_scalar(xn[:, j, :], X[:, Q * g + j, :], stat[:, j, 0:1], rstd[:, j:j + 1],
                                      ALU.subtract, ALU.mult).then_inc(xn_ready, 1)
                dve.wait_ge(xn_ready, Q * (g + 1))
                dve.wait_ge(r_ready, g + 1)
                wait(dve, added, g)
                dve.tensor_tensor(prod[:, :, :], xn[:, :, :], ps_r[:, g % 2, :].rearrange("t (s d) -> t s d", s=Q), ALU.mult).then_inc(multiplied, 1)
                dve.wait_ge(multiplied, g + 1)
                dve.tensor_tensor(X[:, Q * g:Q * (g + 1), :], X[:, Q * g:Q * (g + 1), :], prod[:, :, :], ALU.add).then_inc(added, 1)


def ffn_stage(nc, name, X, w, const, rows_dram, out_dram, top2):
    Q = 4
    N = NSEQ // Q
    K = 2 if top2 else 1
    BLOCKS = rows_dram.shape[0] // SLOTS
    assert BLOCKS % RB == 0
    with semaphores(nc) as take, ExitStack() as ctx:
        def sb(n, shape, dt=F32):
            return ctx.enter_context(nc.sbuf_tensor(f"{name}_{n}", shape, dt))

        def psum(n, shape):
            return ctx.enter_context(nc.psum_tensor(f"{name}_{n}", shape, F32))

        def sem(n):
            return take(f"{name}_{n}")

        W1, W2 = sb("W1", [P, NE, FF + FC]), sb("W2", [P, NE, FF + P])
        w1, w2 = sb("w1", [P, 2, FF + FC]), sb("w2", [P, 2, FF + P])
        wg, bg = sb("wg", [P, NE]), sb("bg", [P, NE])
        tri = sb("tri", [P, P])
        tri16, ones16 = sb("tri16", [P, P], BF16), sb("ones16", [P, P], BF16)
        table = sb("table", [P, TABLE])
        first = table[:, 0:NE]
        steps = table[:, NE:NE + STEPS]
        below = table[:, NE + STEPS:NE + STEPS + NE * NE].rearrange("p (a b) -> p a b", b=NE)
        block_of = table[:, NE + STEPS + NE * NE:NE + STEPS + NE * NE + BLOCKS + 2]
        home = sb("home", [P, NSEQ])
        rows = [sb(f"rows{k}", [P, NSEQ, ROW]) for k in range(K)]
        pad = sb("pad", [P, ROW])
        stat6, stat = sb("stat6", [P, NSEQ, 6]), sb("stat", [P, NSEQ, 2])
        vareps, rstd = sb("vareps", [P, NSEQ]), sb("rstd", [P, NSEQ])
        lg = sb("lg", [P, NSEQ, NE])
        val, best = sb("val", [P, NSEQ, NE]), [sb(f"best{k}", [P, NSEQ, NE]) for k in range(K)]
        top, pick = [sb(f"top{k}", [P, NSEQ]) for k in range(K)], sb("pick", [P, NSEQ])
        ex, den = sb("ex", [P, NSEQ, NE if K == 1 else 1]), sb("den", [P, NSEQ])
        gate1 = sb("gate1", [P, NSEQ])
        best16 = sb("best16", [P, NSEQ, NE], BF16)
        tot = sb("tot", [P, 2, NSEQ, NE])
        count, over = sb("count", [P, NE]), sb("over", [P, NE, STEPS])
        nblk, base, ends = sb("nblk", [P, NE]), sb("base", [P, NE]), sb("ends", [P, NE])
        below_n, past = sb("below_n", [P, NE, NE]), sb("past", [P, BLOCKS + 2, NE])
        owner = sb("owner", [P, BLOCKS + 2])
        expert = sb("expert", [P, BLOCKS + 2], I32)
        slotf = sb("slotf", [P, K, NSEQ])
        slot = sb("slot", [P, K, NSEQ], I32)
        xb = sb("xb", [P, RB, ST, ROW])
        xT = sb("xT", [P, 2, SLOTS])
        hid = sb("hid", [P, 2, FC, SLOTS])
        yb = sb("yb", [P, RB, ST, P])
        goal, gates = sb("goal", [P, RB, ST], I32), sb("gates", [P, RB, ST])
        xnT = hid[:, :, :, :].rearrange("p a c s -> p (a c s)")[:, 0:2 * Q * P].rearrange("p (a c) -> p a c", a=2)
        ps_x = psum("ps_x", [P, 2, 512])
        ps_h = psum("ps_h", [P, 4, 512])
        ps_y = psum("ps_y", [P, 2, 512])
        ps_g, ps_c, ps_n = (ps_h[:, k, 0:NSEQ * NE] for k in range(3))

        w_in, e_in, padded, filled = sem("w_in"), sem("e_in"), sem("padded"), sem("filled")
        stats_a, stats_ready, var_ready, rstd_ready, xn_ready = (sem(k) for k in ("stats_a", "stats_ready", "var_ready", "rstd_ready", "xn_ready"))
        xtr_done, xT_ready, lg_done = (sem(k) for k in ("xtr_done", "xT_ready", "lg_done"))
        step, chosen, diff_ready, ex_ready, counted = (sem(k) for k in ("step", "chosen", "diff_ready", "ex_ready", "counted"))
        copied, ranked, rows_ready, slots_ready, scattered, experts_ready = (sem(k) for k in ("copied", "ranked", "rows_ready", "slots_ready", "scattered", "experts_ready"))
        xb_in = [sem(f"xb_in{k}") for k in range(RB)]
        y_out = [sem(f"y_out{k}") for k in range(RB)]
        w1_ready, w2_ready, btr_done, bT_ready = (sem(k) for k in ("w1_ready", "w2_ready", "btr_done", "bT_ready"))
        h_done, h_ready, y_done, y_biased, y_ready = (sem(k) for k in ("h_done", "h_ready", "y_done", "y_biased", "y_ready"))
        ends_ready = sem("ends_ready")
        passed_act, passed_dve, passed_pool, passed_pe, passed_sync = (sem(f"passed_{k}") for k in ("act", "dve", "pool", "pe", "sync"))
        block = ctx.enter_context(nc.Block())

        def b_on(b, least):
            return not isinstance(b, int) or b >= least

        def blocks(eng, body, engines_loop):
            for b in range(RB):
                body(eng, b, b, 0)
            with engines_loop(1, BLOCKS // RB) as lap:
                for t in range(RB):
                    body(eng, lap * RB + t, t, lap)

        @block.sync
        def _(sync):
            for tile, dram in ((wg[:, :], w["wg"]), (tri[:, :], w["tri"]), (home[:, :], w["home"]), (bg[:, :], w["bg"].partition_broadcast(P)),
                               (table[:, :], w["table"].partition_broadcast(P))):
                sync.dma_start(tile, dram).then_inc(w_in, 16)
            sync.wait_ge(padded, 1)
            sync.dma_start(rows_dram.rearrange("(n p) c -> p n c", p=P), pad[:, :].unsqueeze(1).to_broadcast([P, BLOCKS * ST, ROW])).then_inc(filled, 16)
            sync.dma_start(out_dram.rearrange("(n p) c -> p n c", p=P), X[:, :, :]).then_inc(filled, 16)
            sync.dma_start(W1[:, :, 0:FF], w["w1"].rearrange("e d f -> d e f")).then_inc(e_in, 16)
            sync.dma_start(W1[:, :, FF:], w["b1"]).then_inc(e_in, 16)
            for e in range(NE):
                sync.dma_start(W2[:, e, 0:FF].rearrange("f (c d) -> f c d", d=P), w["w2"][e].rearrange("(c f) d -> f c d", f=P)).then_inc(e_in, 16)
            sync.dma_start(W2[:, :, FF:].rearrange("p e d -> p e d"), w["b2"].rearrange("e d -> (e d)").partition_broadcast(P).rearrange("p (e d) -> p e d", d=P)).then_inc(e_in, 16)
            sync.wait_ge(scattered, 16 * K * NSEQ)

            def body(sync, b, t, lap):
                wait(sync, btr_done, b - RB + 1)
                settle(sync, passed_sync)
                wait(sync, ends_ready, b - RB + 1)
                settle(sync, passed_sync)
                sync.dma_start(xb[:, t, :, :], rows_dram[bass.ds(b * SLOTS, SLOTS)].rearrange("(j p) c -> p j c", p=P)).then_inc(xb_in[t], 16)

            blocks(sync, body, sync.Fori)
            for t in range(RB):
                sync.wait_ge(y_out[t], 16 * ST * (BLOCKS // RB))

        @block.gpsimd
        def _(pool):
            for g in range(N):
                pool.wait_ge(stats_ready, g + 1)
                at = slice(Q * g, Q * (g + 1))
                nc.gpsimd.tensor_scalar(vareps[:, at], stat[:, at, 1], EPS, None, ALU.add).then_inc(var_ready, 1)
                pool.wait_ge(var_ready, g + 1)
                nc.gpsimd.tensor_tensor(rstd[:, at], vareps[:, at], const["minus_half"][:, 0:Q], ALU.pow).then_inc(rstd_ready, 1)
            pool.wait_ge(filled, 32)
            pool.wait_ge(rows_ready, 1)
            pool.wait_ge(slots_ready, 1)
            for k in range(K):
                for s in range(NSEQ):
                    pool.indirect_dma_start(rows_dram, bass.IndirectOffsetOnAxis(ap=slot[:, k, s:s + 1], axis=0), rows[k][:, s, :], None,
                                            bounds_check=BLOCKS * SLOTS - 1, oob_is_err=False).then_inc(scattered, 16)

            def body(pool, b, t, lap):
                if top2 and b_on(b, 1):
                    wait(pool, y_out[(t - 1) % RB], lap + (t - 1) // RB + 1, unit=16 * ST)
                    settle(pool, passed_pool)
                wait(pool, y_ready, b + 1)
                settle(pool, passed_pool)
                for j in range(ST):
                    pool.indirect_dma_start(out_dram, bass.IndirectOffsetOnAxis(ap=goal[:, t, j:j + 1], axis=0), yb[:, t, j, :], None,
                                            bounds_check=NSEQ * P - 1, oob_is_err=False, compute_op=ALU.add).then_inc(y_out[t], 16)

            blocks(pool, body, pool.Fori)

        @block.tensor
        def _(pe):
            pe.wait_ge(w_in, 16 * 5)
            for g in range(N + 1):
                if g < N:
                    pe.wait_ge(xn_ready, Q * (g + 1))
                    wait(pe, xT_ready, g - 1)
                    for j in range(Q):
                        op = pe.transpose(ps_x[:, g % 2, j * P:(j + 1) * P], rows[0][:, Q * g + j, 0:P], const["ident"][:, :])
                    op.then_inc(xtr_done, 1)
                if g:
                    pe.wait_ge(xT_ready, g)
                    for j in range(Q):
                        s = Q * (g - 1) + j
                        op = pe.matmul(ps_g[:, s * NE:(s + 1) * NE], xnT[:, (g - 1) % 2, j * P:(j + 1) * P], wg[:, :], start=True, stop=True)
                    op.then_inc(lg_done, 1)
            pe.wait_ge(chosen, 1)
            pe.matmul(ps_c, tri16[:, :], best16[:, :, :].rearrange("t s e -> t (s e)"), start=True, stop=True)
            pe.matmul(ps_n, ones16[:, :], best16[:, :, :].rearrange("t s e -> t (s e)"), start=True, stop=True).then_inc(counted, 1)

            pe.wait_ge(ranked, 1)

            def transpose(b, t, uses):
                wait(pe, xb_in[t], uses, unit=16)
                wait(pe, bT_ready, b - 1)
                for j in range(ST):
                    op = pe.transpose(ps_x[:, t % 2, j * P:(j + 1) * P], xb[:, t, j, 0:P], const["ident"][:, :])
                op.then_inc(btr_done, 1)

            def hidden(b, t):
                wait(pe, w1_ready, b + 1)
                wait(pe, bT_ready, b + 1)
                for c in range(FC):
                    wait(pe, h_ready, (b - 1) * FC + c + 1)
                    pe.matmul(ps_h[:, c, 0:SLOTS], w1[:, t % 2, c * P:(c + 1) * P], xT[:, t % 2, :],
                              start=True, stop=True).then_inc(h_done, 1)

            def output(b, t):
                wait(pe, w2_ready, b + 1)
                wait(pe, h_ready, (b + 1) * FC)
                wait(pe, y_biased, b - 1)
                for j in range(ST):
                    for c in range(FC):
                        op = pe.matmul(ps_y[:, t % 2, j * P:(j + 1) * P], hid[:, t % 2, c, j * P:(j + 1) * P], w2[:, t % 2, c * P:(c + 1) * P],
                                       start=c == 0, stop=c == FC - 1)
                op.then_inc(y_done, 1)

            def body(pe, b, t, lap):
                transpose(b, t, lap + 1)
                if b_on(b, 1):
                    hidden(b - 1, (t - 1) % RB)
                if b_on(b, 2):
                    output(b - 2, (t - 2) % RB)

            blocks(pe, body, pe.Fori)
            hidden(BLOCKS - 1, RB - 1)
            output(BLOCKS - 2, RB - 2)
            output(BLOCKS - 1, RB - 1)

        @block.scalar
        def _(act):
            for g in range(N):
                act.wait_ge(xtr_done, g + 1)
                wait(act, lg_done, g - 1)
                nc.scalar.activation(xnT[:, g % 2, :], ps_x[:, g % 2, :], ACT.Identity).then_inc(xT_ready, 1)
            if top2:
                for g in range(N):
                    op = nc.scalar.activation(rows[1][:, Q * g:Q * (g + 1), 0:P], rows[0][:, Q * g:Q * (g + 1), 0:P], ACT.Identity)
                op.then_inc(copied, 1)
            act.wait_ge(diff_ready, 1)
            nc.scalar.activation(ex[:, :, :], ex[:, :, :], ACT.Exp).then_inc(ex_ready, 1)
            act.wait_ge(e_in, 16 * (NE + 3))
            act.wait_ge(experts_ready, 1)

            def weights(b, t):
                e = act.value_load(expert[0:1, bass.ds(b, 1)], min_val=0, max_val=NE - 1)
                nc.scalar.activation(w1[:, t % 2, :], W1[:, bass.ds(e, 1), :].rearrange("p e c -> p (e c)"), ACT.Identity).then_inc(w1_ready, 1)

            def hidden(b, t):
                for c in range(FC):
                    wait(act, h_done, b * FC + c + 1)
                    wait(act, y_done, b - 1)
                    nc.scalar.activation(hid[:, t % 2, c, :], ps_h[:, c, 0:SLOTS], ACT.Gelu if top2 else ACT.Relu,
                                         bias=w1[:, t % 2, FF + c:FF + c + 1]).then_inc(h_ready, 1)

            weights(0, 0)
            weights(1, 1)

            def body(act, b, t, lap):
                wait(act, btr_done, b + 1)
                wait(act, h_done, (b - 1) * FC)
                nc.scalar.activation(xT[:, t % 2, :], ps_x[:, t % 2, 0:SLOTS], ACT.Identity).then_inc(bT_ready, 1)
                if b_on(b, 1):
                    hidden(b - 1, (t - 1) % RB)
                    wait(act, h_ready, b * FC)
                    settle(act, passed_act)
                    weights(b + 1, (t + 1) % RB)

            blocks(act, body, act.Fori)
            hidden(BLOCKS - 1, RB - 1)

        @block.vector
        def _(dve):
            dve.memset(pad[:, 0:P], 0.0)
            dve.memset(pad[:, P + 1:], 0.0)
            dve.memset(pad[:, P:P + 1], float(NSEQ * P)).then_inc(padded, 1)

            def normalise(g):
                dve.wait_ge(rstd_ready, g + 1)
                for s in range(Q * g, Q * (g + 1)):
                    dve.tensor_scalar(rows[0][:, s, 0:P], X[:, s, :], stat[:, s, 0:1], rstd[:, s:s + 1],
                                      ALU.subtract, ALU.mult).then_inc(xn_ready, 1)

            for g in range(N):
                for j in range(Q):
                    dve.bn_stats(stat6[:, Q * g + j, :], X[:, Q * g + j, :]).then_inc(stats_a, 1)
                for j in range(Q):
                    dve.wait_ge(stats_a, Q * g + j + 1)
                    op = dve.bn_aggr(stat[:, Q * g + j, :], stat6[:, Q * g + j, :])
                op.then_inc(stats_ready, 1)
                if g:
                    normalise(g - 1)
            normalise(N - 1)
            dve.wait_ge(w_in, 16 * 5)
            dve.wait_ge(lg_done, N)
            n = 0

            def then(op):
                nonlocal n
                n += 1
                op.then_inc(step, 1)
                dve.wait_ge(step, n)

            S3 = [P, NSEQ, NE]

            def per_token(v):
                return v[:, :].unsqueeze(2).to_broadcast(S3)

            def per_expert(v):
                return v.unsqueeze(1).to_broadcast(S3)

            then(dve.tensor_copy(tri16[:, :], tri[:, :]))
            then(dve.memset(ones16[:, :], 1.0))
            then(dve.tensor_tensor(lg[:, :, :], ps_g.rearrange("t (s e) -> t s e", e=NE), per_expert(bg[:, :]), ALU.add))
            left = lg
            for k in range(K):
                then(dve.tensor_reduce(top[k][:, :], left[:, :, :], AX.X, ALU.max))
                then(dve.tensor_tensor(val[:, :, :], left[:, :, :], per_token(top[k]), ALU.is_equal))
                then(dve.tensor_tensor(val[:, :, :], val[:, :, :], per_expert(first), ALU.mult))
                then(dve.tensor_reduce(pick[:, :], val[:, :, :], AX.X, ALU.max))
                then(dve.tensor_tensor(best[k][:, :, :], val[:, :, :], per_token(pick), ALU.is_equal))
                if k + 1 < K:
                    left = val
                    then(dve.scalar_tensor_tensor(out=left[:, :, :], in0=best[k][:, :, :], scalar=-3e38, in1=lg[:, :, :], op0=ALU.mult, op1=ALU.add))
            if top2:
                then(dve.tensor_tensor(best16[:, :, :], best[0][:, :, :], best[1][:, :, :], ALU.add))
            else:
                then(dve.tensor_copy(best16[:, :, :], best[0][:, :, :]))
            dve.sem_inc(chosen, 1)
            if top2:
                then(dve.tensor_tensor(ex[:, :, 0], top[1][:, :], top[0][:, :], ALU.subtract))
            else:
                then(dve.tensor_tensor(ex[:, :, :], lg[:, :, :], per_token(top[0]), ALU.subtract))
            dve.sem_inc(diff_ready, 1)
            dve.wait_ge(counted, 1)
            n_seq = ps_n.rearrange("t (s e) -> t s e", e=NE)
            then(dve.tensor_copy(tot[:, 0, :, :], n_seq))
            a = 0
            for d in (1, 2, 4, 8, 16):
                dve.tensor_copy(tot[:, 1 - a, 0:d, :], tot[:, a, 0:d, :]).then_inc(step, 1)
                n += 1
                then(dve.tensor_tensor(tot[:, 1 - a, d:, :], tot[:, a, d:, :], tot[:, a, :NSEQ - d, :], ALU.add))
                a = 1 - a
            then(dve.tensor_scalar(count[:, :], tot[:, a, NSEQ - 1, :], float(NSEQ * P if top2 else CAP), None, ALU.min))
            then(dve.tensor_tensor(over[:, :, :], count[:, :].unsqueeze(2).to_broadcast([P, NE, STEPS]),
                                   steps.unsqueeze(1).to_broadcast([P, NE, STEPS]), ALU.is_gt))
            then(dve.tensor_reduce(nblk[:, :], over[:, :, :], AX.X, ALU.add))
            then(dve.tensor_tensor(below_n[:, :, :], below, nblk[:, :].unsqueeze(1).to_broadcast([P, NE, NE]), ALU.mult))
            then(dve.tensor_reduce(base[:, :], below_n[:, :, :], AX.X, ALU.add))
            then(dve.tensor_tensor(ends[:, :], base[:, :], nblk[:, :], ALU.add))
            SB = [P, BLOCKS + 2, NE]
            then(dve.tensor_tensor(past[:, :, :], block_of.unsqueeze(2).to_broadcast(SB), ends[:, :].unsqueeze(1).to_broadcast(SB), ALU.is_ge))
            then(dve.tensor_reduce(owner[:, :], past[:, :, :], AX.X, ALU.add))
            then(dve.tensor_scalar(owner[:, :], owner[:, :], float(NE - 1), None, ALU.min))
            then(dve.tensor_copy(expert[:, :], owner[:, :]))
            then(dve.tensor_tensor(tot[:, a, :, :], tot[:, a, :, :], n_seq, ALU.subtract))
            then(dve.tensor_tensor(tot[:, a, :, :], tot[:, a, :, :], ps_c.rearrange("t (s e) -> t s e", e=NE), ALU.add))
            dve.sem_inc(ranked, 1)
            dve.sem_inc(experts_ready, 1)
            if not top2:
                then(dve.tensor_scalar(val[:, :, :], tot[:, a, :, :], float(CAP), None, ALU.is_gt))
                then(dve.scalar_tensor_tensor(out=tot[:, a, :, :], in0=val[:, :, :], scalar=float(2 * BLOCKS * SLOTS), in1=tot[:, a, :, :], op0=ALU.mult, op1=ALU.add))
            then(dve.tensor_scalar(base[:, :], base[:, :], float(SLOTS), -1.0, ALU.mult, ALU.add))
            then(dve.tensor_tensor(tot[:, a, :, :], tot[:, a, :, :], per_expert(base[:, :]), ALU.add))
            for k in range(K):
                then(dve.tensor_tensor(val[:, :, :], tot[:, a, :, :], best[k][:, :, :], ALU.mult))
                then(dve.tensor_reduce(slotf[:, k, :], val[:, :, :], AX.X, ALU.add))
            then(dve.tensor_copy(slot[:, :, :], slotf[:, :, :]))
            dve.sem_inc(slots_ready, 1)
            for k in range(K):
                then(dve.tensor_copy(rows[k][:, :, P], home[:, :]))
            dve.wait_ge(ex_ready, 1)
            if top2:
                then(dve.tensor_scalar(den[:, :], ex[:, :, 0], 1.0, None, ALU.add))
                then(dve.reciprocal(den[:, :], den[:, :]))
                then(dve.tensor_copy(rows[0][:, :, P + 1], den[:, :]))
                then(dve.tensor_tensor(rows[1][:, :, P + 1], ex[:, :, 0], den[:, :], ALU.mult))
                dve.wait_ge(copied, 1)
            else:
                then(dve.tensor_reduce(den[:, :], ex[:, :, :], AX.X, ALU.add))
                then(dve.reciprocal(rows[0][:, :, P + 1], den[:, :]))
            dve.sem_inc(rows_ready, 1)
            dve.wait_ge(e_in, 16 * (NE + 3))

            def weights(b, t):
                e = dve.value_load(expert[0:1, bass.ds(b, 1)], min_val=0, max_val=NE - 1)
                dve.tensor_copy(w2[:, t % 2, :], W2[:, bass.ds(e, 1), :].rearrange("p e c -> p (e c)")).then_inc(w2_ready, 1)

            def output(b, t):
                wait(dve, ends_ready, b + 1)
                wait(dve, y_done, b + 1)
                y = yb[:, t, :, :]
                dve.tensor_tensor(y, ps_y[:, t % 2, 0:SLOTS].rearrange("p (j d) -> p j d", j=ST),
                                  w2[:, t % 2, FF:].unsqueeze(1).to_broadcast([P, ST, P]), ALU.add).then_inc(y_biased, 1)
                wait(dve, y_biased, b + 1)
                dve.tensor_tensor(y, y, gates[:, t, :].unsqueeze(2).to_broadcast([P, ST, P]), ALU.mult).then_inc(y_ready, 1)

            weights(0, 0)
            weights(1, 1)

            def body(dve, b, t, lap):
                wait(dve, xb_in[t], lap + 1, unit=16)
                wait(dve, y_out[t], lap, unit=16 * ST)
                dve.tensor_copy(goal[:, t, :], xb[:, t, :, P])
                dve.tensor_copy(gates[:, t, :], xb[:, t, :, P + 1]).then_inc(ends_ready, 1)
                if b_on(b, 2):
                    output(b - 2, (t - 2) % RB)
                    weights(b, t)

            blocks(dve, body, dve.Fori)
            for b in (BLOCKS - 2, BLOCKS - 1):
                output(b, b % RB)


def store_stage(nc, X, out):
    with semaphores(nc) as take, ExitStack() as ctx:
        stored = take("stored")
        block = ctx.enter_context(nc.Block())

        @block.sync
        def _(sync):
            sync.dma_start(out.rearrange("s t d -> t s d"), X[:, :, :]).then_inc(stored, 16)
            sync.wait_ge(stored, 16)


def ffn_inputs(nc, a, n):
    rows = nc.dram_tensor(f"rows{n}", (blocks_for(n + 1) * SLOTS, ROW), F32, kind="Internal").ap()
    return {k: a[f"F{n}_{k}"] for k in ("wg", "bg", "w1", "b1", "w2", "b2")} | {k: a[f"c_{k}"] for k in ("tri", "home", "table")}, rows


def decoder(nc, a, out, stages=99):
    with ExitStack() as ctx:
        def sb(n, shape, dt=F32):
            return ctx.enter_context(nc.sbuf_tensor(n, shape, dt))

        X = sb("X", [P, NSEQ, P])
        const = {"ident": sb("ident", [P, P]), "ident16": sb("ident16", [P, P], BF16), "minus_half": sb("minus_half", [P, 8])}
        w, loads = [], []
        for n in range(4):
            tiles = {k: sb(f"A{n}_{k}", [P, P]) for k in ("wq", "wk", "wv", "wo")}
            loads += [(tiles[k][:, :], a[f"A{n}_{k}"]) for k in ("wq", "wk", "wv", "wo")]
            for k in ("bq", "bk", "bv", "bo"):
                if f"A{n}_{k}" in a:
                    column = k in ("bq", "bk") or n == 1 and k == "bo"
                    tile = sb(f"A{n}_{k}", [P, 1] if column else [P, P])
                    dram = a[f"A{n}_{k}"]
                    loads.append((tile[:, :], dram if len(dram.shape) == 2 else
                                  dram.rearrange("(a b) -> a b", b=1) if column else dram.partition_broadcast(P)))
                    tiles["bo_col" if n == 1 and k == "bo" else k] = tile
            w.append(tiles)
        with ExitStack() as stacks:
            def sbs(n, shape, dt=F32):
                return stacks.enter_context(nc.sbuf_tensor(n, shape, dt))

            const["qst"], const["kst"] = sbs("qst", [P, RING, H, GT], BF16), sbs("kst", [P, RING, H, GT], BF16)
            const["v1"] = sbs("v1", [P, RING, GS, H, 32])
            with ExitStack() as layer0:
                def sb0(n, shape, dt=F32):
                    return layer0.enter_context(nc.sbuf_tensor(n, shape, dt))

                hT = sb0("hT", [P, NSEQ * P])
                const["dist"] = sb0("dist", [P, P], BF16)
                const["slope"] = sb0("slope", [P, 3, H, P], BF16)
                const["mask_qk"] = sb0("mask_qk", [P, HB, P], BF16)
                const["mask_kq"] = sb0("mask_kq", [P, HB, P], BF16)
                setup_stage(nc, const, {"ident": a["c_ident"], "dist": a["c_dist"], "mask": a["c_mask"], "mask_t": a["c_mask_t"]},
                            a["L0_attn_decay_alpha"], loads)
                attention_stage(nc, "alibi", X, w[0], HD ** -0.5, "alibi", False, None, False, hT, const, x_dram=a["x"])
                if stages > 1:
                    attention_stage(nc, "causal", X, w[1], HD ** -0.5, "causal", False, None, True, hT, const)
                    attention_stage(nc, "cross", X, w[2], HD ** -0.5, None, True, a["ctx"], False, hT, const)
            if stages > 2:
                w0, rows = ffn_inputs(nc, a, 0)
                x_ffn = nc.dram_tensor("x_ffn", (NSEQ, P, P), F32, kind="Internal").ap()
                ffn_stage(nc, "ffn0", X, w0, const, rows, x_ffn.rearrange("s t d -> (s t) d"), False)
            if stages > 3:
                attention_stage(nc, "block", X, w[3], P ** -0.5, None, False, None, False, None, const, x_dram=x_ffn)
        if stages > 4:
            decay_stage(nc, X, a["ctx"], const, a["c_decay"])
        if stages > 5:
            w1, rows = ffn_inputs(nc, a, 1)
            ffn_stage(nc, "ffn1", X, w1, const, rows, out.rearrange("s t d -> (s t) d"), True)
        else:
            store_stage(nc, X, out)


def lay_out(inputs):
    v = {k: np.asarray(x) for k, x in inputs.items()}
    a = {"x": v["x"], "ctx": v["ctx_1024"], "L0_attn_decay_alpha": v["L0_attn_decay_alpha"]}

    def by_dim(wt):
        return wt.reshape(-1, H, HD).swapaxes(1, 2).reshape(-1, P)

    wT = v["L0_attn_qkv_w"].T
    b = v["L0_attn_qkv_b"]
    a["A0_wq"], a["A0_wk"], a["A0_wv"] = by_dim(wT[:, 0:P]), by_dim(wT[:, P:2 * P]), wT[:, 2 * P:]
    a["A0_bq"], a["A0_bk"], a["A0_bv"] = by_dim(b[0:P]).reshape(P, 1), by_dim(b[P:2 * P]).reshape(P, 1), b[2 * P:]
    a["A0_wo"], a["A0_bo"] = v["L0_attn_out_w"].T, v["L0_attn_out_b"]
    for n in (1, 2):
        for k in "qk":
            a[f"A{n}_w{k}"] = v[f"L0_xattn_W{k}{n}"].transpose(1, 2, 0).reshape(P, P)
            a[f"A{n}_b{k}"] = v[f"L0_xattn_b{k}{n}"].T.reshape(P, 1)
        a[f"A{n}_wv"] = v[f"L0_xattn_Wv{n}"].transpose(1, 0, 2).reshape(P, P)
        a[f"A{n}_bv"] = v[f"L0_xattn_bv{n}"].reshape(P)
        a[f"A{n}_wo"], a[f"A{n}_bo"] = v[f"L0_xattn_Wo{n}"], v[f"L0_xattn_bo{n}"]
    for k in "qkv":
        w = np.zeros((H, HD, HD, H) if k != "v" else (H, HD, H, HD), np.float32)
        for h in range(H):
            if k != "v":
                w[h, :, :, h] = v[f"L1_attn_W{k}"].T
            else:
                w[h, :, h, :] = v["L1_attn_Wv"].T
        a[f"A3_w{k}"] = w.reshape(P, P)
    a["A3_wo"], a["A3_bo"] = v["L1_attn_W_out"].T, v["L1_attn_b_out"]
    for n, l, up in ((0, "L0_ffn_w1", "L0_ffn"), (1, "L1_ffn_W1", "L1_ffn")):
        a[f"F{n}_w1"], a[f"F{n}_w2"] = v[l], v[l[:-1] + "2"]
        a[f"F{n}_b1"] = v[f"{up}_b1"].reshape(NE, FC, P).transpose(2, 0, 1)
        a[f"F{n}_b2"] = v[f"{up}_b2"]
    a["F0_wg"], a["F0_bg"] = v["L0_ffn_gate_w"].T, v["L0_ffn_gate_b"]
    a["F1_wg"], a["F1_bg"] = v["L1_ffn_Wg"], v["L1_ffn_bg"]
    n = np.arange(P)
    a["c_tri"] = (n[:, None] <= n[None, :]).astype(np.float32)
    a["c_table"] = np.concatenate([NE - n[:NE], SLOTS * n[:STEPS], (n[None, :NE] < n[:NE, None]).reshape(-1), n[:blocks_for(2) + 2]]).astype(np.float32)
    a["c_home"] = (np.arange(NSEQ)[None, :] * P + n[:, None]).astype(np.float32)
    ahead = n[None, :] - n[:, None]
    a["c_decay"] = np.where(ahead >= 0, DECAY ** np.maximum(ahead, 0).astype(np.float64), 0.0).astype(np.float32)
    a["c_ident"] = np.eye(P, dtype=np.float32)
    a["c_dist"] = np.abs(n[:, None] - n[None, :]).astype(np.float32)
    a["c_mask"] = np.where(n[None, :] > n[:, None], np.float32(-1e30), np.float32(0))
    a["c_mask_t"] = np.ascontiguousarray(a["c_mask"].T)
    return {k: np.ascontiguousarray(x) for k, x in a.items()}


def kernel(**inputs):
    import concourse.bacc as _bacc
    from concourse.bass_utils import run_bass_kernel_spmd as _run

    nc = _bacc.Bacc("TRN2", target_bir_lowering=False, num_devices=1)
    arrays, args = {}, {}
    for name, a in lay_out(inputs).items():
        arrays[f"in_{name}"] = a
        args[name] = nc.dram_tensor(f"in_{name}", a.shape, mybir.dt.from_np(a.dtype), kind="ExternalInput").ap()
    out = nc.dram_tensor("out", (NSEQ, P, P), F32, kind="ExternalOutput").ap()
    decoder(nc, args, out)
    r = _run(nc, [arrays], core_ids=[0])
    return r.results[0]["out"]
```

```python
from contextlib import ExitStack, contextmanager

import numpy as np
import concourse.bass as bass
from concourse import mybir

ALU = mybir.AluOpType
ACT = mybir.ActivationFunctionType
AX = mybir.AxisListType
F32 = mybir.dt.float32
BF16 = mybir.dt.bfloat16
U32 = mybir.dt.uint32
I32 = mybir.dt.int32

P = 128
NSEQ = 32
H = 16
HD = 8
GS = 2
NG = NSEQ // GS
GT = GS * P
RING = 4
HB = 4
NB = H // HB
EPS = 1e-5
DECAY = 0.9
ONES = 0x3F803F80
NE = 8
FF = 512
FC = FF // P
CAP = 640
ST = 2
SLOTS = ST * P
RB = 4
ROW = P + 2
STEPS = NSEQ * P // SLOTS

Q_PART = (0, 0, 0, 1, 1, 2)
K_PART = (0, 1, 2, 0, 1, 0)
PAIRS = len(Q_PART)
ROWS_MAX = P - 2


def blocks_for(k):
    return k * NSEQ * P // SLOTS + NE - 1


def region_for(k):
    return (CAP if k == 1 else NSEQ * P) + SLOTS


def table_for(k):
    e, blk = np.arange(NE), np.arange(blocks_for(k))
    return {"first": NE - e,
            "steps": SLOTS * np.arange(STEPS),
            "below": (e[None, :] < e[:, None]).reshape(-1),
            "start": region_for(k) * e - 1,
            "last": region_for(k) * e - 1 + (CAP if k == 1 else NSEQ * P),
            "block": blk}


def wait(eng, sem, count, most=None, unit=1):
    if isinstance(count, int):
        if most is not None:
            count = min(count, most)
        if count <= 0:
            return
    eng.wait_ge(sem, count * unit)


def settle(eng, passed):
    eng.sem_inc(passed, 1)


@contextmanager
def semaphores(nc):
    taken = []

    def take(name):
        taken.append(nc.alloc_semaphore(name))
        return taken[-1]

    yield take
    nc.clear_and_free_semaphores(taken)
    nc.all_engine_barrier()


def attention_stage(nc, name, X, parts, hT, const, x_dram, later=()):
    with semaphores(nc) as take, ExitStack() as ctx:
        def sb(n, shape, dt=F32):
            return ctx.enter_context(nc.sbuf_tensor(f"{name}_{n}", shape, dt))

        def psum(n, shape):
            return ctx.enter_context(nc.psum_tensor(f"{name}_{n}", shape, F32))

        def sem(n):
            return take(f"{name}_{n}")

        NGALL, NSALL = NG * len(parts), NSEQ * len(parts)
        qst, kst, v1 = const["qst"], const["kst"], const["v1"]
        ps_s = psum("ps_s", [P, 2, 512])
        ps_t = psum("ps_t", [P, 2, 512])
        ps_o = psum("ps_o", [P, NB, P])
        ps_x = psum("ps_x", [P, 512])
        ps_q = psum("ps_q", [P, 512])
        ps_e = psum("ps_e", [P, 512])

        bqs = sb("bqs", [P, len(parts)])
        xn = sb("xn", [P, 2, GS, P])
        stat6 = sb("stat6", [P, GS, 6])
        stat = sb("stat", [P, GS, 2])
        vareps = sb("vareps", [P, GS])
        rstd = sb("rstd", [P, GS])
        xnT = sb("xnT", [P, GT])
        qf, kf = sb("qf", [P, GT]), sb("kf", [P, GT])
        rest = sb("rest", [P, GT])
        qp, kp = sb("qp", [P, 2, 3, GT], BF16), sb("kp", [P, 2, 3, GT], BF16)
        mx = sb("mx", [P, 2, H])
        mp = sb("mp", [P, 2, 2, H], BF16)
        mpT = sb("mpT", [2 * H, 2, P], BF16)
        pt = sb("pt", [P, NB, HB * P])
        osb = sb("osb", [P, GS, NB * P])
        rden = sb("rden", [P, H])
        on = sb("on", [P, GS, P])
        oT = sb("oT", [P, GT])

        passed_pool, passed_dve, passed_sync = sem("passed_pool"), sem("passed_dve"), sem("passed_sync")
        bias_ready, later_in, tables_ready, masks_ready = (sem(n) for n in ("bias_ready", "later_in", "tables_ready", "masks_ready"))
        in_dma, kv_dma = [sem(f"in_dma{k}") for k in range(6)], [sem(f"kv_dma{k}") for k in range(2)]
        stats_a, stats_ready, var_ready, rstd_ready = sem("stats_a"), sem("stats_ready"), sem("var_ready"), sem("rstd_ready")
        xn_ready, xtr_done, xT_ready = sem("xn_ready"), sem("xtr_done"), sem("xT_ready")
        q_done, k_done, v_done = sem("q_done"), sem("k_done"), sem("v_done")
        qf_ready, kf_ready, v_ready = sem("qf_ready"), sem("kf_ready"), sem("v_ready")
        part, q_split, k_split = sem("part"), sem("q_split"), sem("k_split")
        stack_dma = [sem(f"stack_dma{k}") for k in range(RING)]
        s_ready, s_max = sem("s_ready"), sem("s_max")
        mtr_done, m_hi, m_parts, m_split = sem("mtr_done"), sem("m_hi"), sem("m_parts"), sem("m_split")
        m_dma = [sem(f"m_dma{k}") for k in range(2)]
        t_ready, t_fallen, p_ready, pv_done = sem("t_ready"), sem("t_fallen"), sem("p_ready"), sem("pv_done")
        o_copied, otr_done, den_ready, o_normed = sem("o_copied"), sem("otr_done"), sem("den_ready"), sem("o_normed")
        ontr_done, oT_ready, oproj_done, biased, x_done = sem("ontr_done"), sem("oT_ready"), sem("oproj_done"), sem("biased"), sem("x_done")

        def schedule(eng, body, engines_loop):
            straight = 2 * RING
            for i in range(-4, 1):
                body(eng, i, i % RING, i // RING, None)
            for a in range(len(parts)):
                with engines_loop(0, (NG - straight) // RING) as lap:
                    for t in range(1, 1 + RING):
                        body(eng, a * NG + lap * RING + t, t % RING, a * NG // RING + lap + t // RING, a)
                for i in range((a + 1) * NG - straight + 1, (a + 1) * NG + 1):
                    body(eng, i, i % RING, i // RING, None)

        at_late = NG - 2 * RING + 1

        def part_of(g, a):
            return g // NG if isinstance(g, int) else a

        def seq_on(n):
            return not isinstance(n, int) or 0 <= n < NSALL

        def group_on(g):
            return not isinstance(g, int) or 0 <= g < NGALL

        def falls_on_dve(c):
            return c % 2 == 1

        def own_kv(g, a):
            return group_on(g) and parts[part_of(g, a)].get("kv_dram") is None

        def biased_before(a):
            return NG * sum(not p.get("h_out") for p in parts[:a])

        block = ctx.enter_context(nc.Block())

        @block.sync
        def _(sync):
            for g in range(NG):
                sync.dma_start(X[:, GS * g:GS * (g + 1), :],
                               x_dram[GS * g:GS * (g + 1)].rearrange("s t d -> t s d")).then_inc(in_dma[min(g, 5)], 16)

            def body(sync, i, r, lap, a):
                p1, p2 = i + 4, i + 3
                if group_on(p1) and not own_kv(p1, a):
                    at = part_of(p1, a)
                    wait(sync, xtr_done, p1 - 1)
                    settle(sync, passed_sync)
                    sync.dma_start(xn[:, r % 2, :, :], parts[at]["kv_dram"][bass.ds((p1 - at * NG) * GS, GS)].rearrange("s t d -> t s d")).then_inc(kv_dma[r % 2], 16)
                if seq_on(2 * i + 2):
                    max_rows(sync, 2 * i + 2, 0, (r + 1) % RING)
                if group_on(p2):
                    slot = (r + 3) % RING
                    wait(sync, t_ready, (p2 - RING + 1) * GS * NB)
                    settle(sync, passed_sync)
                    stack(qst, qp, Q_PART, qf_ready, q_split, p2, slot, r)
                if group_on(p2):
                    stack(kst, kp, K_PART, kf_ready, k_split, p2, slot, r)
                if seq_on(2 * i + 3):
                    max_rows(sync, 2 * i + 3, 1, (r + 1) % RING)

            def stack(st, parts_of, which, first_ready, all_ready, g, slot, r):
                wait(sync, first_ready, g + 1)
                settle(sync, passed_sync)
                for later_parts in (False, True):
                    if later_parts:
                        wait(sync, all_ready, g + 1)
                        settle(sync, passed_sync)
                    for k in range(PAIRS):
                        if (which[k] > 0) == later_parts:
                            sync.dma_start(st[HD * k:HD * (k + 1), slot, :, :], parts_of[:, (r + 3) % 2, which[k], :]).then_inc(stack_dma[slot], 16)

            def max_rows(sync, m, s, slot):
                wait(sync, m_split, m + 1)
                settle(sync, passed_sync)
                sync.dma_start(qst[ROWS_MAX:P, slot, :, s * P:(s + 1) * P], mpT[:, s, :]).then_inc(m_dma[s], 16)

            schedule(sync, body, sync.Fori)

        @block.gpsimd
        def _(pool):
            def split(pool, src, dst, ready, done, g, n0):
                wait(pool, ready, g + 1)
                nc.gpsimd.tensor_tensor(rest[:, :], src[:, :], dst[:, 0, :], ALU.subtract).then_inc(part, 1)
                nc.gpsimd.tensor_tensor(dst[:, 1, :], src[:, :], dst[:, 0, :], ALU.subtract).then_inc(part, 1)
                wait(pool, part, n0 + 2)
                nc.gpsimd.tensor_tensor(dst[:, 2, :], rest[:, :], dst[:, 1, :], ALU.subtract).then_inc(done, 1)

            def body(pool, i, r, lap, a):
                p1, p2 = i + 4, i + 3
                if own_kv(p1, a):
                    wait(pool, stats_ready, p1 + 1)
                    settle(pool, passed_pool)
                    nc.gpsimd.tensor_scalar(vareps[:, :], stat[:, :, 1], EPS, None, ALU.add).then_inc(var_ready, 1)
                    wait(pool, var_ready, p1 + 1)
                    nc.gpsimd.tensor_tensor(rstd[:, :], vareps[:, :], const["minus_half"][:, 0:GS], ALU.pow).then_inc(rstd_ready, 1)
                if group_on(p2):
                    wait(pool, k_split, p2)
                    split(pool, qf, qp[:, (r + 3) % 2], qf_ready, q_split, p2, 4 * p2)
                    wait(pool, q_split, p2 + 1)
                    split(pool, kf, kp[:, (r + 3) % 2], kf_ready, k_split, p2, 2 + 4 * p2)

            schedule(pool, body, pool.Fori)

        @block.vector
        def _(dve):
            def scale_bias(n):
                if "bq" in parts[n]["w"]:
                    dve.tensor_scalar(bqs[:, n:n + 1], parts[n]["w"]["bq"][:, :], parts[n]["scale"], None, ALU.mult).then_inc(bias_ready, 1)

            scale_bias(0)

            def smax(dve, m, s, c):
                wait(dve, s_ready, m * NB + c + 1)
                if c == 0:
                    wait(dve, m_parts, m - 1)
                dve.tensor_reduce(mx[:, s, HB * c:HB * (c + 1)], ps_s[:, c % 2, :].rearrange("q (h k) -> q h k", h=HB),
                                  AX.X, ALU.max).then_inc(s_max, 1)

            def msplit(dve, m, s):
                wait(dve, s_max, (m + 1) * NB)
                wait(dve, mtr_done, m - 1)
                dve.tensor_scalar(mp[:, s, 0, :], mx[:, s, :], -1.0, None, ALU.mult).then_inc(m_hi, 1)
                wait(dve, m_hi, m + 1)
                dve.scalar_tensor_tensor(out=mp[:, s, 1, :], in0=mx[:, s, :], scalar=-1.0, in1=mp[:, s, 0, :],
                                         op0=ALU.mult, op1=ALU.subtract).then_inc(m_parts, 1)

            def mcopy(dve, m, s, uses):
                wait(dve, mtr_done, m + 1)
                wait(dve, m_dma[s], uses, unit=16)
                dve.tensor_copy(mpT[:, s, :], (ps_x, ps_q)[s][0:2 * H, 0:P // 2].bitcast(BF16)).then_inc(m_split, 1)

            def normalise(dve, n, s):
                wait(dve, otr_done, n + 1)
                heads = ps_e[:, :].rearrange("q (h e) -> q h e", e=32)
                dve.reciprocal(rden[:, :], heads[:, :, HD:HD + 1].rearrange("q h e -> q (h e)")).then_inc(den_ready, 1)
                wait(dve, den_ready, n + 1)
                dve.tensor_tensor(on[:, s, :].rearrange("q (h e) -> q h e", e=HD), heads[:, :, 0:HD],
                                  rden[:, :].unsqueeze(2).to_broadcast([P, H, HD]), ALU.mult).then_inc(o_normed, 1)

            def alibi_tables():
                full = [P, H, P]
                dve.tensor_copy(const["dist"][:, :], const["dist32"][:, :])
                dve.tensor_tensor(const["falloff"][:, :, :], const["dist32"][:, :].unsqueeze(1).to_broadcast(full),
                                  const["neg_alpha"][:, :].unsqueeze(2).to_broadcast(full), ALU.mult)
                for k in range(3):
                    op = dve.tensor_tensor(const["slope"][:, k, :, :], const["ident16"][:, :].unsqueeze(1).to_broadcast(full),
                                           const["alpha_parts"][:, k, :].unsqueeze(2).to_broadcast(full), ALU.mult)
                op.then_inc(tables_ready, 1)

            def body(dve, i, r, lap, a):
                p1, p2 = i + 4, i + 3
                for s in range(GS):
                    m = 2 * i + 3 + s
                    for c in range(NB):
                        if seq_on(m):
                            smax(dve, m, (1 + s) % 2, c)
                        if c == 0 and seq_on(m - 1):
                            msplit(dve, m - 1, s % 2)
                        n = 2 * i + s
                        if seq_on(n) and parts[part_of(i, a)].get("extra") == "alibi" and falls_on_dve(c):
                            wait(dve, t_ready, n * NB + c + 1)
                            dve.tensor_tensor(ps_t[:, c % 2, :], ps_t[:, c % 2, :],
                                              const["falloff"][:, HB * c:HB * (c + 1), :].rearrange("p h q -> p (h q)"), ALU.add).then_inc(t_fallen, 1)
                        at = (s, c)
                        if later and isinstance(i, int) and i == at_late and at == (0, 3):
                            dve.wait_ge(later_in, 16 * len(later))
                            for n in range(1, len(parts)):
                                scale_bias(n)
                            for mask in ("mask_qk", "mask_kq"):
                                op = dve.tensor_copy(const[mask][:, :, :], const[mask + "32"][:, :].unsqueeze(1).to_broadcast([P, HB, P]))
                            op.then_inc(masks_ready, 1)
                        if at == (0, 2) and isinstance(i, int) and i == -2 and parts[0].get("extra") == "alibi":
                            alibi_tables()
                        if at == (0, 1) and seq_on(2 * i - 2):
                            normalise(dve, 2 * i - 2, 0)
                        if at == (0, 1) and seq_on(2 * i + 2):
                            mcopy(dve, 2 * i + 2, 0, i + 1)
                        if at == (0, 1) and own_kv(p1, a):
                            if isinstance(p1, int) and p1 < 5:
                                dve.wait_ge(in_dma[p1], 16)
                            if isinstance(p1, int) and p1 == 4:
                                dve.wait_ge(in_dma[5], 16 * (NG - 5))
                            g1 = p1 - part_of(p1, a) * NG
                            if part_of(p1, a):
                                wait(dve, x_done, p1 - NG + 1)
                            wait(dve, xn_ready, GS * p1)
                            for j in range(GS):
                                dve.bn_stats(stat6[:, j, :], X[:, bass.ds(g1 * GS + j, 1), :].rearrange("t s d -> t (s d)")).then_inc(stats_a, 1)
                            for j in range(GS):
                                wait(dve, stats_a, GS * p1 + j + 1)
                                settle(dve, passed_dve)
                                op = dve.bn_aggr(stat[:, j, :], stat6[:, j, :])
                            op.then_inc(stats_ready, 1)
                        if at == (0, 3) and seq_on(2 * i - 1):
                            normalise(dve, 2 * i - 1, 1)
                        if at == (0, 3) and own_kv(p1, a):
                            g1 = p1 - part_of(p1, a) * NG
                            wait(dve, rstd_ready, p1 + 1)
                            wait(dve, xtr_done, p1 - 1)
                            for j in range(GS):
                                dve.tensor_scalar(xn[:, r % 2, j, :], X[:, bass.ds(g1 * GS + j, 1), :].rearrange("t s d -> t (s d)"),
                                                  stat[:, j, 0:1], rstd[:, j:j + 1], ALU.subtract, ALU.mult).then_inc(xn_ready, 1)
                        if at == (1, 3) and seq_on(2 * i + 3):
                            mcopy(dve, 2 * i + 3, 1, i + 1)
                        if at == (1, 0) and group_on(p2):
                            wait(dve, v_done, p2 + 1)
                            wait(dve, pv_done, (p2 - RING + 1) * GS * NB)
                            out = v1[:, (r + 3) % RING, :, :, 0:HD]
                            vals = ps_x[:, 0:GT].rearrange("t (s h e) -> t s h e", s=GS, e=HD)
                            bv = parts[part_of(p2, a)]["w"].get("bv")
                            if bv is not None:
                                for j in range(GS):
                                    op = dve.tensor_tensor(out[:, j], vals[:, j], bv[:, :].rearrange("t (h e) -> t h e", e=HD), ALU.add)
                            else:
                                op = dve.tensor_copy(out, vals)
                            op.then_inc(v_ready, 1)
                        if at == (1, 3) and group_on(i - 1) and not parts[part_of(i - 1, a)].get("h_out"):
                            pa = part_of(i - 1, a)
                            g = i - 1 - pa * NG
                            bo = parts[pa]["w"]["bo"]
                            wait(dve, oproj_done, i)
                            res = ps_e[:, 0:GT].rearrange("t (s d) -> t s d", s=GS)
                            dve.tensor_tensor(res, res, bo[:, :].unsqueeze(1).to_broadcast([P, GS, P]), ALU.add).then_inc(biased, 1)
                            wait(dve, biased, biased_before(pa) + g + 1)
                            xg = X[:, bass.ds(g * GS, GS), :]
                            dve.tensor_tensor(xg, xg, res, ALU.add).then_inc(x_done, 1)

            schedule(dve, body, dve.Fori)

        @block.scalar
        def _(act):
            if "bq" in parts[0]["w"]:
                act.wait_ge(bias_ready, 1)

            def exp_bank(act, n, c, extra):
                wait(act, t_ready, n * NB + c + 1)
                if extra == "alibi" and falls_on_dve(c):
                    wait(act, t_fallen, n * (NB // 2) + c // 2 + 1)
                wait(act, pv_done, (n - 1) * NB + c + 1)
                nc.scalar.activation(pt[:, c, :], ps_t[:, c % 2, :], ACT.Exp).then_inc(p_ready, 1)

            def copy_o(act, n, s):
                wait(act, pv_done, (n + 1) * NB)
                wait(act, otr_done, n - 1)
                nc.scalar.activation(osb[:, s, :], ps_o[:, :, :].rearrange("p b q -> p (b q)"), ACT.Identity).then_inc(o_copied, 1)

            def parts_free(act, p2, r, lap):
                wait(act, stack_dma[(r + 1) % RING], lap + (r + 1) // RING + 1, unit=16 * 2 * PAIRS)

            def body(act, i, r, lap, a):
                p1, p2 = i + 4, i + 3
                if isinstance(i, int) and i <= 0:
                    for tile, dram in later[i + 4::5]:
                        act.dma_start(tile, dram).then_inc(later_in, 16)
                if later and isinstance(i, int) and i == at_late + 2:
                    act.wait_ge(later_in, 16 * len(later))
                    act.wait_ge(bias_ready, len(parts))
                for s in range(GS):
                    n = 2 * i + s
                    for c in range(NB):
                        if seq_on(n):
                            exp_bank(act, n, c, parts[part_of(i, a)].get("extra"))
                        at = (s, c)
                        if at == (0, 1) and seq_on(2 * i - 1):
                            copy_o(act, 2 * i - 1, 1)
                        if at == (0, 2) and group_on(p2):
                            wait(act, q_done, p2 + 1)
                            wait(act, q_split, p2)
                            pa = part_of(p2, a)
                            parts_free(act, p2, r, lap)
                            for dst in (qf[:, :], qp[:, (r + 3) % 2, 0, :]):
                                op = nc.scalar.activation(dst, ps_q[:, 0:GT], ACT.Identity, scale=parts[pa]["scale"],
                                                          **({"bias": bqs[:, pa:pa + 1]} if "bq" in parts[pa]["w"] else {}))
                            op.then_inc(qf_ready, 1)
                        if at == (0, 3) and group_on(p2):
                            wait(act, k_done, p2 + 1)
                            wait(act, k_split, p2)
                            pw = parts[part_of(p2, a)]["w"]
                            for dst in (kf[:, :], kp[:, (r + 3) % 2, 0, :]):
                                op = nc.scalar.activation(dst, ps_q[:, 0:GT], ACT.Identity,
                                                          **({"bias": pw["bk"][:, :]} if "bk" in pw else {}))
                            op.then_inc(kf_ready, 1)
                        if at == (1, 1) and seq_on(2 * i):
                            copy_o(act, 2 * i, 0)
                        if at == (1, 2) and group_on(i - 1):
                            wait(act, ontr_done, i)
                            wait(act, oproj_done, i - 1)
                            nc.scalar.activation(oT[:, :], ps_e[:, 0:GT], ACT.Identity).then_inc(oT_ready, 1)
                        if at == (1, 3) and group_on(i - 1) and parts[part_of(i - 1, a)].get("h_out"):
                            pa = part_of(i - 1, a)
                            wait(act, oproj_done, i)
                            nc.scalar.activation(hT[:, bass.ds((i - 1 - pa * NG) * GT, GT)], ps_e[:, 0:GT], ACT.Identity,
                                                 bias=parts[pa]["w"]["bo_col"][:, :]).then_inc(x_done, 1)
                        if at == (1, 3) and group_on(p1):
                            wait(act, xtr_done, p1 + 1)
                            wait(act, v_done, p1)
                            nc.scalar.activation(xnT[:, :], ps_x[:, 0:GT], ACT.Identity).then_inc(xT_ready, 1)

            schedule(act, body, act.Fori)

        @block.tensor
        def _(pe):
            def scores(pe, m, s, c, slot, uses, extra):
                wait(pe, s_max, m * NB + c - 1)
                if c == 0:
                    wait(pe, stack_dma[slot], uses, unit=16 * 2 * PAIRS)
                if extra == "alibi":
                    pe.matmul(ps_s[:, c % 2, :], const["dist"][:, :], const["slope"][:, 0, HB * c:HB * (c + 1), :],
                              start=True, stop=False, skip_group_check=True)
                if extra == "causal":
                    pe.matmul(ps_s[:, c % 2, :], const["ident16"][:, :], const["mask_qk"][:, :, :],
                              start=True, stop=False, skip_group_check=True)
                for j in range(HB):
                    h = HB * c + j
                    op = pe.matmul(ps_s[:, c % 2, j * P:(j + 1) * P], qst[0:ROWS_MAX, slot, h, s * P:(s + 1) * P],
                                   kst[0:ROWS_MAX, slot, h, s * P:(s + 1) * P], start=extra is None, stop=True, skip_group_check=extra is not None)
                op.then_inc(s_ready, 1)

            def scores_t(pe, n, s, c, slot, i, extra):
                wait(pe, p_ready, n * NB + c - 1)
                if c == 0:
                    wait(pe, m_dma[s], i + 1, unit=16)
                if extra == "alibi" and not falls_on_dve(c):
                    for k in range(3):
                        pe.matmul(ps_t[:, c % 2, :], const["dist"][:, :], const["slope"][:, k, HB * c:HB * (c + 1), :],
                                  start=k == 0, stop=False, skip_group_check=True)
                if extra == "causal":
                    pe.matmul(ps_t[:, c % 2, :], const["ident16"][:, :], const["mask_kq"][:, :, :],
                              start=True, stop=False, skip_group_check=True)
                mixed = extra == "causal" or extra == "alibi" and not falls_on_dve(c)
                for j in range(HB):
                    h = HB * c + j
                    op = pe.matmul(ps_t[:, c % 2, j * P:(j + 1) * P], kst[:, slot, h, s * P:(s + 1) * P],
                                   qst[:, slot, h, s * P:(s + 1) * P], start=not mixed, stop=True, skip_group_check=mixed)
                op.then_inc(t_ready, 1)

            def weigh(pe, n, s, c, slot, g):
                wait(pe, p_ready, n * NB + c + 1)
                if c == 0:
                    wait(pe, o_copied, n)
                    wait(pe, v_ready, g + 1)
                for j in range(HB):
                    op = pe.matmul(ps_o[32 * j:32 * (j + 1), c, :], v1[:, slot, s, HB * c + j, :],
                                   pt[:, c, j * P:(j + 1) * P], start=True, stop=True, tile_position=(0, 32 * j))
                op.then_inc(pv_done, 1)

            def body(pe, i, r, lap, a):
                p1, p2 = i + 4, i + 3
                if later and isinstance(i, int) and i == at_late + 2:
                    pe.wait_ge(later_in, 16 * len(later))
                    pe.wait_ge(masks_ready, 1)
                for s in range(GS):
                    m, n = 2 * i + 3 + s, 2 * i + s
                    m_slot = (r + 1 + s) % RING
                    if isinstance(i, int) and (i, s) == (-2, 1) and parts[0].get("extra") == "alibi":
                        pe.wait_ge(tables_ready, 1)
                    for c in range(NB):
                        at = (s, c)
                        if seq_on(m):
                            scores(pe, m, (1 + s) % 2, c, m_slot, lap + (r + 1 + s) // RING + 1, parts[part_of(i + 1 + s, a)].get("extra"))
                        if seq_on(n):
                            scores_t(pe, n, s, c, r, i, parts[part_of(i, a)].get("extra"))
                        if c > 1 and seq_on(n):
                            weigh(pe, n, s, c - 2, r, i)
                        if c <= 1 and seq_on(n - 1):
                            weigh(pe, n - 1, 1 - s, NB - 2 + c, (r - 1 + s) % RING, i - 1 + s)
                        if at == (0, 1) and group_on(p2):
                            wait(pe, xT_ready, p2 + 1)
                            wait(pe, m_split, 2 * i + 2, NSALL)
                            wait(pe, kf_ready, p2)
                            pa = part_of(p2, a)
                            if parts[pa].get("q_from_h"):
                                wait(pe, x_done, p2 - NG + 1)
                                src = hT[:, bass.ds((p2 - pa * NG) * GT, GT)]
                            else:
                                src = xnT[:, :]
                            pe.matmul(ps_q[:, 0:GT], parts[pa]["w"]["wq"][:, :], src, start=True, stop=True).then_inc(q_done, 1)
                        if at == (0, 1) and seq_on(2 * i - 2):
                            wait(pe, x_done, i - 1)
                            transpose_out(pe, 2 * i - 2, 0)
                        if at == (0, 1) and seq_on(2 * i + 2):
                            transpose_max(pe, 2 * i + 2, 0, i)
                        if at == (0, 3) and seq_on(2 * i - 1):
                            transpose_out(pe, 2 * i - 1, 1)
                        if at == (0, 3) and group_on(p2):
                            wait(pe, m_split, 2 * i + 3, NSALL)
                            for j in range(GS):
                                op = pe.matmul(ps_x[:, j * P:(j + 1) * P], xnT[:, j * P:(j + 1) * P], parts[part_of(p2, a)]["w"]["wv"][:, :], start=True, stop=True)
                            op.then_inc(v_done, 1)
                        if at == (0, 3) and group_on(p2):
                            wait(pe, qf_ready, p2 + 1)
                            pe.matmul(ps_q[:, 0:GT], parts[part_of(p2, a)]["w"]["wk"][:, :], xnT[:, :], start=True, stop=True).then_inc(k_done, 1)
                        if at == (1, 1) and group_on(i - 1):
                            wait(pe, o_normed, 2 * i)
                            for j in range(GS):
                                op = pe.transpose(ps_e[:, j * P:(j + 1) * P], on[:, j, :], const["ident"][:, :])
                            op.then_inc(ontr_done, 1)
                        if at == (1, 2) and seq_on(2 * i + 3):
                            transpose_max(pe, 2 * i + 3, 1, i)
                        if at == (1, 3) and group_on(i - 1):
                            wait(pe, oT_ready, i)
                            wo = parts[part_of(i - 1, a)]["w"]["wo"]
                            if parts[part_of(i - 1, a)].get("h_out"):
                                op = pe.matmul(ps_e[:, 0:GT], wo[:, :], oT[:, :], start=True, stop=True)
                            else:
                                for j in range(GS):
                                    op = pe.matmul(ps_e[:, j * P:(j + 1) * P], oT[:, j * P:(j + 1) * P], wo[:, :], start=True, stop=True)
                            op.then_inc(oproj_done, 1)
                        if at == (1, 2) and group_on(p1):
                            if own_kv(p1, a):
                                wait(pe, xn_ready, GS * (p1 + 1))
                            else:
                                wait(pe, kv_dma[r % 2], 2 * lap + r // 2 + 3 - part_of(p1, a) * NG // 2, unit=16)
                            wait(pe, v_ready, p1)
                            for j in range(GS):
                                op = pe.transpose(ps_x[:, j * P:(j + 1) * P], xn[:, r % 2, j, :], const["ident"][:, :])
                            op.then_inc(xtr_done, 1)

            def transpose_max(pe, m, s, i):
                wait(pe, m_parts, m + 1)
                wait(pe, m_split, m)
                wait(pe, xT_ready if s == 0 else kf_ready, i + 4, NGALL)
                pe.transpose((ps_x, ps_q)[s][0:2 * H, 0:P // 2].bitcast(BF16), mp[:, s, :, :].rearrange("q k h -> q (k h)"), const["ident16"][:, :]).then_inc(mtr_done, 1)

            def transpose_out(pe, n, s):
                wait(pe, o_copied, n + 1)
                wait(pe, o_normed, n)
                for b in range(NB):
                    op = pe.transpose(ps_e[:, b * P:(b + 1) * P], osb[:, s, b * P:(b + 1) * P], const["ident"][:, :])
                op.then_inc(otr_done, 1)

            schedule(pe, body, pe.Fori)


def setup_stage(nc, const, alpha, loads):
    with semaphores(nc) as take, ExitStack() as ctx:
        def sb(n, shape, dt=F32):
            return ctx.enter_context(nc.sbuf_tensor(f"set_{n}", shape, dt))

        def sem(n):
            return take(f"set_{n}")

        a = sb("a", [P, H])
        pos, neg, low = sb("pos", [P, H]), sb("neg", [P, H]), sb("low", [P, H])
        rest = sb("rest", [P, H])
        part, neg_alpha = const["alpha_parts"], const["neg_alpha"]
        landed, step, act_step, loaded = sem("landed"), sem("step"), sem("act_step"), sem("loaded")
        v1_clear = sem("v1_clear")
        qst, kst = const["qst"], const["kst"]
        block = ctx.enter_context(nc.Block())

        @block.sync
        def _(sync):
            sync.dma_start(const["ident"][:, :], loads[0][1]).then_inc(landed, 16)
            sync.dma_start(a[:, :], alpha.partition_broadcast(P)).then_inc(landed, 16)
            for tile, dram in loads[1:]:
                sync.dma_start(tile, dram).then_inc(loaded, 16)
            sync.wait_ge(landed, 32)
            sync.wait_ge(loaded, 16 * (len(loads) - 1))

        @block.gpsimd
        def _(pool):
            pool.memset(const["v1"][:, :, :, :, :].bitcast(U32), 0).then_inc(v1_clear, 1)
            pool.wait_ge(v1_clear, 1)
            pool.memset(const["v1"][:, :, :, :, HD:HD + 1], 1.0)
            pool.memset(kst[:, 1:, :, :].bitcast(U32), ONES)

        @block.scalar
        def _(act):
            act.wait_ge(landed, 32)
            act.wait_ge(step, 1)
            nc.scalar.activation(low[:, :], neg[:, :], ACT.Exp).then_inc(act_step, 1)
            act.wait_ge(act_step, 1)
            nc.scalar.activation(neg[:, :], low[:, :], ACT.Ln, bias=1.0).then_inc(act_step, 1)
            half = qst[:, RING // 2:, :, :].rearrange("p r h t -> p (r h t)").bitcast(F32)
            nc.scalar.activation(half, const["ident"][:, 0:1].to_broadcast([P, RING // 2 * H * GT // 2]), ACT.Identity, scale=0.0)

        @block.vector
        def _(dve):
            dve.memset(const["minus_half"][:, :], -0.5)
            dve.wait_ge(landed, 32)
            n = 0

            def then(op):
                nonlocal n
                n += 1
                op.then_inc(step, 1)
                dve.wait_ge(step, n)

            then(dve.scalar_tensor_tensor(out=neg[:, :], in0=a[:, :], scalar=-1.0, in1=a[:, :], op0=ALU.mult, op1=ALU.min))
            then(dve.tensor_scalar(pos[:, :], a[:, :], 0.0, None, ALU.max))
            dve.memset(qst[:, 0:RING // 2, :, :].bitcast(U32), 0)
            dve.memset(kst[:, 0:1, :, :].bitcast(U32), ONES)
            dve.wait_ge(act_step, 2)
            then(dve.scalar_tensor_tensor(out=neg_alpha[:, :], in0=pos[:, :], scalar=-1.0, in1=neg[:, :], op0=ALU.mult, op1=ALU.subtract))
            then(dve.tensor_copy(part[:, 0, :], neg_alpha[:, :]))
            then(dve.tensor_tensor(rest[:, :], neg_alpha[:, :], part[:, 0, :], ALU.subtract))
            then(dve.tensor_copy(part[:, 1, :], rest[:, :]))
            then(dve.tensor_tensor(part[:, 2, :], rest[:, :], part[:, 1, :], ALU.subtract))
            then(dve.tensor_copy(const["ident16"][:, :], const["ident"][:, :]))


def ffn_stage(nc, name, X, w, const, rows_dram, out_dram, top2, decay=None):
    Q = 4
    N = NSEQ // Q
    K = 2 if top2 else 1
    BLOCKS, REGION = blocks_for(K), region_for(K)
    EMPTY = NE * REGION
    C = 8
    NC = NSEQ // C
    CQ = C // Q
    with semaphores(nc) as take, ExitStack() as ctx:
        def sb(n, shape, dt=F32):
            return ctx.enter_context(nc.sbuf_tensor(f"{name}_{n}", shape, dt))

        def psum(n, shape):
            return ctx.enter_context(nc.psum_tensor(f"{name}_{n}", shape, F32))

        def sem(n):
            return take(f"{name}_{n}")

        W1, W2 = sb("W1", [P, NE, FF + FC]), sb("W2", [P, NE, FF + P])
        w1, w2 = sb("w1", [P, 2, FF + FC]), sb("w2", [P, 2, FF + P])
        wg, bg = sb("wg", [P, NE]), sb("bg", [P, NE])
        tri = sb("tri", [P, P])
        tri16, ones16 = sb("tri16", [P, P], BF16), sb("ones16", [P, P], BF16)
        consts, at = table_for(K), 0
        table = sb("table", [P, sum(len(v) for v in consts.values())])
        small = {}
        for key, v in consts.items():
            small[key] = table[:, at:at + len(v)]
            at += len(v)
        home = sb("home", [P, NSEQ])
        rows = [sb(f"rows{k}", [P, NSEQ, ROW]) for k in range(K)]
        pad = sb("pad", [P, ROW])
        stat6, stat = sb("stat6", [P, NSEQ, 6]), sb("stat", [P, NSEQ, 2])
        vareps, rstd = sb("vareps", [P, NSEQ]), sb("rstd", [P, NSEQ])
        lg = sb("lg", [P, NSEQ, NE])
        CE = [P, C, NE]
        val, best = sb("val", CE), [sb(f"best{k}", CE) for k in range(K)]
        top, pick = [sb(f"top{k}", [P, C]) for k in range(K)], sb("pick", [P, C])
        ex, den = sb("ex", [P, C, NE if K == 1 else 1]), sb("den", [P, C])
        best16 = sb("best16", CE, BF16)
        ranks, chunk = sb("ranks", CE), sb("chunk", [P, NE])
        run = sb("run", [P, NC + 1, NE])
        count, over = sb("count", [P, NE]), sb("over", [P, NE, STEPS])
        nblk, base, ends = sb("nblk", [P, NE]), sb("base", [P, NE]), sb("ends", [P, NE])
        below_n, offset, pads = sb("below_n", [P, NE, NE]), sb("offset", [P, NE]), sb("pads", [P, NE])
        BE = [P, BLOCKS, NE]
        begun, past = sb("begun", BE), sb("past", BE)
        owner, used, source = sb("owner", [P, BLOCKS]), sb("used", [P, BLOCKS]), sb("source", [P, BLOCKS])
        expert = sb("expert", [P, BLOCKS + 2], I32)
        source_i, pads_i = sb("source_i", [P, BLOCKS], I32), sb("pads_i", [P, NE], I32)
        slotf = sb("slotf", [P, K, C])
        slot = sb("slot", [P, K, NSEQ], I32)
        xb = sb("xb", [P, RB, ST, ROW])
        xT = sb("xT", [P, 2, SLOTS])
        hid = sb("hid", [P, 2, FC, SLOTS])
        yb = sb("yb", [P, RB, ST, P])
        goal, gates = sb("goal", [P, RB, ST], I32), sb("gates", [P, RB, ST])
        xnT = hid[:, :, :, :].rearrange("p a c s -> p (a c s)")[:, 0:2 * Q * P].rearrange("p (a c) -> p a c", a=2)
        ps_x = psum("ps_x", [P, 2, 512])
        ps_h = psum("ps_h", [P, 4, 512])
        ps_y = psum("ps_y", [P, 2, 512])
        ps_g = ps_h[:, 0:2, 0:C * NE]
        ps_c, ps_n = (ps_h[:, k, 0:C * NE] for k in (2, 3))
        if decay is not None:
            ctx_dram, weights_dram = decay
            weights = sb("weights", [P, P])
            cb, sq = sb("cb", [P, 2, Q, P]), sb("sq", [P, 2, Q * P])
            dstat6, dstat = sb("dstat6", [P, NSEQ, 6]), sb("dstat", [P, NSEQ, 2])
            dvareps, drstd = sb("dvareps", [P, NSEQ]), sb("drstd", [P, NSEQ])
            dxn, prod = sb("dxn", [P, Q, P]), sb("prod", [P, Q, P])
            ps_r = ps_y
        if decay is not None:
            order = "P0 N0 P1 N1 G0 P2 G1 N2 P3 G2 N3 G3".split()
        else:
            order = "P0 P1 P2 P3 N0 N1 G0 N2 G1 N3 G2 G3".split()

        def prologue(steps, order=order):
            for at in order:
                if at[0] in steps:
                    steps[at[0]](int(at[1]))

        w_in, e_in, padded = sem("w_in"), sem("e_in"), sem("padded")
        stats_a, stats_ready, var_ready, rstd_ready, xn_ready = (sem(k) for k in ("stats_a", "stats_ready", "var_ready", "rstd_ready", "xn_ready"))
        xtr_done, xT_ready, lg_done, lg_ready = (sem(k) for k in ("xtr_done", "xT_ready", "lg_done", "lg_ready"))
        step, chosen, diff_ready, ex_ready, counted = (sem(k) for k in ("step", "chosen", "diff_ready", "ex_ready", "counted"))
        copied, ranked, slots_ready, scattered, experts_ready = (sem(k) for k in ("copied", "ranked", "slots_ready", "scattered", "experts_ready"))
        xb_in = [sem(f"xb_in{k}") for k in range(RB)]
        y_out = [sem(f"y_out{k}") for k in range(RB)]
        w1_ready, w2_ready, btr_done, bT_ready = (sem(k) for k in ("w1_ready", "w2_ready", "btr_done", "bT_ready"))
        h_done, h_ready, y_done, y_biased, y_ready = (sem(k) for k in ("h_done", "h_ready", "y_done", "y_biased", "y_ready"))
        summed = sem("summed")
        pads_ready, goal_ready, pad_landed, c_in, d_in = sem("pads_ready"), sem("goal_ready"), sem("pad_landed"), [sem("c_in0"), sem("c_in1")], sem("d_in")
        dstats_a, dstats_ready, dvar_ready, drstd_ready = (sem(k) for k in ("dstats_a", "dstats_ready", "dvar_ready", "drstd_ready"))
        squared, r_ready, dxn_ready, multiplied, updated, stored = (sem(k) for k in ("squared", "r_ready", "dxn_ready", "multiplied", "updated", "stored"))
        passed_act, passed_pool, passed_sync = (sem(f"passed_{k}") for k in ("act", "pool", "sync"))
        block = ctx.enter_context(nc.Block())

        def b_on(b, least):
            return not isinstance(b, int) or b >= least

        def blocks(eng, body, engines_loop):
            for b in range(RB):
                body(eng, b, b, 0)
            with engines_loop(1, BLOCKS // RB) as lap:
                for t in range(RB):
                    body(eng, lap * RB + t, t, lap)
            for b in range(BLOCKS // RB * RB, BLOCKS):
                body(eng, b, b % RB, b // RB)

        padding = pad[:, :].unsqueeze(1).to_broadcast([P, ST, ROW])

        def pad_regions(eng, experts):
            eng.wait_ge(pads_ready, 1)
            for e in experts:
                at = eng.value_load(pads_i[0:1, e:e + 1], min_val=0, max_val=EMPTY - SLOTS)
                eng.dma_start(rows_dram[bass.ds(at, SLOTS)].rearrange("(j p) c -> p j c", p=P), padding).then_inc(pad_landed, 16)

        @block.sync
        def _(sync):
            for tile, dram in ((wg[:, :], w["wg"]), (tri[:, :], w["tri"]), (home[:, :], w["home"]), (bg[:, :], w["bg"].partition_broadcast(P)),
                               (table[:, :], w["table"].partition_broadcast(P))):
                sync.dma_start(tile, dram).then_inc(w_in, 16)
            if decay is not None:
                sync.dma_start(weights[:, :], weights_dram).then_inc(d_in, 16)
                for g in range(N):
                    wait(sync, squared, g - 1)
                    sync.dma_start(cb[:, g % 2, :, :], ctx_dram[Q * g:Q * (g + 1)].rearrange("s t d -> t s d")).then_inc(c_in[g % 2], 16)
            sync.dma_start(W1[:, :, 0:FF], w["w1"].rearrange("e d f -> d e f")).then_inc(e_in, 16)
            sync.dma_start(W1[:, :, FF:], w["b1"]).then_inc(e_in, 16)
            for e in range(NE):
                sync.dma_start(W2[:, e, 0:FF].rearrange("f (c d) -> f c d", d=P), w["w2"][e].rearrange("(c f) d -> f c d", f=P)).then_inc(e_in, 16)
            sync.dma_start(W2[:, :, FF:], w["b2"].rearrange("e d -> (e d)").partition_broadcast(P).rearrange("p (e d) -> p e d", d=P)).then_inc(e_in, 16)
            for c in range(NC):
                if decay is not None:
                    sync.wait_ge(updated, CQ * (c + 1))
                sync.dma_start(out_dram[c * C * P:(c + 1) * C * P].rearrange("(n p) c -> p n c", p=P), X[:, c * C:(c + 1) * C, :]).then_inc(stored, 16)
            sync.wait_ge(padded, 1)
            sync.dma_start(rows_dram[EMPTY:EMPTY + SLOTS].rearrange("(j p) c -> p j c", p=P), padding).then_inc(pad_landed, 16)
            pad_regions(sync, range(0, NE, 2))
            sync.wait_ge(experts_ready, 1)
            sync.wait_ge(pad_landed, 16 * (NE + 1))
            sync.wait_ge(scattered, 16 * K * NSEQ)

            def body(sync, b, t, lap):
                wait(sync, btr_done, b - RB + 1)
                settle(sync, passed_sync)
                wait(sync, goal_ready, b - RB + 1)
                settle(sync, passed_sync)
                at = sync.value_load(source_i[0:1, bass.ds(b, 1)], min_val=0, max_val=EMPTY)
                sync.dma_start(xb[:, t, :, :], rows_dram[bass.ds(at, SLOTS)].rearrange("(j p) c -> p j c", p=P)).then_inc(xb_in[t], 16)

            blocks(sync, body, sync.Fori)
            for t in range(RB):
                sync.wait_ge(y_out[t], 16 * ST * len(range(t, BLOCKS, RB)))

        @block.gpsimd
        def _(pool):
            def rsqrt(n, ready, var, st, ve, done, out):
                pool.wait_ge(ready, CQ * (n + 1))
                at = slice(C * n, C * (n + 1))
                nc.gpsimd.tensor_scalar(ve[:, at], st[:, at, 1], EPS, None, ALU.add).then_inc(var, 1)
                pool.wait_ge(var, n + 1)
                nc.gpsimd.tensor_tensor(out[:, at], ve[:, at], const["minus_half"][:, 0:C], ALU.pow).then_inc(done, 1)

            if decay is not None:
                for c in range(NC):
                    rsqrt(c, dstats_ready, dvar_ready, dstat, dvareps, drstd_ready, drstd)

            def scatter(c):
                pool.wait_ge(slots_ready, c + 1)
                for k in range(K):
                    for s in range(C * c, C * (c + 1)):
                        pool.indirect_dma_start(rows_dram, bass.IndirectOffsetOnAxis(ap=slot[:, k, s:s + 1], axis=0), rows[k][:, s, :], None,
                                                bounds_check=EMPTY - 1, oob_is_err=False).then_inc(scattered, 16)

            prologue({"P": lambda c: rsqrt(c, stats_ready, var_ready, stat, vareps, rstd_ready, rstd), "G": scatter},
                     "P0 P1 G0 P2 G1 P3 G2 G3".split() if decay is not None else order)
            pool.wait_ge(stored, 16 * NC)

            def body(pool, b, t, lap):
                if top2 and b_on(b, 1):
                    wait(pool, y_out[(t - 1) % RB], lap + (t - 1) // RB + 1, unit=16 * ST)
                    settle(pool, passed_pool)
                wait(pool, y_ready, b + 1)
                settle(pool, passed_pool)
                for j in range(ST):
                    pool.indirect_dma_start(out_dram, bass.IndirectOffsetOnAxis(ap=goal[:, t, j:j + 1], axis=0), yb[:, t, j, :], None,
                                            bounds_check=NSEQ * P - 1, oob_is_err=False, compute_op=ALU.add).then_inc(y_out[t], 16)

            blocks(pool, body, pool.Fori)

        @block.tensor
        def _(pe):
            pe.wait_ge(w_in, 16 * 5)
            if decay is not None:
                pe.wait_ge(d_in, 16)

            def decayed(c):
                for g in range(CQ * c, CQ * (c + 1)):
                    pe.wait_ge(squared, g + 1)
                    wait(pe, multiplied, g - 1)
                    pe.matmul(ps_r[:, g % 2, :], weights[:, :], sq[:, g % 2, :], start=True, stop=True).then_inc(r_ready, 1)

            def logits(c):
                wait(pe, lg_ready, c - 1)
                for g in range(CQ * c, CQ * (c + 1)):
                    pe.wait_ge(xn_ready, Q * (g + 1))
                    wait(pe, xT_ready, g - 1)
                    for j in range(Q):
                        op = pe.transpose(ps_x[:, g % 2, j * P:(j + 1) * P], rows[0][:, Q * g + j, 0:P], const["ident"][:, :])
                    op.then_inc(xtr_done, 1)
                for g in range(CQ * c, CQ * (c + 1)):
                    pe.wait_ge(xT_ready, g + 1)
                    for j in range(Q):
                        s = Q * (g % CQ) + j
                        op = pe.matmul(ps_g[:, c % 2, s * NE:(s + 1) * NE], xnT[:, g % 2, j * P:(j + 1) * P], wg[:, :], start=True, stop=True)
                    op.then_inc(lg_done, 1)

            def counts(c):
                pe.wait_ge(chosen, c + 1)
                wait(pe, ranked, c)
                op = pe.matmul(ps_c, tri16[:, :], best16[:, :, :].rearrange("t s e -> t (s e)"), start=True, stop=False, skip_group_check=True)
                for s in range(C - 1):
                    pe.matmul(ps_c[:, (s + 1) * NE:], ones16[:, :], best16[:, s:s + 1, :].to_broadcast([P, C - 1 - s, NE]),
                              start=False, stop=s == C - 2, skip_group_check=True)
                pe.matmul(ps_n, ones16[:, :], best16[:, :, :].rearrange("t s e -> t (s e)"), start=True, stop=True).then_inc(counted, 1)

            prologue({"P": decayed if decay is not None else lambda c: None, "N": logits, "G": counts})
            pe.wait_ge(ranked, NC)
            wait(pe, multiplied, N if decay is not None else 0)

            def transpose(b, t, uses):
                wait(pe, xb_in[t], uses, unit=16)
                wait(pe, bT_ready, b - 1)
                for j in range(ST):
                    op = pe.transpose(ps_x[:, t % 2, j * P:(j + 1) * P], xb[:, t, j, 0:P], const["ident"][:, :])
                op.then_inc(btr_done, 1)

            def hidden(b, t):
                wait(pe, w1_ready, b + 1)
                wait(pe, bT_ready, b + 1)
                for c in range(FC):
                    wait(pe, h_ready, (b - 1) * FC + c + 1)
                    pe.matmul(ps_h[:, c, 0:SLOTS], w1[:, t % 2, c * P:(c + 1) * P], xT[:, t % 2, :],
                              start=True, stop=True).then_inc(h_done, 1)

            def output(b, t):
                wait(pe, w2_ready, b + 1)
                wait(pe, h_ready, (b + 1) * FC)
                wait(pe, y_biased, b - 1)
                for j in range(ST):
                    for c in range(FC):
                        op = pe.matmul(ps_y[:, t % 2, j * P:(j + 1) * P], hid[:, t % 2, c, j * P:(j + 1) * P], w2[:, t % 2, c * P:(c + 1) * P],
                                       start=c == 0, stop=c == FC - 1)
                op.then_inc(y_done, 1)

            def body(pe, b, t, lap):
                transpose(b, t, lap + 1)
                if b_on(b, 1):
                    hidden(b - 1, (t - 1) % RB)
                if b_on(b, 2):
                    output(b - 2, (t - 2) % RB)

            blocks(pe, body, pe.Fori)
            hidden(BLOCKS - 1, (BLOCKS - 1) % RB)
            for b in (BLOCKS - 2, BLOCKS - 1):
                output(b, b % RB)

        @block.scalar
        def _(act):
            def squares(c):
                for g in range(CQ * c, CQ * (c + 1)):
                    act.wait_ge(c_in[g % 2], 16 * (g // 2 + 1))
                    wait(act, r_ready, g - 1)
                    nc.scalar.activation(sq[:, g % 2, :], cb[:, g % 2, :, :].rearrange("t s d -> t (s d)"), ACT.Square).then_inc(squared, 1)

            def copies(c):
                for g in range(CQ * c, CQ * (c + 1)):
                    act.wait_ge(xtr_done, g + 1)
                    wait(act, lg_done, g - 1)
                    nc.scalar.activation(xnT[:, g % 2, :], ps_x[:, g % 2, :], ACT.Identity).then_inc(xT_ready, 1)
                if top2:
                    nc.scalar.activation(rows[1][:, C * c:C * (c + 1), 0:P], rows[0][:, C * c:C * (c + 1), 0:P], ACT.Identity).then_inc(copied, 1)

            def exponentials(c):
                act.wait_ge(diff_ready, c + 1)
                nc.scalar.activation(ex[:, :, :], ex[:, :, :], ACT.Exp).then_inc(ex_ready, 1)

            prologue({"P": squares if decay is not None else lambda c: None, "N": copies, "G": exponentials})
            act.wait_ge(padded, 1)
            pad_regions(act, range(1, NE, 2))
            act.wait_ge(e_in, 16 * (NE + 3))
            act.wait_ge(experts_ready, 1)

            def weights(b, t):
                e = act.value_load(expert[0:1, bass.ds(b, 1)], min_val=0, max_val=NE - 1)
                nc.scalar.activation(w1[:, t % 2, :], W1[:, bass.ds(e, 1), :].rearrange("p e c -> p (e c)"), ACT.Identity).then_inc(w1_ready, 1)

            def hidden(b, t):
                for c in range(FC):
                    wait(act, h_done, b * FC + c + 1)
                    wait(act, y_done, b - 1)
                    nc.scalar.activation(hid[:, t % 2, c, :], ps_h[:, c, 0:SLOTS], ACT.Gelu if top2 else ACT.Relu,
                                         bias=w1[:, t % 2, FF + c:FF + c + 1]).then_inc(h_ready, 1)

            weights(0, 0)
            weights(1, 1)

            def body(act, b, t, lap):
                wait(act, btr_done, b + 1)
                wait(act, h_done, (b - 1) * FC)
                nc.scalar.activation(xT[:, t % 2, :], ps_x[:, t % 2, 0:SLOTS], ACT.Identity).then_inc(bT_ready, 1)
                if b_on(b, 1):
                    hidden(b - 1, (t - 1) % RB)
                    wait(act, h_ready, b * FC)
                    settle(act, passed_act)
                    weights(b + 1, (t + 1) % RB)

            blocks(act, body, act.Fori)
            hidden(BLOCKS - 1, (BLOCKS - 1) % RB)

        @block.vector
        def _(dve):
            dve.memset(pad[:, 0:P], 0.0)
            dve.memset(pad[:, P + 1:], 0.0)
            dve.memset(pad[:, P:P + 1], float(NSEQ * P)).then_inc(padded, 1)

            if decay is not None:
                for g in range(N):
                    for j in range(Q):
                        dve.bn_stats(dstat6[:, Q * g + j, :], X[:, Q * g + j, :]).then_inc(dstats_a, 1)
                    for j in range(Q):
                        dve.wait_ge(dstats_a, Q * g + j + 1)
                        op = dve.bn_aggr(dstat[:, Q * g + j, :], dstat6[:, Q * g + j, :])
                    op.then_inc(dstats_ready, 1)

            def prepare(c):
                for g in range(CQ * c, CQ * (c + 1)):
                    if decay is not None:
                        dve.wait_ge(drstd_ready, c + 1)
                        wait(dve, multiplied, g)
                        for j in range(Q):
                            s = Q * g + j
                            dve.tensor_scalar(dxn[:, j, :], X[:, s, :], dstat[:, s, 0:1], drstd[:, s:s + 1],
                                              ALU.subtract, ALU.mult).then_inc(dxn_ready, 1)
                        dve.wait_ge(dxn_ready, Q * (g + 1))
                        dve.wait_ge(r_ready, g + 1)
                        wait(dve, updated, g)
                        dve.tensor_tensor(prod[:, :, :], dxn[:, :, :], ps_r[:, g % 2, :].rearrange("t (s d) -> t s d", s=Q), ALU.mult).then_inc(multiplied, 1)
                        dve.wait_ge(multiplied, g + 1)
                        xg = X[:, Q * g:Q * (g + 1), :]
                        dve.tensor_tensor(xg, xg, prod[:, :, :], ALU.add).then_inc(updated, 1)
                        dve.wait_ge(updated, g + 1)
                    for j in range(Q):
                        dve.bn_stats(stat6[:, Q * g + j, :], X[:, Q * g + j, :]).then_inc(stats_a, 1)
                    for j in range(Q):
                        dve.wait_ge(stats_a, Q * g + j + 1)
                        op = dve.bn_aggr(stat[:, Q * g + j, :], stat6[:, Q * g + j, :])
                    op.then_inc(stats_ready, 1)

            def normalise(c):
                dve.wait_ge(rstd_ready, c + 1)
                for s in range(C * c, C * (c + 1)):
                    dve.tensor_scalar(rows[0][:, s, 0:P], X[:, s, :], stat[:, s, 0:1], rstd[:, s:s + 1],
                                      ALU.subtract, ALU.mult).then_inc(xn_ready, 1)
                if c == 0:
                    dve.wait_ge(w_in, 16 * 5)
                    dve.tensor_copy(tri16[:, :], tri[:, :])
                    dve.memset(ones16[:, :], 1.0)
                    dve.tensor_copy(run[:, 0, :], small["start"])
                    for k in range(K):
                        op = dve.tensor_copy(rows[k][:, :, P], home[:, :])
                    op.then_inc(step, 1)

            n = 1

            def then(op):
                nonlocal n
                n += 1
                op.then_inc(step, 1)
                dve.wait_ge(step, n)

            def per_token(v):
                return v[:, :].unsqueeze(2).to_broadcast(CE)

            def per_expert(v):
                return v.unsqueeze(1).to_broadcast(CE)

            def gating(c):
                seqs = slice(C * c, C * (c + 1))
                lgc = lg[:, seqs, :]
                dve.wait_ge(lg_done, CQ * (c + 1))
                dve.tensor_tensor(lgc, ps_g[:, c % 2, :].rearrange("t (s e) -> t s e", e=NE), per_expert(bg[:, :]), ALU.add).then_inc(lg_ready, 1)
                dve.wait_ge(lg_ready, c + 1)
                left = lgc
                for k in range(K):
                    then(dve.tensor_reduce(top[k][:, :], left, AX.X, ALU.max))
                    then(dve.tensor_tensor(val[:, :, :], left, per_token(top[k]), ALU.is_equal))
                    then(dve.tensor_tensor(val[:, :, :], val[:, :, :], per_expert(small["first"]), ALU.mult))
                    then(dve.tensor_reduce(pick[:, :], val[:, :, :], AX.X, ALU.max))
                    then(dve.tensor_tensor(best[k][:, :, :], val[:, :, :], per_token(pick), ALU.is_equal))
                    if k + 1 < K:
                        left = val[:, :, :]
                        then(dve.scalar_tensor_tensor(out=left, in0=best[k][:, :, :], scalar=-3e38, in1=lgc, op0=ALU.mult, op1=ALU.add))
                if top2:
                    then(dve.tensor_tensor(best16[:, :, :], best[0][:, :, :], best[1][:, :, :], ALU.add))
                else:
                    then(dve.tensor_copy(best16[:, :, :], best[0][:, :, :]))
                dve.sem_inc(chosen, 1)
                if top2:
                    then(dve.tensor_tensor(ex[:, :, 0], top[1][:, :], top[0][:, :], ALU.subtract))
                else:
                    then(dve.tensor_tensor(ex[:, :, :], lgc, per_token(top[0]), ALU.subtract))
                dve.sem_inc(diff_ready, 1)
                dve.wait_ge(counted, c + 1)
                dve.tensor_reduce(chunk[:, :], ps_n.rearrange("t (s e) -> t e s", e=NE), AX.X, ALU.add).then_inc(summed, 1)
                then(dve.tensor_tensor(ranks[:, :, :], ps_c.rearrange("t (s e) -> t s e", e=NE), per_expert(run[:, c, :]), ALU.add))
                dve.sem_inc(ranked, 1)
                dve.wait_ge(summed, c + 1)
                dve.tensor_tensor(run[:, c + 1, :], run[:, c, :], chunk[:, :], ALU.add)
                if not top2:
                    then(dve.tensor_tensor(val[:, :, :], ranks[:, :, :], per_expert(small["last"]), ALU.is_gt))
                    then(dve.scalar_tensor_tensor(out=ranks[:, :, :], in0=val[:, :, :], scalar=float(2 * EMPTY), in1=ranks[:, :, :], op0=ALU.mult, op1=ALU.add))
                for k in range(K):
                    then(dve.tensor_tensor(val[:, :, :], ranks[:, :, :], best[k][:, :, :], ALU.mult))
                    then(dve.tensor_reduce(slotf[:, k, :], val[:, :, :], AX.X, ALU.add))
                then(dve.tensor_copy(slot[:, :, seqs], slotf[:, :, :]))
                dve.wait_ge(ex_ready, c + 1)
                if top2:
                    then(dve.tensor_scalar(den[:, :], ex[:, :, 0], 1.0, None, ALU.add))
                    then(dve.reciprocal(den[:, :], den[:, :]))
                    dve.tensor_copy(rows[0][:, seqs, P + 1], den[:, :])
                    then(dve.tensor_tensor(rows[1][:, seqs, P + 1], ex[:, :, 0], den[:, :], ALU.mult))
                    dve.wait_ge(copied, c + 1)
                else:
                    then(dve.tensor_reduce(den[:, :], ex[:, :, :], AX.X, ALU.add))
                    then(dve.reciprocal(rows[0][:, seqs, P + 1], den[:, :]))
                dve.sem_inc(slots_ready, 1)

            prologue({"P": prepare, "N": normalise, "G": gating})

            then(dve.tensor_tensor(count[:, :], run[:, NC, :], small["last"], ALU.min))
            then(dve.tensor_scalar(pads[:, :], count[:, :], 1.0, None, ALU.add))
            dve.tensor_copy(pads_i[:, :], pads[:, :]).then_inc(pads_ready, 1)
            then(dve.tensor_tensor(count[:, :], count[:, :], small["start"], ALU.subtract))
            then(dve.tensor_tensor(over[:, :, :], count[:, :].unsqueeze(2).to_broadcast([P, NE, STEPS]),
                                   small["steps"].unsqueeze(1).to_broadcast([P, NE, STEPS]), ALU.is_gt))
            then(dve.tensor_reduce(nblk[:, :], over[:, :, :], AX.X, ALU.add))
            then(dve.tensor_tensor(below_n[:, :, :], small["below"].rearrange("p (a b) -> p a b", b=NE),
                                   nblk[:, :].unsqueeze(1).to_broadcast([P, NE, NE]), ALU.mult))
            then(dve.tensor_reduce(base[:, :], below_n[:, :, :], AX.X, ALU.add))
            then(dve.tensor_tensor(ends[:, :], base[:, :], nblk[:, :], ALU.add))
            then(dve.scalar_tensor_tensor(out=offset[:, :], in0=base[:, :], scalar=float(-SLOTS), in1=small["start"], op0=ALU.mult, op1=ALU.add))
            blk = small["block"]
            then(dve.tensor_tensor(past[:, :, :], blk.unsqueeze(2).to_broadcast(BE), ends[:, :].unsqueeze(1).to_broadcast(BE), ALU.is_ge))
            then(dve.tensor_tensor(begun[:, :, :], blk.unsqueeze(2).to_broadcast(BE), base[:, :].unsqueeze(1).to_broadcast(BE), ALU.is_ge))
            then(dve.tensor_reduce(owner[:, :], past[:, :, :], AX.X, ALU.add))
            then(dve.tensor_tensor(begun[:, :, :], begun[:, :, :], past[:, :, :], ALU.subtract))
            then(dve.tensor_reduce(used[:, :], begun[:, :, :], AX.X, ALU.add))
            then(dve.tensor_tensor(begun[:, :, :], begun[:, :, :], offset[:, :].unsqueeze(1).to_broadcast(BE), ALU.mult))
            then(dve.tensor_reduce(source[:, :], begun[:, :, :], AX.X, ALU.add))
            then(dve.tensor_scalar(owner[:, :], owner[:, :], float(NE - 1), None, ALU.min))
            then(dve.tensor_scalar(past[:, :, 0], blk, float(SLOTS), float(1 - EMPTY), ALU.mult, ALU.add))
            then(dve.tensor_tensor(past[:, :, 0], past[:, :, 0], used[:, :], ALU.mult))
            then(dve.scalar_tensor_tensor(out=source[:, :], in0=source[:, :], scalar=float(EMPTY), in1=past[:, :, 0], op0=ALU.add, op1=ALU.add))
            dve.tensor_copy(source_i[:, :], source[:, :])
            dve.memset(expert[:, BLOCKS:], 0)
            then(dve.tensor_copy(expert[:, 0:BLOCKS], owner[:, :]))
            dve.sem_inc(experts_ready, 1)
            dve.wait_ge(e_in, 16 * (NE + 3))

            def weights(b, t):
                e = dve.value_load(expert[0:1, bass.ds(b, 1)], min_val=0, max_val=NE - 1)
                dve.tensor_copy(w2[:, t % 2, :], W2[:, bass.ds(e, 1), :].rearrange("p e c -> p (e c)")).then_inc(w2_ready, 1)

            def output(b, t):
                wait(dve, goal_ready, b + 1)
                wait(dve, y_done, b + 1)
                y = yb[:, t, :, :]
                dve.tensor_tensor(y, ps_y[:, t % 2, 0:SLOTS].rearrange("p (j d) -> p j d", j=ST),
                                  w2[:, t % 2, FF:].unsqueeze(1).to_broadcast([P, ST, P]), ALU.add).then_inc(y_biased, 1)
                wait(dve, y_biased, b + 1)
                dve.tensor_tensor(y, y, gates[:, t, :].unsqueeze(2).to_broadcast([P, ST, P]), ALU.mult).then_inc(y_ready, 1)

            weights(0, 0)
            weights(1, 1)

            def body(dve, b, t, lap):
                wait(dve, xb_in[t], lap + 1, unit=16)
                wait(dve, y_out[t], lap, unit=16 * ST)
                dve.tensor_copy(goal[:, t, :], xb[:, t, :, P])
                dve.tensor_copy(gates[:, t, :], xb[:, t, :, P + 1]).then_inc(goal_ready, 1)
                if b_on(b, 2):
                    output(b - 2, (t - 2) % RB)
                    weights(b, t)

            blocks(dve, body, dve.Fori)
            for b in (BLOCKS - 2, BLOCKS - 1):
                output(b, b % RB)


def store_stage(nc, X, out):
    with semaphores(nc) as take, ExitStack() as ctx:
        stored = take("stored")
        block = ctx.enter_context(nc.Block())

        @block.sync
        def _(sync):
            sync.dma_start(out.rearrange("s t d -> t s d"), X[:, :, :]).then_inc(stored, 16)
            sync.wait_ge(stored, 16)


def ffn_inputs(nc, a, n):
    rows = nc.dram_tensor(f"rows{n}", (NE * region_for(n + 1) + SLOTS, ROW), F32, kind="Internal").ap()
    return {k: a[f"F{n}_{k}"] for k in ("wg", "bg", "w1", "b1", "w2", "b2")} | {"tri": a["c_tri"], "home": a["c_home"], "table": a[f"c_table{n}"]}, rows


def decoder(nc, a, out, stages=99):
    with ExitStack() as ctx:
        def sb(n, shape, dt=F32):
            return ctx.enter_context(nc.sbuf_tensor(n, shape, dt))

        X = sb("X", [P, NSEQ, P])
        const = {"ident": sb("ident", [P, P]), "ident16": sb("ident16", [P, P], BF16), "minus_half": sb("minus_half", [P, 8])}
        w, loads = [], []
        for n in range(4):
            tiles = {k: sb(f"A{n}_{k}", [P, P]) for k in ("wq", "wk", "wv", "wo")}
            loads.append([(tiles[k][:, :], a[f"A{n}_{k}"]) for k in ("wq", "wk", "wv", "wo")])
            for k in ("bq", "bk", "bv", "bo"):
                if f"A{n}_{k}" in a:
                    column = k in ("bq", "bk") or n == 1 and k == "bo"
                    tile = sb(f"A{n}_{k}", [P, 1] if column else [P, P])
                    dram = a[f"A{n}_{k}"]
                    loads[n].append((tile[:, :], dram if len(dram.shape) == 2 else
                                  dram.rearrange("(a b) -> a b", b=1) if column else dram.partition_broadcast(P)))
                    tiles["bo_col" if n == 1 and k == "bo" else k] = tile
            w.append(tiles)
        with ExitStack() as stacks:
            def sbs(n, shape, dt=F32):
                return stacks.enter_context(nc.sbuf_tensor(n, shape, dt))

            const["qst"], const["kst"] = sbs("qst", [P, RING, H, GT], BF16), sbs("kst", [P, RING, H, GT], BF16)
            const["v1"] = sbs("v1", [P, RING, GS, H, 32])
            with ExitStack() as layer0:
                def sb0(n, shape, dt=F32):
                    return layer0.enter_context(nc.sbuf_tensor(n, shape, dt))

                hT = sb0("hT", [P, NSEQ * P])
                const["dist"] = sb0("dist", [P, P], BF16)
                const["slope"] = sb0("slope", [P, 3, H, P], BF16)
                const["falloff"] = sb0("falloff", [P, H, P])
                const["mask_qk"] = sb0("mask_qk", [P, HB, P], BF16)
                const["mask_kq"] = sb0("mask_kq", [P, HB, P], BF16)
                const["dist32"] = sb0("dist32", [P, P])
                const["mask_qk32"], const["mask_kq32"] = sb0("mask_qk32", [P, P]), sb0("mask_kq32", [P, P])
                const["neg_alpha"], const["alpha_parts"] = sb0("neg_alpha", [P, H]), sb0("alpha_parts", [P, 3, H], BF16)
                first = [(const["ident"][:, :], a["c_ident"]), (const["dist32"][:, :], a["c_dist"])] + loads[0]
                later = [(const["mask_qk32"][:, :], a["c_mask"]), (const["mask_kq32"][:, :], a["c_mask_t"])] + loads[1] + loads[2] + loads[3]
                setup_stage(nc, const, a["L0_attn_decay_alpha"], first)
                parts = [{"w": w[0], "scale": HD ** -0.5, "extra": "alibi"},
                         {"w": w[1], "scale": HD ** -0.5, "extra": "causal", "h_out": True},
                         {"w": w[2], "scale": HD ** -0.5, "q_from_h": True, "kv_dram": a["ctx"]}]
                attention_stage(nc, "attn0", X, parts, hT, const, a["x"], later)
            if stages > 2:
                w0, rows = ffn_inputs(nc, a, 0)
                x_ffn = nc.dram_tensor("x_ffn", (NSEQ, P, P), F32, kind="Internal").ap()
                ffn_stage(nc, "ffn0", X, w0, const, rows, x_ffn.rearrange("s t d -> (s t) d"), False)
            if stages > 3:
                attention_stage(nc, "attn1", X, [{"w": w[3], "scale": P ** -0.5}], None, const, x_ffn)
        if stages > 5:
            w1, rows = ffn_inputs(nc, a, 1)
            ffn_stage(nc, "ffn1", X, w1, const, rows, out.rearrange("s t d -> (s t) d"), True, decay=(a["ctx"], a["c_decay"]))
        else:
            store_stage(nc, X, out)


def lay_out(inputs):
    v = {k: np.asarray(x) for k, x in inputs.items()}
    a = {"x": v["x"], "ctx": v["ctx_1024"], "L0_attn_decay_alpha": v["L0_attn_decay_alpha"]}

    def by_dim(wt):
        return wt.reshape(-1, H, HD).swapaxes(1, 2).reshape(-1, P)

    wT = v["L0_attn_qkv_w"].T
    b = v["L0_attn_qkv_b"]
    a["A0_wq"], a["A0_wk"], a["A0_wv"] = by_dim(wT[:, 0:P]), by_dim(wT[:, P:2 * P]), wT[:, 2 * P:]
    a["A0_bq"], a["A0_bk"], a["A0_bv"] = by_dim(b[0:P]).reshape(P, 1), by_dim(b[P:2 * P]).reshape(P, 1), b[2 * P:]
    a["A0_wo"], a["A0_bo"] = v["L0_attn_out_w"].T, v["L0_attn_out_b"]
    for n in (1, 2):
        for k in "qk":
            a[f"A{n}_w{k}"] = v[f"L0_xattn_W{k}{n}"].transpose(1, 2, 0).reshape(P, P)
            a[f"A{n}_b{k}"] = v[f"L0_xattn_b{k}{n}"].T.reshape(P, 1)
        a[f"A{n}_wv"] = v[f"L0_xattn_Wv{n}"].transpose(1, 0, 2).reshape(P, P)
        a[f"A{n}_bv"] = v[f"L0_xattn_bv{n}"].reshape(P)
        a[f"A{n}_wo"], a[f"A{n}_bo"] = v[f"L0_xattn_Wo{n}"], v[f"L0_xattn_bo{n}"]
    for k in "qkv":
        w = np.zeros((H, HD, HD, H) if k != "v" else (H, HD, H, HD), np.float32)
        for h in range(H):
            if k != "v":
                w[h, :, :, h] = v[f"L1_attn_W{k}"].T
            else:
                w[h, :, h, :] = v["L1_attn_Wv"].T
        a[f"A3_w{k}"] = w.reshape(P, P)
    a["A3_wo"], a["A3_bo"] = v["L1_attn_W_out"].T, v["L1_attn_b_out"]
    for n, l, up in ((0, "L0_ffn_w1", "L0_ffn"), (1, "L1_ffn_W1", "L1_ffn")):
        a[f"F{n}_w1"], a[f"F{n}_w2"] = v[l], v[l[:-1] + "2"]
        a[f"F{n}_b1"] = v[f"{up}_b1"].reshape(NE, FC, P).transpose(2, 0, 1)
        a[f"F{n}_b2"] = v[f"{up}_b2"]
    a["F0_wg"], a["F0_bg"] = v["L0_ffn_gate_w"].T, v["L0_ffn_gate_b"]
    a["F1_wg"], a["F1_bg"] = v["L1_ffn_Wg"], v["L1_ffn_bg"]
    n = np.arange(P)
    a["c_tri"] = (n[:, None] <= n[None, :]).astype(np.float32)
    for i in (0, 1):
        a[f"c_table{i}"] = np.concatenate(list(table_for(i + 1).values())).astype(np.float32)
    a["c_home"] = (np.arange(NSEQ)[None, :] * P + n[:, None]).astype(np.float32)
    ahead = n[None, :] - n[:, None]
    a["c_decay"] = np.where(ahead >= 0, DECAY ** np.maximum(ahead, 0).astype(np.float64), 0.0).astype(np.float32)
    a["c_ident"] = np.eye(P, dtype=np.float32)
    a["c_dist"] = np.abs(n[:, None] - n[None, :]).astype(np.float32)
    a["c_mask"] = np.where(n[None, :] > n[:, None], np.float32(-1e30), np.float32(0))
    a["c_mask_t"] = np.ascontiguousarray(a["c_mask"].T)
    return {k: np.ascontiguousarray(x) for k, x in a.items()}


def kernel(**inputs):
    import concourse.bacc as _bacc
    from concourse.bass_utils import run_bass_kernel_spmd as _run

    nc = _bacc.Bacc("TRN2", target_bir_lowering=False, num_devices=1)
    arrays, args = {}, {}
    for name, a in lay_out(inputs).items():
        arrays[f"in_{name}"] = a
        args[name] = nc.dram_tensor(f"in_{name}", a.shape, mybir.dt.from_np(a.dtype), kind="ExternalInput").ap()
    out = nc.dram_tensor("out", (NSEQ, P, P), F32, kind="ExternalOutput").ap()
    decoder(nc, args, out)
    r = _run(nc, [arrays], core_ids=[0])
    return r.results[0]["out"]
```
